# Optimizing a Trainium2 kernel written in Bass

```python
import numpy as np
import jax
import jax.numpy as jnp

def _softmax(x, axis=-1):
    return jax.nn.softmax(x, axis=axis)

def _gelu(x):
    return jax.nn.gelu(x, approximate=True)

def _silu(x):
    return jax.nn.silu(x)

def _sigmoid(x):
    return jax.nn.sigmoid(x)

def _layernorm(x, axis=-1, eps=1e-05):
    m = jnp.mean(x, axis=axis, keepdims=True)
    v = jnp.var(x, axis=axis, keepdims=True)
    return (x - m) / jnp.sqrt(v + eps)

def _scatter_add(tgt, idx, src, axis=0):
    return tgt.at[idx].add(src)

def _segment_sum(src, seg, n):
    return jax.ops.segment_sum(src, seg, n)
kernel_name = 'mk_flamingo_gated_d2_seqx_r4_596fcd'

def setup_inputs(seed: int=0):
    np.random.seed(seed)
    _w = jnp.asarray

    def _rec_inputs():
        import jax
        import jax.numpy as jnp
        _rk = jax.random.key(seed)
        x = -0.0002928 + 1 * jax.random.normal(jax.random.fold_in(_rk, 1), (2, 1024, 256), jnp.float32)
        _lenS = 1024 - jax.random.randint(jax.random.fold_in(_rk, 7), (2,), 0, max(1, 1024 // 4) + 1, jnp.int32)
        _lenS2 = 154 - jax.random.randint(jax.random.fold_in(_rk, 8), (2,), 0, max(1, 154 // 4) + 1, jnp.int32)
        _ctx_1024P = jax.random.normal(jax.random.fold_in(_rk, 11), (2, 16, 256), jnp.float32)
        _ctx_1024c = jax.random.dirichlet(jax.random.fold_in(_rk, 511), 0.3 * jnp.ones((16,), jnp.float32), (2, 154))
        _ctx_1024t = jnp.einsum('bsk,bkd->bsd', _ctx_1024c, _ctx_1024P)
        _ctx_1024t = _ctx_1024t * jax.lax.rsqrt(jnp.mean(jnp.square(_ctx_1024t)) + 1e-12) * 0.953939
        ctx_1024 = -1.39393e-06 + 0.999914 * (_ctx_1024t + 0.3 * jax.random.normal(jax.random.fold_in(_rk, 611), (2, 154, 256), jnp.float32))
        _validS = jnp.arange(1024)[None, :] < _lenS[:, None]
        _validS2 = jnp.arange(154)[None, :] < _lenS2[:, None]
        _causal = jnp.tril(jnp.ones((1024, 1024), dtype=bool))
        mask_BxSxS2_fk1 = jnp.where(jnp.broadcast_to(_validS2[:, None, :], (2, 1024, 154)), 1.0, 0.0).astype(jnp.float32)
        mask_BxS_ff1 = jnp.where(jnp.ones((2, 1024), dtype=bool), 1.0, 0.0).astype(jnp.float32)
        mask_BxS2_ik0 = jnp.where(jnp.broadcast_to(_validS2[:, :], (2, 154)), 0, 1).astype(jnp.int32)
        _g = jax.random.normal(jax.random.fold_in(_rk, 9001), (2, 2), jnp.float32)
        _g = jnp.sign(_g) * jnp.maximum(jnp.abs(_g), 1.0) + (_g == 0) * 1.0
        g_xattn = _g[0]
        g_ffn = _g[1]
        return (x, ctx_1024, mask_BxSxS2_fk1, mask_BxS_ff1, mask_BxS2_ik0, g_xattn, g_ffn)
    x, ctx_1024, mask_BxSxS2_fk1, mask_BxS_ff1, mask_BxS2_ik0, g_xattn, g_ffn = _rec_inputs()

    def _L0_xattn_setup():
        import jax, jax.numpy as jnp
        import numpy as np
        D = 256
        H = 16
        P = D // H
        NEG = -10000000000.0
        key = jax.random.key(seed)
        ks = jax.random.split(key, 12)
        b, n, m = (2, 512, 512)
        s = 1.0 / np.sqrt(D)
        inp = {'queries': jax.random.normal(ks[0], (b, n, D), jnp.float32), 'keys': jax.random.normal(ks[1], (b, m, D), jnp.float32), 'values': jax.random.normal(ks[2], (b, m, D), jnp.float32), 'visible_masking': jax.random.randint(ks[3], (b, n, m), 0, 2).astype(jnp.float32), 'Wq': jax.random.normal(ks[4], (D, D), jnp.float32) * s, 'bq': jnp.zeros((D,), jnp.float32), 'Wk': jax.random.normal(ks[5], (D, D), jnp.float32) * s, 'bk': jnp.zeros((D,), jnp.float32), 'Wv': jax.random.normal(ks[6], (D, D), jnp.float32) * s, 'bv': jnp.zeros((D,), jnp.float32), 'Wo': jax.random.normal(ks[7], (D, D), jnp.float32) * s, 'bo': jnp.zeros((D,), jnp.float32)}
        return inp
    _L0_xattn_all = _L0_xattn_setup()
    _L0_xattn_in = {k: v for k, v in _L0_xattn_all.items() if k in ('Wq', 'bq', 'Wk', 'bk', 'Wv', 'bv', 'Wo', 'bo')}
    del _L0_xattn_all

    def _L0_ffn_setup():
        import jax, jax.numpy as jnp
        import numpy as np
        B, T, H = (2, 512, 256)
        I = 1024
        HEADS = 4
        RET = 128
        NUM_EXPERTS = 1024
        NUM_KEYS = 64
        K = 8
        key = jax.random.key(seed)
        ks = jax.random.split(key, 7)
        return {'hidden_states': jax.random.normal(ks[0], (B, T, H), jnp.float32), 'W_up': jax.random.normal(ks[1], (I, H), jnp.float32) * 0.02, 'W_down': jax.random.normal(ks[2], (H, I), jnp.float32) * 0.02, 'W_q': jax.random.normal(ks[3], (HEADS * RET, H), jnp.float32) * 0.02, 'keys': jax.random.normal(ks[4], (HEADS, NUM_KEYS, 2, RET // 2), jnp.float32) * 0.02, 'down_embed': jax.random.normal(ks[5], (NUM_EXPERTS, H), jnp.float32) * 0.02, 'up_embed': jax.random.normal(ks[6], (NUM_EXPERTS, H), jnp.float32) * 0.02}
    _L0_ffn_all = _L0_ffn_setup()
    _L0_ffn_in = {k: v for k, v in _L0_ffn_all.items() if k in ('W_up', 'W_down', 'W_q', 'keys', 'down_embed', 'up_embed')}
    del _L0_ffn_all

    def _L1_xattn_setup():
        import jax, jax.numpy as jnp
        import numpy as np
        B, F, T, D = (8, 64, 32, 256)
        NEG = -1e+30
        key = jax.random.key(seed)
        ks = jax.random.split(key, 10)
        s = 1.0 / np.sqrt(D)
        return {'features': jax.random.normal(ks[0], (B, F, D), jnp.float32), 'masks': jnp.ones((B, F), jnp.float32), 'textual_features': jax.random.normal(ks[1], (B, T, D), jnp.float32), 'q_masks': jax.random.randint(ks[2], (B, T), 0, 2, jnp.int32), 'Ws': jax.random.normal(ks[3], (D, D), jnp.float32) * s, 'W': jax.random.normal(ks[4], (D, D), jnp.float32) * s, 'w': jax.random.normal(ks[5], (D, 1), jnp.float32) * s, 'b': jax.random.normal(ks[6], (1, D), jnp.float32) * s, 'Wcw': jax.random.normal(ks[7], (1, D), jnp.float32) * s, 'bcw': jnp.zeros((1,), jnp.float32), 'Wcb': jax.random.normal(ks[8], (1, D), jnp.float32) * s, 'bcb': jnp.zeros((1,), jnp.float32)}
    _L1_xattn_all = _L1_xattn_setup()
    _L1_xattn_in = {k: v for k, v in _L1_xattn_all.items() if k in ('Ws', 'W', 'w', 'b', 'Wcw', 'bcw', 'Wcb', 'bcb')}
    del _L1_xattn_all

    def _L1_ffn_setup():
        import jax, jax.numpy as jnp
        import numpy as np
        N_EMBD = 256
        NUM_EXPERTS = 8
        TOP_K = 2

        def new_gelu(x):
            c = jnp.sqrt(2.0 / jnp.pi).astype(x.dtype)
            return 0.5 * x * (1.0 + jnp.tanh(c * (x + 0.044715 * x ** 3)))
        key = jax.random.key(seed)
        ks = jax.random.split(key, 6)
        C, E, H = (N_EMBD, NUM_EXPERTS, 4 * N_EMBD)
        x = jax.random.normal(ks[0], (4, 512, C), dtype=jnp.float32)
        router_w = 0.02 * jax.random.normal(ks[1], (E, C), dtype=jnp.float32)
        w1 = 0.02 * jax.random.normal(ks[2], (E, H, C), dtype=jnp.float32)
        b1 = jnp.zeros((E, H), dtype=jnp.float32)
        w2 = 0.02 * jax.random.normal(ks[3], (E, C, H), dtype=jnp.float32)
        b2 = jnp.zeros((E, C), dtype=jnp.float32)
        return {'x': x, 'router_w': router_w, 'w1': w1, 'b1': b1, 'w2': w2, 'b2': b2}
    _L1_ffn_all = _L1_ffn_setup()
    _L1_ffn_in = {k: v for k, v in _L1_ffn_all.items() if k in ('router_w', 'w1', 'b1', 'w2', 'b2')}
    del _L1_ffn_all
    return {'x': x, 'ctx_1024': ctx_1024, 'mask_BxSxS2_fk1': mask_BxSxS2_fk1, 'mask_BxS_ff1': mask_BxS_ff1, 'mask_BxS2_ik0': mask_BxS2_ik0, 'g_xattn': g_xattn, 'g_ffn': g_ffn, 'L0_xattn_Wq': _L0_xattn_in['Wq'], 'L0_xattn_bq': _L0_xattn_in['bq'], 'L0_xattn_Wk': _L0_xattn_in['Wk'], 'L0_xattn_bk': _L0_xattn_in['bk'], 'L0_xattn_Wv': _L0_xattn_in['Wv'], 'L0_xattn_bv': _L0_xattn_in['bv'], 'L0_xattn_Wo': _L0_xattn_in['Wo'], 'L0_xattn_bo': _L0_xattn_in['bo'], 'L0_ffn_W_up': _L0_ffn_in['W_up'], 'L0_ffn_W_down': _L0_ffn_in['W_down'], 'L0_ffn_W_q': _L0_ffn_in['W_q'], 'L0_ffn_keys': _L0_ffn_in['keys'], 'L0_ffn_down_embed': _L0_ffn_in['down_embed'], 'L0_ffn_up_embed': _L0_ffn_in['up_embed'], 'L1_xattn_Ws': _L1_xattn_in['Ws'], 'L1_xattn_W': _L1_xattn_in['W'], 'L1_xattn_w': _L1_xattn_in['w'], 'L1_xattn_b': _L1_xattn_in['b'], 'L1_xattn_Wcw': _L1_xattn_in['Wcw'], 'L1_xattn_bcw': _L1_xattn_in['bcw'], 'L1_xattn_Wcb': _L1_xattn_in['Wcb'], 'L1_xattn_bcb': _L1_xattn_in['bcb'], 'L1_ffn_router_w': _L1_ffn_in['router_w'], 'L1_ffn_w1': _L1_ffn_in['w1'], 'L1_ffn_b1': _L1_ffn_in['b1'], 'L1_ffn_w2': _L1_ffn_in['w2'], 'L1_ffn_b2': _L1_ffn_in['b2']}

def reference(x, ctx_1024, mask_BxSxS2_fk1, mask_BxS_ff1, mask_BxS2_ik0, g_xattn, g_ffn, L0_xattn_Wq, L0_xattn_bq, L0_xattn_Wk, L0_xattn_bk, L0_xattn_Wv, L0_xattn_bv, L0_xattn_Wo, L0_xattn_bo, L0_ffn_W_up, L0_ffn_W_down, L0_ffn_W_q, L0_ffn_keys, L0_ffn_down_embed, L0_ffn_up_embed, L1_xattn_Ws, L1_xattn_W, L1_xattn_w, L1_xattn_b, L1_xattn_Wcw, L1_xattn_bcw, L1_xattn_Wcb, L1_xattn_bcb, L1_ffn_router_w, L1_ffn_w1, L1_ffn_b1, L1_ffn_w2, L1_ffn_b2):
    import jax
    import jax.numpy as jnp

    def _L0_xattn_ref(queries, keys, values, visible_masking, Wq, bq, Wk, bk, Wv, bv, Wo, bo):
        import jax, jax.numpy as jnp
        import numpy as np
        D = 256
        H = 16
        P = D // H
        NEG = -10000000000.0
        b, n, d = queries.shape
        m = keys.shape[1]
        q = (queries @ Wq.T + bq).reshape(b, n, H, P)
        k = (keys @ Wk.T + bk).reshape(b, m, H, P)
        v = (values @ Wv.T + bv).reshape(b, m, H, P)
        temperature = jnp.asarray(P, queries.dtype) ** 0.5
        scores = jnp.einsum('bnhp,bmhp->bhnm', q, k) / temperature
        scores = jnp.where(visible_masking[:, None, :, :] == 0.0, NEG, scores)
        attn = jax.nn.softmax(scores, axis=-1)
        out = jnp.einsum('bhnm,bmhp->bnhp', attn, v).reshape(b, n, d)
        return out @ Wo.T + bo

    def _L0_ffn_ref(hidden_states, W_up, W_down, W_q, keys, down_embed, up_embed):
        import jax, jax.numpy as jnp
        import numpy as np
        B, T, H = (2, 512, 256)
        I = 1024
        HEADS = 4
        RET = 128
        NUM_EXPERTS = 1024
        NUM_KEYS = 64
        K = 8
        b, t, hd = hidden_states.shape
        h, nk, _, n = keys.shape
        q = jnp.einsum('btd,ed->bte', hidden_states, W_q)
        q = q.reshape(b, t, 2, h, n).transpose(2, 0, 1, 3, 4)
        sim = jnp.einsum('pbthn,hkpn->pbthk', q, keys)
        scores_xy, idx_xy = jax.lax.top_k(sim, K)
        sx, sy = (scores_xy[0], scores_xy[1])
        ix, iy = (idx_xy[0], idx_xy[1])
        all_scores = (sx[..., :, None] + sy[..., None, :]).reshape(b, t, h, K * K)
        all_idx = (ix[..., :, None] * nk + iy[..., None, :]).reshape(b, t, h, K * K)
        scores, pk = jax.lax.top_k(all_scores, K)
        indices = jnp.take_along_axis(all_idx, pk, axis=-1)
        de = down_embed[indices]
        ue = up_embed[indices]
        w = jax.nn.silu(jnp.einsum('btd,bthkd->bthk', hidden_states, de) * jax.nn.softmax(scores, axis=-1))
        experts_states = jnp.einsum('bthk,bthkd->btd', w, ue)
        dense = jnp.einsum('bti,di->btd', jax.nn.silu(jnp.einsum('btd,id->bti', hidden_states, W_up)), W_down)
        return dense + experts_states

    def _L1_xattn_ref(features, masks, textual_features, q_masks, Ws, W, w, b, Wcw, bcw, Wcb, bcb):
        import jax, jax.numpy as jnp
        import numpy as np
        B, F, T, D = (8, 64, 32, 256)
        NEG = -1e+30
        txt_proj = jnp.einsum('btd,de->bte', textual_features, Ws)
        feat_proj = jnp.einsum('bfd,de->bfe', features, W)
        h = jnp.tanh(txt_proj[:, None, :, :] + feat_proj[:, :, None, :] + b[None, None, :, :][..., 0, :])
        rho = jnp.einsum('bftd,d->bft', h, w[:, 0])
        qm = q_masks.astype(jnp.float32)
        rho = rho + (1.0 - qm)[:, None, :] * NEG
        att = jax.nn.softmax(rho, axis=-1)
        txt_h = jnp.einsum('bft,btd->bfd', att, textual_features)
        w_s = jnp.tanh(jnp.einsum('bfd,od->bfo', txt_h, Wcw) + bcw)
        b_s = jnp.tanh(jnp.einsum('bfd,od->bfo', txt_h, Wcb) + bcb)
        return w_s * features + b_s

    def _L1_ffn_ref(x, router_w, w1, b1, w2, b2):
        import jax, jax.numpy as jnp
        import numpy as np
        N_EMBD = 256
        NUM_EXPERTS = 8
        TOP_K = 2

        def new_gelu(x):
            c = jnp.sqrt(2.0 / jnp.pi).astype(x.dtype)
            return 0.5 * x * (1.0 + jnp.tanh(c * (x + 0.044715 * x ** 3)))
        B, T, C = x.shape
        E = router_w.shape[0]
        x_flat = x.reshape(B * T, C)
        router_logits = x_flat @ router_w.T
        router_probs = jax.nn.softmax(router_logits, axis=-1)
        top_k_probs, top_k_idx = jax.lax.top_k(router_probs, TOP_K)
        top_k_probs = top_k_probs / (top_k_probs.sum(axis=-1, keepdims=True) + 1e-08)
        cw = (jax.nn.one_hot(top_k_idx, E, dtype=x.dtype) * top_k_probs[..., None]).sum(axis=1)
        output = jnp.zeros_like(x_flat)
        for e in range(E):
            h = new_gelu(x_flat @ w1[e].T + b1[e])
            out_e = h @ w2[e].T + b2[e]
            output = output + cw[:, e:e + 1] * out_e
        return output.reshape(B, T, C)
    x = x + jnp.tanh(g_xattn[0]) * _L0_xattn_ref(_layernorm(x, axis=-1), ctx_1024, ctx_1024, mask_BxSxS2_fk1, L0_xattn_Wq, L0_xattn_bq, L0_xattn_Wk, L0_xattn_bk, L0_xattn_Wv, L0_xattn_bv, L0_xattn_Wo, L0_xattn_bo)
    x = x + jnp.tanh(g_ffn[0]) * _L0_ffn_ref(_layernorm(x, axis=-1), L0_ffn_W_up, L0_ffn_W_down, L0_ffn_W_q, L0_ffn_keys, L0_ffn_down_embed, L0_ffn_up_embed)
    x = x + jnp.tanh(g_xattn[1]) * _L1_xattn_ref(_layernorm(x, axis=-1), mask_BxS_ff1, ctx_1024, mask_BxS2_ik0, L1_xattn_Ws, L1_xattn_W, L1_xattn_w, L1_xattn_b, L1_xattn_Wcw, L1_xattn_bcw, L1_xattn_Wcb, L1_xattn_bcb)
    x = x + jnp.tanh(g_ffn[1]) * _L1_ffn_ref(_layernorm(x, axis=-1), L1_ffn_router_w, L1_ffn_w1, L1_ffn_b1, L1_ffn_w2, L1_ffn_b2)
    return x

_drawn_inputs = setup_inputs


def setup_inputs(seed=0):
    import zlib

    import numpy as np

    out = dict(_drawn_inputs(seed))
    spreads = {'g_ffn': (-1.0, 0.6),
     'L0_xattn_bq': (0.0, 0.441),
     'L0_xattn_bk': (0.0, 0.8),
     'L0_xattn_bv': (0.0, 0.1),
     'L0_xattn_bo': (0.0, 0.1),
     'L1_ffn_b1': (0.0, 0.5),
     'L1_ffn_b2': (0.0, 0.1)}
    factors = {'L0_ffn_W_q': 8.0,
     'L0_ffn_keys': 8.0,
     'L0_ffn_down_embed': 6.788,
     'L0_ffn_up_embed': 6.811,
     'L1_xattn_b': 8.0}
    for name, (base, spread) in spreads.items():
        noise = np.random.default_rng([zlib.crc32(name.encode()), seed]).standard_normal(out[name].shape)
        drawn = base * np.exp(spread * noise) if base else spread * noise
        out[name] = jnp.asarray(drawn.astype(out[name].dtype))
    for name, factor in factors.items():
        out[name] = (out[name] * factor).astype(out[name].dtype)
    return out
```

```python
from contextlib import ExitStack

import numpy as np

import concourse.bass as bass
from concourse import mybir

ALU = mybir.AluOpType
ACT = mybir.ActivationFunctionType
F32 = mybir.dt.float32
BF16 = mybir.dt.bfloat16
I32 = mybir.dt.int32
U32 = mybir.dt.uint32
AX = mybir.AxisListType

P = 128
B, S, D = 2, 1024, 256
M = 154
NT = B * S // P
NTB = S // P
DC = D // P
H, HD = 16, 16
HG = P // HD
MT = M - P
TQ = 4
FF = 1024
FC = FF // P
PH, NK, TOPK = 4, 64, 8
NE = 1024
NX = NE // NK
MASKED = -(2.0 ** 100)
FAR = 3.0e38
EPS = 1e-5
IT, TI = 7, 22
TR = 6
RI = 4 * TR
E = 8
MOE_TILES = 2 * S // P + E - 1
NEG = -1e30


def build(nc, t, out):
    ctx = ExitStack()
    with ctx:
        arena = ctx.enter_context(nc.sbuf_tensor("arena", [P, 53200], F32))
        top = [0]

        def words(n, at=None):
            o = top[0] if at is None else at
            if at is None:
                top[0] += n
            assert o + n <= 53200, (o, n)
            return arena[:, o:o + n]

        def sem(name):
            return ctx.enter_context(nc.semaphore(name))

        x = words(NT * D).rearrange("p (i d) -> p i d", i=NT)
        feat0 = top[0]
        feat_t = words(B * DC * S).rearrange("p (b c n) -> p b c n", b=B, c=DC)
        mean3 = words(NT)
        rstd3 = words(NT)
        gate = words(8)
        ident = words(P)
        ident_bf = words(P // 2).bitcast(BF16)
        headmask = words(HG)
        iota16 = words(NX)
        neg_half = words(1)
        window = words(DC * 63).rearrange("p (c n) -> p c n", c=DC)
        w_rho = words(DC)
        q_bias = words(B * IT * RI).rearrange("p (b n) -> p b n", b=B)
        gate_rows = words(2 * B * IT * RI).rearrange("p (k b n) -> p k b n", k=2, b=B)
        gate_bias = words(2)
        w_router = words(DC * E).rearrange("p (c n) -> p c n", c=DC)
        before = words(P)
        ones = words(P)
        steps128 = words(E)
        tile_no = words(MOE_TILES)
        rho_rows = words(S)
        gates3 = words(NTB * 2)
        neg_half8 = words(NTB)
        dots = words(NTB * 4)
        logits = words(NTB * E)
        picks = words(2 * B * NTB)
        slots = words(2 * B * NTB)
        owner = words(B * MOE_TILES)
        route = words(12 * NTB * E)
        carrier4 = words(1)
        bn4 = words(6)
        stat4 = words(2)
        var_eps = words(1)
        rstd = words(1)
        own_w = words(224)
        ones3 = words(P // 2).bitcast(BF16)
        ctx_t = words(DC * B * M).rearrange("p (c m) -> p c m", c=DC)
        txt_bias = words(DC * B * M).rearrange("p (c m) -> p c m", c=DC)
        ring = words(4 * S).rearrange("p (k n) -> p k n", k=4)
        front0 = top[0]
        wq = words(DC * D).rearrange("p (c n) -> p c n", c=DC)
        wo = words(DC * D).rearrange("p (c n) -> p c n", c=DC)
        w_feat = words(DC * D).rearrange("p (c n) -> p c n", c=DC)
        w_up = words(DC * FF).rearrange("p (c n) -> p c n", c=DC)
        w_down = words(FC * D).rearrange("p (c n) -> p c n", c=FC)
        w_pq = words(DC * 2 * D).rearrange("p (c n) -> p c n", c=DC)
        keys = words(4 * P).rearrange("p (c n) -> p c n", c=4)
        de = words(DC * NE).rearrange("p (c n) -> p c n", c=DC)
        ue = words(NE // P * D).rearrange("p (c n) -> p c n", c=NE // P)
        bq = words(DC)
        bk = words(DC)
        b_txt = words(DC)
        bo = words(D)
        mask_bias = words(NT * M // 2).bitcast(BF16)
        k_blocks = words(B * H * M)
        v_main = words(B * H * (HD + 1)).rearrange("p (b h e) -> p b h e", b=B, h=H)
        v_rest = words(B * H * (HD + 1)).rearrange("p (b q n) -> p b q n", b=B, q=H // TQ)
        xn = words(D)
        xn_t = words(D).rearrange("p (c n) -> p c n", c=DC)
        bn = words(6)
        stat = words(2)
        q_t = words(D).rearrange("p (c n) -> p c n", c=DC)
        row_max = words(HG)
        rest_max = words(HG)
        r_den = words(H)
        up_act = words(FF)
        up_t = words(FF)
        scores = words(8 * NK)
        pq_t = words(512)
        top_xy = words(64)
        idx = words(32)
        idx_f = words(32)
        far_off = words(32)
        grid = words(256)
        grid_rep = words(256)
        grid_sel = words(256)
        grid_b = words(256)
        top_s = words(32)
        t8 = words(32)
        t16 = words(64)
        cmp16 = words(512)
        e_in = words(4 * 104).rearrange("p (h n) -> p h n", h=PH)
        den4 = words(PH)
        last_sum = words(1)
        carrier = words(1)
        front_end = top[0]
        big1 = words(PH * NE)
        big2 = words(PH * NE)
        prob = big1[:, 0:H * M].rearrange("p (g n) -> p g n", g=DC)
        prob_t = big2[:, 0:5 * 512].rearrange("p (k n) -> p k n", k=5)
        att = up_act[:, 0:D]
        att_t = up_t[:, 0:D].rearrange("p (c n) -> p c n", c=DC)
        proj = up_act[:, 512:512 + D]
        assert NT * M <= PH * NE
        mask = big2[:, 0:NT * M]
        w1 = words(E * DC * FF, front0)
        w2 = words(E * FC * D, front0 + E * DC * FF)
        late0 = front0 + E * DC * FF + E * FC * D
        rho_t = words(NTB * IT * RI, late0).rearrange("p (i n) -> p i n", i=NTB)
        rho_w = words(NTB // 2 * IT * RI, late0 + NTB * IT * RI).rearrange("p (i n) -> p i n", i=NTB // 2)
        row_in = words(D, late0)
        row_t = words(D, late0 + D)
        row_out = words(D, late0 + 2 * D)
        bias_rows = words((FF + D) // 2, late0 + 3 * D).bitcast(BF16)
        xn4 = words(D, late0 + 6 * D)
        xn4_t = words(D, late0 + 7 * D).rearrange("p (c n) -> p c n", c=DC)
        rho_back = [words(2 * S, feat0 + b * DC * S).rearrange("p (k n) -> p k n", k=2) for b in range(B)]
        rows4 = [words(NTB * D, feat0 + b * DC * S).rearrange("p (i d) -> p i d", i=NTB) for b in range(B)]
        hid = [words(FF, feat0 + b * DC * S) for b in range(B)]
        hid_t = [words(FF, feat0 + b * DC * S + FF) for b in range(B)]
        back = [words(NTB * D, feat0 + b * DC * S).rearrange("p (i k d) -> p i k d", k=2, d=D) for b in range(B)]
        zero_rows = rho_rows[:, 0:D]
        wk = ring[:, 0, 0:512].rearrange("p (c n) -> p c n", c=DC)
        wv = ring[:, 0, 512:1024].rearrange("p (c n) -> p c n", c=DC)
        w_txt = ring[:, 1, 0:512].rearrange("p (c n) -> p c n", c=DC)
        bv = ring[:, 1, 512:768]
        k_t = ring[:, 2, 0:DC * B * M].rearrange("p (c m) -> p c m", c=DC)
        gate_w = ring[:, 2, 700:704].rearrange("p (k c) -> p k c", k=2)
        q_mask = ring[:, 2, 704:704 + B * M].bitcast(I32)
        bias_all = ring[:, 3, 600:680]
        bias_left = ring[:, 3, 680:760]
        bias_part = [ring[:, 3, 760 + 40 * k:800 + 40 * k].bitcast(BF16) for k in range(3)]
        v_short = ring[:, 3, 0:B * H * (HD + 1)].rearrange("p (b h e) -> p b h e", b=B, h=H)
        print("arena words", top[0])

        rho_d = nc.dram_tensor("rho_d", (B, IT * RI, S), F32, kind="Internal").ap()
        rows_d = [nc.dram_tensor(f"rows_d{b}", ((MOE_TILES + 1) * P, D), F32, kind="Internal").ap() for b in range(B)]
        outs_d = [nc.dram_tensor(f"outs_d{b}", (MOE_TILES * P, D), F32, kind="Internal").ap() for b in range(B)]
        bias_d = nc.dram_tensor("bias_d", (3, E, FF + D), BF16, kind="Internal").ap()

        pa = ctx.enter_context(nc.psum_tensor("pa", [P, 3, 512], F32))
        pr = ctx.enter_context(nc.psum_tensor("pr", [P, 2, 512], F32))
        pc = [ctx.enter_context(nc.psum_tensor(f"pc{k}", [P, 512], F32)) for k in range(3)]
        pa_flat = pa[:, :, :].rearrange("p k n -> p (k n)")

        consts_in = sem("consts_in")
        weights_in = sem("weights_in")
        rows_in = sem("rows_in")
        gates_on = sem("gates_on")
        v_rest_in = sem("v_rest_in")
        setup_mm = sem("setup_mm")
        setup_step = sem("setup_step")
        setup_done = sem("setup_done")
        ones_set = sem("ones_set")
        var_ready = sem("var_ready")
        rstd_ready = sem("rstd_ready")
        xn_ready = sem("xn_ready")
        xn_turned = sem("xn_turned")
        xn_t_ready = sem("xn_t_ready")
        q_made = sem("q_made")
        q_ready = sem("q_ready")
        mask_ready = sem("mask_ready")
        scores_made = sem("scores_made")
        shifted = sem("shifted")
        exp_done = sem("exp_done")
        prob_turned = sem("prob_turned")
        prob_t_ready = sem("prob_t_ready")
        att_made = sem("att_made")
        att_ready = sem("att_ready")
        att_turned = sem("att_turned")
        att_t_ready = sem("att_t_ready")
        wo_made = sem("wo_made")
        up_made = sem("up_made")
        up_tanh = sem("up_tanh")
        up_ready = sem("up_ready")
        pq_made = sem("pq_made")
        pq_ready = sem("pq_ready")
        sims_made = sem("sims_made")
        e_in_ready = sem("e_in_ready")
        e_done = sem("e_done")
        g_made = sem("g_made")
        u_ready = sem("u_ready")
        u_tanh = sem("u_tanh")
        w_ready = sem("w_ready")
        w_turned = sem("w_turned")
        w_t_ready = sem("w_t_ready")
        ffn_made = sem("ffn_made")
        feat_made = sem("feat_made")
        dve_step = sem("dve_step")
        front_done = sem("front_done")
        setup_link = sem("setup_link")
        bias_split = sem("bias_split")
        bias_out = sem("bias_out")
        zeroed = sem("zeroed")
        experts_in = sem("experts_in")
        h_ready = sem("h_ready")
        h_used = sem("h_used")
        rho_ready = sem("rho_ready")
        rho_out = sem("rho_out")
        rho_in = sem("rho_in")
        rho_turned = sem("rho_turned")
        late_exp = sem("late_exp")
        late_exp_done = sem("late_exp_done")
        post_step = sem("post_step")
        late_step = sem("late_step")
        var4_ready = sem("var4_ready")
        rstd4_ready = sem("rstd4_ready")
        xn4_ready = sem("xn4_ready")
        xn4_turned = sem("xn4_turned")
        xn4_t_ready = sem("xn4_t_ready")
        router_made = sem("router_made")
        router_read = sem("router_read")
        pick_ready = sem("pick_ready")
        ranks_made = sem("ranks_made")
        slots_ready = sem("slots_ready")
        scattered = sem("scattered")
        row_landed = [sem(f"row_landed{k}") for k in range(2)]
        bias_landed = [sem(f"bias_landed{k}") for k in range(2)]
        row_turned = sem("row_turned")
        row_t_ready = sem("row_t_ready")
        hid_made = sem("hid_made")
        hid_ready = sem("hid_ready")
        hid_turned = sem("hid_turned")
        hid_t_ready = sem("hid_t_ready")
        y_made = sem("y_made")
        y_ready = sem("y_ready")
        y_stored = [sem(f"y_stored{k}") for k in range(2)]
        gathered = sem("gathered")
        batch_done = sem("batch_done")
        stored = sem("stored")

        CONSTS = 19
        fold_step = sem("fold_step")
        POST_STEPS = 5
        LATE_STEPS = 53
        FRONT_STEPS = 35

        ORDER = [(r, c, j) for r in range(TR) for c in range(DC) for j in range(4) if 4 * r + j < TI]

        block = ctx.enter_context(nc.Block())

        @block.sync
        def _(sp):
            small = [(ident, t["ident"]), (ctx_t, t["ctx_t"]), (wk, t["wk_t"]), (wv, t["wv_t"]), (w_txt, t["w_txt"]),
                     (headmask, t["headmask"]), (bk, t["bk"]), (bq, t["bq"]), (b_txt, t["b_txt"]),
                     (w_rho, t["w_rho"]), (w_router, t["w_router"]), (before, t["before"]), (gate_w, t["gate_w"]),
                     (gate_bias, t["gate_bias"].partition_broadcast(P)), (q_mask, t["q_mask"].partition_broadcast(P)),
                     (bias_all, t["expert_bias"]),
                     (bv, t["bv"].partition_broadcast(P)), (bo, t["bo"].partition_broadcast(P)),
                     (gate[:, 0:4], t["gates"].partition_broadcast(P))]
            for dst, src in small:
                sp.dma_start(dst, src).then_inc(consts_in, 16)
            for b in range(B):
                n = slice(b * NTB, (b + 1) * NTB)
                sp.dma_start(x[:, n, :], t["x"].rearrange("(i p) d -> p i d", p=P)[:, n, :]).then_inc(rows_in, 16)
                sp.dma_start(mask.rearrange("p (i m) -> p i m", i=NT)[:, n, :],
                             t["mask"].rearrange("(i p) m -> p i m", p=P)[:, n, :]).then_inc(rows_in, 16)
            for dst, src in [(wq, t["wq_t"]), (wo, t["wo_t"]), (w_up, t["w_up_t"]), (w_pq, t["w_pq_t"]), (keys, t["keys"]),
                             (de, t["de_t"]), (w_down, t["w_down_t"]), (ue, t["ue"]), (w_feat, t["w_feat"])]:
                sp.dma_start(dst, src).then_inc(weights_in, 16)
            sp.wait_ge(ones_set, 1)
            for b in range(B):
                sp.dma_start(rows_d[b].rearrange("(i p) d -> p i d", p=P),
                             zero_rows.unsqueeze(1).broadcast_to([P, MOE_TILES + 1, D])).then_inc(zeroed, 16)
            sp.wait_ge(ones_set, 3)
            for b in range(B):
                for j in range(TQ):
                    dst = v_rest[MT * j:MT * j + MT, b, :, 17 * j:17 * j + 17]
                    src = v_short[0:MT, b, :, :].rearrange("p (q j) e -> p q j e", j=TQ)[:, :, j, :]
                    sp.dma_start(dst, src).then_inc(v_rest_in, 16)
            sp.wait_ge(bias_split, 1)
            for k in range(3):
                sp.dma_start(bias_d[k].rearrange("e (q n) -> (e q) n", n=80), bias_part[k]).then_inc(bias_out, 16)

            def rho_round(b, it):
                n = b * IT + it
                sp.wait_ge(rho_ready, n + 2)
                for j in range(4):
                    sp.dma_start(rho_d[b, bass.ds(it * RI + j * TR, TR), :], rho_rows[32 * j:32 * j + TR, :]).then_inc(rho_out, 16)

            def rho_load(b):
                sp.wait_ge(rho_out, 64 * IT * (b + 1) + 64)
                if b:
                    sp.wait_ge(batch_done, b)
                sp.dma_start(rho_back[b][0:RI * IT // 2, :, :], rho_d[b].rearrange("(k p) n -> p k n", k=2)).then_inc(rho_in, 16)

            def experts_load():
                sp.wait_ge(front_done, 1)
                for e in range(E):
                    sp.dma_start(w1[:, e * DC * FF:(e + 1) * DC * FF], t["w1"][:, e * DC * FF:(e + 1) * DC * FF]).then_inc(experts_in, 16)
                    sp.dma_start(w2[:, e * FC * D:(e + 1) * FC * D], t["w2"][:, e * FC * D:(e + 1) * FC * D]).then_inc(experts_in, 16)

            for b in range(B):
                with sp.Fori(0, IT) as it:
                    rho_round(b, it)
                if b == 0:
                    experts_load()
                rho_load(b)
                sp.wait_ge(bias_out, 48)
                sp.wait_ge(scattered, 16 * 2 * NTB * (b + 1))
                owner_i = owner[0:1, b * MOE_TILES:(b + 1) * MOE_TILES].bitcast(I32)
                done = b * MOE_TILES
                with sp.Fori(0, MOE_TILES) as m:
                    sp.wait_ge(row_turned, m + done + 1)
                    sp.dma_start(row_in, rows_d[b][bass.ds(m * P, P), :]).then_inc(row_landed[0], 16)
                    e = sp.value_load(owner_i[:, bass.ds(m, 1)], min_val=0, max_val=E - 1)
                    sp.wait_ge(y_made, m + done + 1)
                    sp.dma_start(bias_rows[0:3, :], bias_d[:, bass.ds(e, 1), :].rearrange("k e n -> k (e n)")).then_inc(bias_landed[0], 16)
                    sp.wait_ge(y_ready, m + done + 1)
                    sp.dma_start(outs_d[b][bass.ds(m * P, P), :], row_out).then_inc(y_stored[0], 16)
                sp.wait_ge(batch_done, b + 1)
                sp.dma_start(out.rearrange("(i p) d -> p i d", p=P)[:, b * NTB:(b + 1) * NTB, :],
                             x[:, b * NTB:(b + 1) * NTB, :]).then_inc(stored, 16)
            sp.wait_ge(stored, 32)

        @block.gpsimd
        def _(pool):
            pool.memset(v_main[:, :, :, HD:HD + 1], 1.0)
            pool.memset(v_short[:, :, :, HD:HD + 1], 1.0)
            pool.memset(v_rest[:, :, :, :], 0.0)
            pool.memset(neg_half, -0.5)
            pool.memset(neg_half8, -0.5)
            pool.memset(ones3, 1.0)
            pool.iota(steps128, [[P, E]], base=0, channel_multiplier=0, allow_small_or_imprecise_dtypes=True)
            pool.iota(tile_no, [[1, MOE_TILES]], base=0, channel_multiplier=0, allow_small_or_imprecise_dtypes=True)
            pool.memset(zero_rows, 0.0)
            pool.iota(iota16, [[1, NX]], base=0, channel_multiplier=0,
                      allow_small_or_imprecise_dtypes=True).then_inc(ones_set, 1)

            def rstd_step(i, k):
                pool.wait_ge(var_ready, i * 3 + k + 1)
                nc.gpsimd.tensor_tensor(rstd, var_eps, neg_half, ALU.pow).then_inc(rstd_ready, 1)

            with pool.Fori(0, NT) as i:
                for k in range(3):
                    rstd_step(i, k)

            for b in range(B):
                with pool.Fori(b * NTB, (b + 1) * NTB) as i:
                    pool.wait_ge(var4_ready, i + 1)
                    nc.gpsimd.tensor_tensor(rstd, var_eps, neg_half, ALU.pow).then_inc(rstd4_ready, 1)
                pool.wait_ge(slots_ready, b + 1)
                pool.wait_ge(zeroed, 32)
                for n in range(NTB):
                    for k in range(2):
                        at = (b * 2 + k) * NTB + n
                        pool.indirect_dma_start(out=rows_d[b], out_offset=bass.IndirectOffsetOnAxis(ap=slots[:, at:at + 1].bitcast(U32), axis=0),
                                                in_=rows4[b][:, n, :], in_offset=None).then_inc(scattered, 16)
                pool.wait_ge(scattered, 16 * 2 * NTB * (b + 1))
                pool.wait_ge(y_stored[0], 16 * MOE_TILES * (b + 1) + 16)
                pool.wait_ge(y_made, (b + 1) * MOE_TILES + 1)
                pool.wait_ge(y_ready, (b + 1) * MOE_TILES)
                for n in range(NTB):
                    if n == NTB // 2:
                        pool.wait_ge(fold_step, (2 * b + 1) * NTB)
                    for k in range(2):
                        at = (b * 2 + k) * NTB + n
                        pool.indirect_dma_start(out=back[b][:, n % (NTB // 2), k, :], out_offset=None, in_=outs_d[b],
                                                in_offset=bass.IndirectOffsetOnAxis(ap=slots[:, at:at + 1].bitcast(U32), axis=0)).then_inc(gathered, 16)

        @block.scalar
        def _(act):
            act.wait_ge(consts_in, 16 * CONSTS)
            nc.scalar.activation(gate[:, 4:8], gate[:, 0:4], ACT.Tanh).then_inc(gates_on, 1)

            def front_a(i, g):
                act.wait_ge(shifted, i * 2 + g + 1)
                p = prob[:, g, :]
                nc.scalar.activation(p, p, ACT.Exp, scale=0.25).then_inc(exp_done, 1)

            def front_up(i):
                act.wait_ge(up_made, i + 1)
                nc.scalar.activation(up_act, pa_flat[:, 0:FF], ACT.Tanh, scale=0.5).then_inc(up_tanh, 1)

            def front_e(i):
                act.wait_ge(e_in_ready, i + 1)
                nc.scalar.activation(e_in[:, :, :], e_in[:, :, :], ACT.Exp).then_inc(e_done, 1)

            def front_u(i, g):
                act.wait_ge(u_ready, i * 3 + g + 1)
                if g == 0:
                    nc.scalar.activation(grid_rep, grid_b, ACT.Tanh, scale=0.5).then_inc(u_tanh, 1)
                else:
                    h = slice((g - 1) * 2 * NE, g * 2 * NE)
                    nc.scalar.activation(big2[:, h], big1[:, h], ACT.Tanh, scale=0.5).then_inc(u_tanh, 1)

            with act.Fori(0, NT) as i:
                front_a(i, 0)
                front_a(i, 1)
                front_up(i)
                front_e(i)
                for g in range(3):
                    front_u(i, g)

            def tanh_round(b, it):
                for k, (r, c, j) in enumerate(ORDER):
                    n = (it + b * IT) * len(ORDER) + k
                    act.wait_ge(h_used, n + 1)
                    tt = it * TI + (b * M + 4 * r + j)
                    nc.scalar.activation(ring[:, k % 4, :], feat_t[:, b, c, :], ACT.Tanh,
                                         bias=txt_bias[:, c, bass.ds(tt, 1)]).then_inc(h_ready, 1)

            act.wait_ge(bias_out, 48)
            act.wait_ge(v_rest_in, 16 * TQ * B)
            act.wait_ge(front_done, 1)
            for b in range(B):
                with act.Fori(0, IT) as it:
                    tanh_round(b, it)
                act.wait_ge(late_exp, 3 * b + 1)
                nc.scalar.activation(rho_t[:, :, :], rho_t[:, :, :], ACT.Exp).then_inc(late_exp_done, 1)
                act.wait_ge(late_exp, 3 * b + 2)
                nc.scalar.activation(gates3, gates3, ACT.Tanh).then_inc(late_exp_done, 1)
                act.wait_ge(late_exp, 3 * b + 3)
                nc.scalar.activation(route[:, 0:64], route[:, 0:64], ACT.Exp).then_inc(late_exp_done, 1)
                with act.Fori(0, MOE_TILES) as m:
                    n = m + b * MOE_TILES
                    act.wait_ge(hid_made, n + 1)
                    nc.scalar.activation(hid[b], pa_flat[:, 0:FF], ACT.Gelu_apprx_tanh).then_inc(hid_ready, 1)

        @block.vector
        def _(dve):
            steps = [0]

            def link(ins):
                steps[0] += 1
                ins.then_inc(setup_step, 1)
                dve.wait_ge(setup_step, steps[0])

            dve.sem_inc(rho_ready, 1)
            dve.sem_inc(rho_out, 64)
            dve.sem_inc(y_stored[0], 16)
            dve.wait_ge(consts_in, 16 * CONSTS)
            nc.vector.tensor_copy(ident_bf, ident)
            dve.wait_ge(setup_mm, 1)
            for c in range(DC):
                v = nc.vector.tensor_scalar(txt_bias[:, c, :], pc[c][:, 0:B * M], b_txt[:, c:c + 1], None, ALU.add)
            link(v)
            dve.wait_ge(setup_mm, 2)
            for c in range(DC):
                v = nc.vector.tensor_scalar(k_t[:, c, :], pa[:, c, 0:B * M], bk[:, c:c + 1], None, ALU.add)
            link(v)
            kb = k_blocks.rearrange("p (b g n) -> p b g n", b=B, g=DC)
            for g in range(DC):
                for h in range(HG):
                    for dst, m0, m1 in ((h * P, 0, P), (HG * P + h * MT, P, M)):
                        v = nc.vector.tensor_scalar(kb[:, :, g, dst:dst + m1 - m0],
                                                    k_t[:, g, :].rearrange("p (b m) -> p b m", b=B)[:, :, m0:m1],
                                                    headmask[:, h:h + 1], None, ALU.mult)
            dve.wait_ge(setup_mm, 3)
            dve.wait_ge(ones_set, 1)
            bv_h = bv.rearrange("p (h e) -> p h e", h=H)
            for b in range(B):
                nc.vector.tensor_tensor(v_main[:, b, :, 0:HD], pr[:, b, 0:D].rearrange("p (h e) -> p h e", h=H),
                                        bv_h, ALU.add)
                v = nc.vector.tensor_tensor(v_short[0:MT, b, :, 0:HD],
                                            pr[0:MT, b, D:2 * D].rearrange("p (h e) -> p h e", h=H),
                                            bv_h[0:MT], ALU.add)
                v.then_inc(ones_set, 1)
            dve.wait_ge(gates_on, 1)
            nc.vector.tensor_scalar(gate[:, 6:7], gate[:, 6:7], 0.5, None, ALU.mult).then_inc(setup_done, 1)
            dve.wait_ge(setup_done, 1)
            dve.wait_ge(rows_in, 64)
            link(nc.vector.tensor_scalar(mask_bias, mask, 0.0, MASKED, ALU.is_equal, ALU.mult))
            nc.vector.memset(window[:, :, :], 0.0)
            nc.vector.memset(q_bias[:, :, :], -FAR)
            nc.vector.memset(gate_rows[:, :, :, :], 0.0)
            link(nc.vector.memset(ones, 1.0))
            for c in range(DC):
                nc.vector.tensor_copy(window[:, c, 31:32], w_rho[:, c:c + 1])
            dve.wait_ge(setup_mm, 4)
            for r0, r1, nj in ((0, TR - 1, 4), (TR - 1, TR, 2)):
                for b in range(B):
                    for jj in range(nj):
                        for src, dst in ((q_mask[:, b * M:(b + 1) * M], q_bias[:, b, :]),
                                         (pr[:, 0, b * M:(b + 1) * M], gate_rows[:, 0, b, :]),
                                         (pr[:, 1, b * M:(b + 1) * M], gate_rows[:, 1, b, :])):
                            n = r1 - r0
                            sv = src.rearrange("p (i t) -> p i t", i=IT)[:, :, 4 * r0 + jj:4 * (r1 - 1) + jj + 1:4]
                            dv = dst.rearrange("p (i j r) -> p i j r", i=IT, j=4)[:, :, jj, r0:r1]
                            if src.dtype == I32:
                                v = nc.vector.tensor_scalar(dv, sv, -NEG, NEG, ALU.mult, ALU.add)
                            else:
                                v = nc.vector.tensor_copy(dv, sv)
            link(v)
            link(nc.vector.tensor_copy(bias_part[0], bias_all))
            link(nc.vector.tensor_tensor(bias_left, bias_all, bias_part[0], ALU.subtract))
            link(nc.vector.tensor_copy(bias_part[1], bias_left))
            link(nc.vector.tensor_tensor(bias_left, bias_left, bias_part[1], ALU.subtract))
            nc.vector.tensor_copy(bias_part[2], bias_left).then_inc(bias_split, 1)
            dve.wait_ge(bias_split, 1)

            def front(i, b):
                n = [0]
                xi = x[:, bass.ds(i, 1), :].rearrange("p i d -> p (i d)")

                def link(ins, plain=False):
                    n[0] += 1
                    ins.then_inc(dve_step, 1)
                    dve.wait_ge(dve_step, i * FRONT_STEPS + n[0])
                    if plain:
                        nc.vector.memset(carrier, 0.0)

                def norm(k):
                    link(nc.vector.bn_stats(bn, xi), plain=True)
                    link(nc.vector.bn_aggr(stat, bn))
                    nc.vector.tensor_scalar(var_eps, stat[:, 1:2], EPS, None, ALU.add).then_inc(var_ready, 1)
                    dve.wait_ge(rstd_ready, i * 3 + k + 1)
                    if k == 2:
                        nc.vector.tensor_copy(mean3[:, bass.ds(i, 1)], stat[:, 0:1])
                        nc.vector.tensor_copy(rstd3[:, bass.ds(i, 1)], rstd)
                    nc.vector.tensor_scalar(xn, xi, stat[:, 0:1], rstd, ALU.subtract, ALU.mult).then_inc(xn_ready, 1)
                    dve.wait_ge(xn_turned, i * 3 + k + 1)
                    nc.vector.tensor_copy(xn_t[:, :, :].rearrange("p c n -> p (c n)"), pc[0][:, 0:D]).then_inc(xn_t_ready, 1)

                norm(0)
                dve.wait_ge(q_made, i + 1)
                for c in range(DC):
                    v = nc.vector.tensor_scalar(q_t[:, c, :], pc[1][:, c * P:(c + 1) * P], bq[:, c:c + 1], None, ALU.add)
                v.then_inc(q_ready, 1)
                for g in range(DC):
                    dve.wait_ge(scores_made, i * 2 + g + 1)
                    first = pa_flat[:, 0:HG * P].rearrange("p (h m) -> p h m", h=HG)
                    rest = pa_flat[:, HG * P:HG * M].rearrange("p (h m) -> p h m", h=HG)
                    nc.vector.tensor_reduce(row_max, first, AX.X, ALU.max)
                    link(nc.vector.tensor_reduce(rest_max, rest, AX.X, ALU.max))
                    link(nc.vector.tensor_tensor(row_max, row_max, rest_max, ALU.max))
                    mx = row_max.unsqueeze(2)
                    nc.vector.tensor_tensor(prob[:, g, 0:HG * P].rearrange("p (h m) -> p h m", h=HG), first,
                                            mx.broadcast_to([P, HG, P]), ALU.subtract)
                    nc.vector.tensor_tensor(prob[:, g, HG * P:HG * M].rearrange("p (h m) -> p h m", h=HG), rest,
                                            mx.broadcast_to([P, HG, MT]), ALU.subtract).then_inc(shifted, 1)
                for k in range(5):
                    dve.wait_ge(prob_turned, i * 5 + k + 1)
                    rows = P if k < 4 else TQ * MT
                    nc.vector.tensor_copy(prob_t[0:rows, k, :], pc[k % 2][0:rows, :]).then_inc(prob_t_ready, 1)
                dve.wait_ge(att_made, i + 1)
                o = pc[2][:, 0:H * (HD + 1)].rearrange("p (h e) -> p h e", h=H)
                link(nc.vector.reciprocal(r_den.unsqueeze(2), o[:, :, HD:HD + 1]))
                nc.vector.tensor_tensor(att.rearrange("p (h e) -> p h e", h=H), o[:, :, 0:HD],
                                        r_den.unsqueeze(2).broadcast_to([P, H, HD]), ALU.mult).then_inc(att_ready, 1)
                dve.wait_ge(att_turned, i + 1)
                nc.vector.tensor_copy(att_t[:, :, :].rearrange("p c n -> p (c n)"), pc[0][:, 0:D]).then_inc(att_t_ready, 1)
                dve.wait_ge(wo_made, i + 1)
                link(nc.vector.tensor_tensor(proj, pc[1][:, 0:D], bo, ALU.add))
                link(nc.vector.scalar_tensor_tensor(xi, proj, gate[:, 4:5], xi, ALU.mult, ALU.add), plain=True)

                norm(1)
                dve.wait_ge(pq_made, i + 1)
                nc.vector.tensor_copy(pq_t, pc[1][:, :]).then_inc(pq_ready, 1)
                dve.wait_ge(up_tanh, i + 1)
                nc.vector.scalar_tensor_tensor(up_t, up_act, 1.0, pa_flat[:, 0:FF], ALU.add, ALU.mult).then_inc(up_ready, 1)
                dve.wait_ge(sims_made, i + 1)
                link(nc.vector.tensor_copy(scores, pc[0][:, :]), plain=True)
                for r in range(2 * PH):
                    v = nc.vector.max(top_xy[:, 8 * r:8 * r + 8], scores[:, NK * r:NK * r + NK])
                link(v, plain=True)
                idx_u = idx.bitcast(U32)
                for h in range(PH):
                    nc.vector.max_index(idx_u[:, 8 * h:8 * h + 8], top_xy[:, 8 * h:8 * h + 8], scores[:, NK * h:NK * h + NK])
                tx = top_xy[:, 0:32].rearrange("p (h k) -> p h k", h=PH)
                ty = top_xy[:, 32:64].rearrange("p (h k) -> p h k", h=PH)
                g4 = grid.rearrange("p (h i j) -> p h i j", h=PH, i=8)
                link(nc.vector.tensor_tensor(g4, tx.unsqueeze(3).broadcast_to([P, PH, 8, 8]),
                                             ty.unsqueeze(2).broadcast_to([P, PH, 8, 8]), ALU.add), plain=True)
                for h in range(PH):
                    v = nc.vector.max(top_s[:, 8 * h:8 * h + 8], grid[:, 64 * h:64 * h + 64])
                link(v)
                sc = scores.rearrange("p (r k) -> p r k", k=NK)
                ts = top_s.rearrange("p (h k) -> p h k", h=PH)
                for at, src, best in ((0, sc[:, 0:PH, 0:NX], tx), (16, sc[:, PH:2 * PH, :], ty), (80, ts, ts), (88, tx, tx), (96, ty, ty)):
                    w = src.shape[2]
                    v = nc.vector.tensor_tensor(e_in[:, :, at:at + w], src, best[:, :, 0:1].broadcast_to([P, PH, w]), ALU.subtract)
                v.then_inc(e_in_ready, 1)
                nc.vector.tensor_copy(idx_f, idx_u)
                for h in range(PH):
                    v = nc.vector.match_replace(grid_rep[:, 64 * h:64 * h + 64], top_s[:, 8 * h:8 * h + 8],
                                                grid[:, 64 * h:64 * h + 64], -FAR)
                link(v)
                nc.vector.tensor_scalar(far_off, idx_f, float(NX), None, ALU.is_ge)
                link(nc.vector.tensor_tensor(grid_sel, grid_rep, grid, ALU.not_equal))
                link(nc.vector.tensor_scalar(grid_b, grid_sel, 0.0, FAR, ALU.is_equal, ALU.mult))
                gb4 = grid_b.rearrange("p (h i j) -> p h i j", h=PH, i=8)
                link(nc.vector.tensor_tensor(gb4, gb4, ty.unsqueeze(2).broadcast_to([P, PH, 8, 8]), ALU.add))
                t8_ = t8.rearrange("p (h i) -> p h i", h=PH)
                c4 = cmp16.rearrange("p (h x i) -> p h x i", h=PH, x=NX)
                nc.vector.tensor_reduce(t8_, gb4, AX.X, ALU.min)
                link(nc.vector.tensor_tensor(c4, idx_f.rearrange("p (h i) -> p h i", h=PH).unsqueeze(2).broadcast_to([P, PH, NX, 8]),
                                             iota16.unsqueeze(1).unsqueeze(3).broadcast_to([P, PH, NX, 8]), ALU.not_equal))
                link(nc.vector.tensor_scalar(cmp16, cmp16, FAR, None, ALU.mult))
                link(nc.vector.tensor_tensor(c4, c4, t8_.unsqueeze(2).broadcast_to([P, PH, NX, 8]), ALU.max))
                t16_ = t16.rearrange("p (h x) -> p h x", h=PH)
                link(nc.vector.tensor_reduce(t16_, c4, AX.X, ALU.min))
                b4 = big1.rearrange("p (h x y) -> p h x y", h=PH, x=NX)
                link(nc.vector.tensor_tensor(b4, sc[:, PH:2 * PH, :].unsqueeze(2).broadcast_to([P, PH, NX, NK]),
                                             t16_.unsqueeze(3).broadcast_to([P, PH, NX, NK]), ALU.is_ge))
                dve.wait_ge(e_done, i + 1)
                nc.vector.tensor_tensor(b4, b4, e_in[:, :, 16:80].unsqueeze(2).broadcast_to([P, PH, NX, NK]), ALU.mult)
                link(nc.vector.tensor_reduce(den4, e_in[:, :, 80:88], AX.X, ALU.add))
                link(nc.vector.reciprocal(den4, den4))
                d4 = den4.unsqueeze(2)
                nc.vector.tensor_tensor(e_in[:, :, 0:16], e_in[:, :, 0:16], d4.broadcast_to([P, PH, 16]), ALU.mult)
                link(nc.vector.tensor_tensor(e_in[:, :, 88:96], e_in[:, :, 88:96], d4.broadcast_to([P, PH, 8]), ALU.mult))
                nc.vector.tensor_tensor(b4, b4, e_in[:, :, 0:16].unsqueeze(3).broadcast_to([P, PH, NX, NK]), ALU.mult)
                link(nc.vector.tensor_tensor(e_in[:, :, 88:96], e_in[:, :, 88:96], far_off.rearrange("p (h i) -> p h i", h=PH), ALU.mult))
                link(nc.vector.tensor_tensor(gb4, grid_sel.rearrange("p (h i j) -> p h i j", h=PH, i=8),
                                             e_in[:, :, 88:96].unsqueeze(3).broadcast_to([P, PH, 8, 8]), ALU.mult))
                link(nc.vector.tensor_tensor(gb4, gb4, e_in[:, :, 96:104].unsqueeze(2).broadcast_to([P, PH, 8, 8]), ALU.mult))
                dve.wait_ge(g_made, i + 1)
                nc.vector.tensor_scalar(grid_b, grid_b, pa_flat[:, NE - 1:NE], None, ALU.mult).then_inc(u_ready, 1)
                for g in range(2):
                    bh = big1[:, g * 2 * NE:(g + 1) * 2 * NE].rearrange("p (h e) -> p h e", h=2)
                    nc.vector.tensor_tensor(bh, bh, pa_flat[:, 0:NE].unsqueeze(1).broadcast_to([P, 2, NE]),
                                            ALU.mult).then_inc(u_ready, 1)
                dve.wait_ge(u_tanh, i * 3 + 1)
                nc.vector.scalar_tensor_tensor(grid, grid_rep, 1.0, grid_b, ALU.add, ALU.mult, accum_out=last_sum)
                for g in range(2):
                    dve.wait_ge(u_tanh, i * 3 + g + 2)
                    h = slice(g * 2 * NE, (g + 1) * 2 * NE)
                    v = nc.vector.scalar_tensor_tensor(big1[:, h], big2[:, h], 1.0, big1[:, h], ALU.add, ALU.mult)
                link(v)
                nc.vector.tensor_scalar(big1[:, NE - 1:NE], big1[:, NE - 1:NE], last_sum, None, ALU.add).then_inc(w_ready, 1)
                for k in range(2):
                    dve.wait_ge(w_turned, i * 2 + k + 1)
                    nc.vector.tensor_copy(big2[:, 512 * k:512 * k + 512], pc[k][:, :]).then_inc(w_t_ready, 1)
                dve.wait_ge(ffn_made, i + 1)
                link(nc.vector.scalar_tensor_tensor(xi, pc[2][:, 0:D], gate[:, 6:7], xi, ALU.mult, ALU.add), plain=True)

                norm(2)
                dve.wait_ge(feat_made, i + 1)
                f = feat_t[:, b, :, bass.ds((i - b * NTB) * P, P)]
                link(nc.vector.tensor_copy(f, pc[1][:, 0:D].rearrange("p (c n) -> p c n", c=DC)))
                assert n[0] == FRONT_STEPS, n[0]

            for b in range(B):
                with dve.Fori(b * NTB, (b + 1) * NTB) as i:
                    front(i, b)
            nc.vector.memset(last_sum, 0.0).then_inc(front_done, 1)

            def rho_round(b, it):
                n = b * IT + it
                dve.wait_ge(h_used, (n + 1) * len(ORDER) + 4)
                dve.wait_ge(rho_out, n * 64 + 64)
                nc.vector.tensor_copy(rho_rows, pr[:, :, :].rearrange("p k n -> p (k n)")).then_inc(rho_ready, 1)

            dve.wait_ge(zeroed, 32)

            def attend(b):
                n = [0]

                def link(ins):
                    n[0] += 1
                    ins.then_inc(late_step, 1)
                    dve.wait_ge(late_step, b * LATE_STEPS + n[0])

                def wide(a, w):
                    return a.unsqueeze(2).broadcast_to([P, NTB, w])

                dve.wait_ge(rho_turned, b + 1)
                R = IT * RI
                for k in range(3):
                    i0, i1 = 3 * k, min(3 * k + 3, NTB)
                    v = nc.vector.tensor_tensor(rho_t[:, i0:i1, :], pa[:, k, 0:(i1 - i0) * R].rearrange("p (i n) -> p i n", n=R),
                                                q_bias[:, b, :].unsqueeze(1).broadcast_to([P, i1 - i0, R]), ALU.add)
                link(v)
                mx, den, dot = dots[:, 0:NTB], dots[:, NTB:2 * NTB], dots[:, 2 * NTB:4 * NTB].rearrange("p (k i) -> p k i", k=2)
                link(nc.vector.tensor_reduce(mx, rho_t, AX.X, ALU.max))
                nc.vector.tensor_tensor(rho_t, rho_t, wide(mx, R), ALU.subtract).then_inc(late_exp, 1)
                dve.wait_ge(late_exp_done, 3 * b + 1)
                nc.vector.tensor_reduce(den, rho_t, AX.X, ALU.add)
                hn = NTB // 2
                for k in range(2):
                    for h in range(0, NTB, hn):
                        link(nc.vector.tensor_tensor(rho_w, rho_t[:, h:h + hn, :],
                                                     gate_rows[:, k, b, :].unsqueeze(1).broadcast_to([P, hn, R]), ALU.mult))
                        link(nc.vector.tensor_reduce(dot[:, k, h:h + hn], rho_w, AX.X, ALU.add))
                link(nc.vector.reciprocal(den, den))
                g3 = gates3.rearrange("p (k i) -> p k i", k=2)
                link(nc.vector.tensor_tensor(g3, dot, den.unsqueeze(1).broadcast_to([P, 2, NTB]), ALU.mult))
                nc.vector.tensor_tensor(g3, g3, gate_bias.unsqueeze(2).broadcast_to([P, 2, NTB]), ALU.add).then_inc(late_exp, 1)
                dve.wait_ge(late_exp_done, 3 * b + 2)
                link(nc.vector.tensor_scalar(gates3, gates3, gate[:, 5:6], None, ALU.mult))
                assert n[0] == 13, n[0]

            def post(i, b):
                n = [0]
                xi = x[:, bass.ds(i, 1), :].rearrange("p i d -> p (i d)")

                def link(ins, plain=False):
                    n[0] += 1
                    ins.then_inc(post_step, 1)
                    dve.wait_ge(post_step, i * POST_STEPS + n[0])
                    if plain:
                        nc.vector.memset(carrier4, 0.0)

                m = i - b * NTB
                link(nc.vector.tensor_scalar(xn4, xi, mean3[:, bass.ds(i, 1)], rstd3[:, bass.ds(i, 1)], ALU.subtract, ALU.mult))
                link(nc.vector.tensor_scalar(xn4, xn4, gates3[:, bass.ds(m, 1)], gates3[:, bass.ds(m + NTB, 1)], ALU.mult, ALU.add))
                link(nc.vector.tensor_tensor(xi, xi, xn4, ALU.add), plain=True)
                link(nc.vector.bn_stats(bn4, xi), plain=True)
                link(nc.vector.bn_aggr(stat4, bn4))
                nc.vector.tensor_scalar(var_eps, stat4[:, 1:2], EPS, None, ALU.add).then_inc(var4_ready, 1)
                dve.wait_ge(rstd4_ready, i + 1)
                r4 = rows4[b][:, bass.ds(m, 1), :].rearrange("p i d -> p (i d)")
                nc.vector.tensor_scalar(r4, xi, stat4[:, 0:1], rstd, ALU.subtract, ALU.mult)
                nc.vector.tensor_scalar(xn4, xi, stat4[:, 0:1], rstd, ALU.subtract, ALU.mult).then_inc(xn4_ready, 1)
                dve.wait_ge(xn4_turned, i + 1)
                nc.vector.tensor_copy(xn4_t[:, :, :].rearrange("p c n -> p (c n)"), pc[0][:, 0:D]).then_inc(xn4_t_ready, 1)
                dve.wait_ge(router_made, i + 1)
                nc.vector.tensor_copy(logits[:, bass.ds(m * E, E)], pc[1][:, 0:E]).then_inc(router_read, 1)
                assert n[0] == POST_STEPS, n[0]

            def routing(b):
                n = [13]

                def link(ins):
                    n[0] += 1
                    ins.then_inc(late_step, 1)
                    dve.wait_ge(late_step, b * LATE_STEPS + n[0])

                T = NTB * E
                part = [route[:, k * T:(k + 1) * T] for k in range(12)]
                v3 = [a.rearrange("p (i e) -> p i e", i=NTB) for a in part]
                best, ids, hot = part[1], part[2], [v3[3], v3[4]]
                dve.wait_ge(router_read, (b + 1) * NTB)
                for i in range(NTB):
                    v = nc.vector.max(best[:, i * E:(i + 1) * E], logits[:, i * E:(i + 1) * E])
                link(v)
                for i in range(NTB):
                    v = nc.vector.max_index(ids.bitcast(U32)[:, i * E:(i + 1) * E], best[:, i * E:(i + 1) * E], logits[:, i * E:(i + 1) * E])
                link(v)
                nc.vector.tensor_tensor(v3[0], v3[1], v3[1][:, :, 0:1].broadcast_to([P, NTB, E]), ALU.subtract).then_inc(late_exp, 1)
                link(nc.vector.tensor_copy(part[5], ids.bitcast(U32)))
                for k in range(2):
                    v = nc.vector.tensor_tensor(hot[k], v3[5][:, :, k:k + 1].broadcast_to([P, NTB, E]),
                                                iota16[:, 0:E].unsqueeze(1).broadcast_to([P, NTB, E]), ALU.is_equal)
                link(v)
                nc.vector.tensor_tensor(part[6], part[3], part[4], ALU.add).then_inc(pick_ready, 1)
                dve.wait_ge(late_exp_done, 3 * b + 3)
                link(nc.vector.tensor_reduce(dots[:, 0:NTB], v3[0], AX.X, ALU.add))
                link(nc.vector.reciprocal(dots[:, 0:NTB], dots[:, 0:NTB]))
                pk = picks[:, b * 2 * NTB:(b + 1) * 2 * NTB].rearrange("p (k i) -> p i k", k=2)
                link(nc.vector.tensor_tensor(pk, v3[0][:, :, 0:2], dots[:, 0:NTB].unsqueeze(2).broadcast_to([P, NTB, 2]), ALU.mult))
                link(nc.vector.tensor_reduce(dots[:, NTB:2 * NTB], pk, AX.X, ALU.add))
                link(nc.vector.tensor_scalar(dots[:, NTB:2 * NTB], dots[:, NTB:2 * NTB], 1e-8, None, ALU.add))
                link(nc.vector.reciprocal(dots[:, NTB:2 * NTB], dots[:, NTB:2 * NTB]))
                link(nc.vector.tensor_tensor(pk, pk, dots[:, NTB:2 * NTB].unsqueeze(2).broadcast_to([P, NTB, 2]), ALU.mult))
                pf = picks[:, b * 2 * NTB:(b + 1) * 2 * NTB]
                nc.vector.tensor_scalar(pf, pf, gate[:, 7:8], None, ALU.mult)
                dve.wait_ge(ranks_made, b + 1)
                rank, total, first = part[7], part[8], part[9]
                nc.vector.tensor_copy(rank, pc[0][:, 0:T])
                nc.vector.tensor_copy(total, pc[0][:, T:2 * T])
                link(nc.vector.memset(first, 0.0))
                for i in range(1, NTB):
                    link(nc.vector.tensor_tensor(v3[9][:, i, :], v3[9][:, i - 1, :], v3[8][:, i - 1, :], ALU.add))
                cnt, tiles, start = part[0][:, 0:E], part[0][:, E:2 * E], part[0][:, 2 * E:3 * E]
                link(nc.vector.tensor_tensor(cnt, v3[9][:, NTB - 1, :], v3[8][:, NTB - 1, :], ALU.add))
                link(nc.vector.tensor_tensor(v3[10], cnt.unsqueeze(2).broadcast_to([P, E, E]),
                                             steps128.unsqueeze(1).broadcast_to([P, E, E]), ALU.is_gt))
                nc.vector.memset(start, 0.0)
                link(nc.vector.tensor_reduce(tiles, v3[10], AX.X, ALU.add))
                for e in range(1, E):
                    link(nc.vector.tensor_tensor(start[:, e:e + 1], start[:, e - 1:e], tiles[:, e - 1:e], ALU.add))
                link(nc.vector.tensor_scalar(tiles, start, float(P), None, ALU.mult))
                link(nc.vector.tensor_tensor(rank, rank, first, ALU.add))
                link(nc.vector.tensor_tensor(v3[7], v3[7], tiles.unsqueeze(1).broadcast_to([P, NTB, E]), ALU.add))
                for k in range(2):
                    link(nc.vector.tensor_tensor(v3[10], hot[k], v3[7], ALU.mult))
                    link(nc.vector.tensor_reduce(dots[:, 0:NTB], v3[10], AX.X, ALU.add))
                    link(nc.vector.tensor_copy(slots[:, (b * 2 + k) * NTB:(b * 2 + k + 1) * NTB].bitcast(I32), dots[:, 0:NTB]))
                own = own_w[:, 0:MOE_TILES * E].rearrange("p (m e) -> p m e", e=E)
                link(nc.vector.tensor_tensor(own, tile_no.unsqueeze(2).broadcast_to([P, MOE_TILES, E]),
                                             start.unsqueeze(1).broadcast_to([P, MOE_TILES, E]), ALU.is_ge))
                link(nc.vector.tensor_reduce(own_w[:, 192:192 + MOE_TILES], own, AX.X, ALU.add))
                nc.vector.tensor_scalar(owner[:, b * MOE_TILES:(b + 1) * MOE_TILES].bitcast(I32), own_w[:, 192:192 + MOE_TILES],
                                        -1.0, None, ALU.add).then_inc(slots_ready, 1)
                assert n[0] == LATE_STEPS, n[0]

            def experts(b):
                done = b * MOE_TILES

                def take_rows(m):
                    dve.wait_ge(row_turned, m + done + 2)
                    nc.vector.tensor_copy(row_t, pc[0][:, 0:D]).then_inc(row_t_ready, 1)

                def take_hid(m):
                    for k in range(2):
                        dve.wait_ge(hid_turned, (m + done) * 2 + k + 1)
                        nc.vector.tensor_copy(hid_t[b][:, 512 * k:512 * k + 512], pc[1 + k][:, :]).then_inc(hid_t_ready, 1)

                def take_y(m):
                    dve.wait_ge(y_made, m + done + 2)
                    dve.wait_ge(y_stored[0], (m + done) * 16 + 16)
                    nc.vector.tensor_copy(row_out, pa[:, 2, 0:D]).then_inc(y_ready, 1)

                with dve.Fori(0, MOE_TILES) as m:
                    take_rows(m)
                    take_hid(m)
                    take_y(m)

            def combine(b):
                for n in range(NTB):
                    if n % (NTB // 2) == 0:
                        dve.wait_ge(gathered, 16 * (2 * NTB * b + 2 * n + NTB))
                    i = b * NTB + n
                    for k in range(2):
                        at = (b * 2 + k) * NTB + n
                        v = nc.vector.scalar_tensor_tensor(x[:, i, :], back[b][:, n % (NTB // 2), k, :], picks[:, at:at + 1], x[:, i, :], ALU.mult, ALU.add)
                        v.then_inc(fold_step, 1)
                        dve.wait_ge(fold_step, at_count(b, n, k))
                nc.vector.memset(last_sum, 0.0).then_inc(batch_done, 1)

            def at_count(b, n, k):
                return (b * NTB + n) * 2 + k + 1

            for b in range(B):
                with dve.Fori(0, IT) as it:
                    rho_round(b, it)
                attend(b)
                with dve.Fori(b * NTB, (b + 1) * NTB) as i:
                    post(i, b)
                routing(b)
                experts(b)
                combine(b)

        @block.tensor
        def _(pe):
            mm = nc.tensor.matmul
            pe.sem_inc(h_used, 4)
            pe.sem_inc(row_turned, 1)
            pe.sem_inc(y_made, 1)
            pe.wait_ge(consts_in, 16 * CONSTS)
            for c in range(DC):
                for k in range(DC):
                    v = mm(pc[c][:, 0:B * M], w_txt[:, k, c * P:(c + 1) * P], ctx_t[:, k, :], start=k == 0, stop=k == 1)
            v.then_inc(setup_mm, 1)
            for c in range(DC):
                for k in range(DC):
                    v = mm(pa[:, c, 0:B * M], wk[:, k, c * P:(c + 1) * P], ctx_t[:, k, :], start=k == 0, stop=k == 1)
            v.then_inc(setup_mm, 1)
            for b in range(B):
                for at, m in ((0, P), (P, MT)):
                    for k in range(DC):
                        v = mm(pr[0:m, b, at * 2:at * 2 + D], ctx_t[:, k, b * M + at:b * M + at + m], wv[:, k, :],
                               start=k == 0, stop=k == 1)
            v.then_inc(setup_mm, 1)
            pe.wait_ge(setup_done, 1)
            for k in range(2):
                for c in range(DC):
                    v = mm(pr[:, k, 0:B * M], gate_w[:, k, c:c + 1].broadcast_to([P, P]), ctx_t[:, c, :], start=c == 0, stop=c == 1)
            v.then_inc(setup_mm, 1)
            pe.wait_ge(weights_in, 16 * 9)
            pe.wait_ge(v_rest_in, 16 * 8)
            pe.wait_ge(setup_done, 1)

            def turn_rows(i, k):
                pe.wait_ge(xn_ready, i * 3 + k + 1)
                for c in range(DC):
                    v = nc.tensor.transpose(pc[0][:, c * P:(c + 1) * P], xn[:, c * P:(c + 1) * P], ident)
                v.then_inc(xn_turned, 1)
                pe.wait_ge(xn_t_ready, i * 3 + k + 1)

            def front_attention(i, b):
                turn_rows(i, 0)
                for g in range(DC):
                    for k in range(DC):
                        v = mm(pc[1][:, g * P:(g + 1) * P], wq[:, k, g * P:(g + 1) * P], xn_t[:, k, :], start=k == 0, stop=k == 1)
                v.then_inc(q_made, 1)
                pe.wait_ge(q_ready, i + 1)
                for g in range(DC):
                    if g:
                        pe.wait_ge(shifted, i * 2 + g)
                    for k, (nh, m0, m1) in enumerate(((TQ, 0, P), (TQ, 0, P), (HG, P, M))):
                        at = (b * DC + g) * HG * M + 512 * k
                        n = nh * (m1 - m0)
                        mm(pa[:, k, 0:n], q_t[:, g, :], k_blocks[:, at:at + n], start=True, stop=False)
                        v = mm(pa[:, k, 0:n], ident_bf, mask_bias[:, bass.ds(i * M + m0, m1 - m0)].unsqueeze(1).broadcast_to([P, nh, m1 - m0]),
                               start=False, stop=True)
                    v.then_inc(scores_made, 1)
                for k in range(5):
                    if k in (0, 2):
                        pe.wait_ge(exp_done, i * 2 + k // 2 + 1)
                    if k >= 2:
                        pe.wait_ge(prob_t_ready, i * 5 + k - 1)
                    for j in range(TQ):
                        if k < 4:
                            v = nc.tensor.transpose(pc[k % 2][:, j * P:(j + 1) * P], prob[:, k // 2, (TQ * (k % 2) + j) * P:(TQ * (k % 2) + j + 1) * P], ident)
                        else:
                            v = nc.tensor.transpose(pc[k % 2][0:TQ * MT, j * P:(j + 1) * P],
                                                    prob[:, j // 2, HG * P + (j % 2) * TQ * MT:HG * P + (j % 2 + 1) * TQ * MT], ident)
                    v.then_inc(prob_turned, 1)
                pe.wait_ge(prob_t_ready, i * 5 + 5)
                E1 = HD + 1
                for q in range(H // TQ):
                    mm(pc[2][:, q * TQ * E1:(q + 1) * TQ * E1], prob_t[0:TQ * MT, 4, q * P:(q + 1) * P],
                       v_rest[0:TQ * MT, b, q, :], start=True, stop=False)
                    for j in range(TQ):
                        h = TQ * q + j
                        v = mm(pc[2][:, h * E1:(h + 1) * E1], prob_t[:, q, j * P:(j + 1) * P], v_main[:, b, h, :],
                               start=False, stop=j == TQ - 1)
                v.then_inc(att_made, 1)
                pe.wait_ge(att_ready, i + 1)
                for c in range(DC):
                    v = nc.tensor.transpose(pc[0][:, c * P:(c + 1) * P], att[:, c * P:(c + 1) * P], ident)
                v.then_inc(att_turned, 1)
                pe.wait_ge(att_t_ready, i + 1)
                for k in range(DC):
                    v = mm(pc[1][:, 0:D], att_t[:, k, :], wo[:, k, :], start=k == 0, stop=k == 1)
                v.then_inc(wo_made, 1)

            def front_ffn(i):
                turn_rows(i, 1)
                for e in range(4):
                    for k in range(DC):
                        v = mm(pc[1][:, e * P:(e + 1) * P], w_pq[:, k, e * P:(e + 1) * P], xn_t[:, k, :], start=k == 0, stop=k == 1)
                v.then_inc(pq_made, 1)
                for f in range(FC):
                    for k in range(DC):
                        v = mm(pa_flat[:, f * P:(f + 1) * P], w_up[:, k, f * P:(f + 1) * P], xn_t[:, k, :], start=k == 0, stop=k == 1)
                v.then_inc(up_made, 1)
                pe.wait_ge(pq_ready, i + 1)
                for e in range(4):
                    v = mm(pc[0][:, e * P:(e + 1) * P], pq_t[:, e * P:(e + 1) * P], keys[:, e, :], start=True, stop=True)
                v.then_inc(sims_made, 1)
                pe.wait_ge(up_ready, i + 1)
                for n in range(2):
                    for k in range(DC):
                        v = mm(pa[:, n, :], xn_t[:, k, :], de[:, k, n * 512:(n + 1) * 512], start=k == 0, stop=k == 1)
                v.then_inc(g_made, 1)
                for f in range(FC):
                    mm(pc[2][:, 0:D], up_t[:, f * P:(f + 1) * P], w_down[:, f, :], start=f == 0, stop=False)
                pe.wait_ge(w_ready, i + 1)
                for e in range(NE // P):
                    for h in range(PH):
                        v = mm(pc[e // 4][:, (e % 4) * P:(e % 4 + 1) * P], big1[:, h * NE + e * P:h * NE + (e + 1) * P], ident,
                               start=h == 0, stop=h == PH - 1)
                    if e % 4 == 3:
                        v.then_inc(w_turned, 1)
                for e in range(NE // P):
                    if e % 4 == 0:
                        pe.wait_ge(w_t_ready, i * 2 + e // 4 + 1)
                    v = mm(pc[2][:, 0:D], big2[:, e * P:(e + 1) * P], ue[:, e, :], start=False, stop=e == NE // P - 1)
                v.then_inc(ffn_made, 1)
                turn_rows(i, 2)
                for c in range(DC):
                    for k in range(DC):
                        v = mm(pc[1][:, c * P:(c + 1) * P], w_feat[:, k, c * P:(c + 1) * P], xn_t[:, k, :], start=k == 0, stop=k == 1)
                v.then_inc(feat_made, 1)

            for b in range(B):
                with pe.Fori(b * NTB, (b + 1) * NTB) as i:
                    front_attention(i, b)
                    front_ffn(i)

            def tanh_round(b, it):
                n0 = (it + b * IT) * len(ORDER)
                pe.wait_ge(rho_ready, it + b * IT + 1)
                for k, (r, c, j) in enumerate(ORDER):
                    pe.wait_ge(h_ready, n0 + k + 1)
                    last = c == DC - 1 and (r == TR - 1 or 4 * (r + 1) + j >= TI)
                    for h in range(2):
                        v = mm(pr[32 * j:32 * j + 32, h, :], window[:, c, 31 - r:63 - r], ring[:, k % 4, h * 512:(h + 1) * 512],
                               start=r == 0 and c == 0, stop=last)
                    v.then_inc(h_used, 1)

            def experts(b):
                done = b * MOE_TILES
                owner_i = owner[0:1, b * MOE_TILES:(b + 1) * MOE_TILES].bitcast(I32)

                def turn_rows(m):
                    pe.wait_ge(row_landed[0], (m + done + 1) * 16)
                    for c in range(DC):
                        v = nc.tensor.transpose(pc[0][:, c * P:(c + 1) * P], row_in[:, c * P:(c + 1) * P], ident)
                    v.then_inc(row_turned, 1)

                def up(m, e):
                    pe.wait_ge(row_t_ready, m + done + 1)
                    pe.wait_ge(bias_landed[0], (m + done + 1) * 16)
                    for n in range(2):
                        for k in range(DC):
                            mm(pa[:, n, :], row_t[:, k * P:(k + 1) * P], w1[:, bass.ds((e * DC + k) * FF + n * 512, 512)], start=k == 0, stop=False)
                        v = mm(pa[:, n, :], ones3[0:3, :], bias_rows[0:3, n * 512:(n + 1) * 512], start=False, stop=True)
                    v.then_inc(hid_made, 1)

                def turn_hid(m):
                    pe.wait_ge(hid_ready, m + done + 1)
                    for f in range(FC):
                        v = nc.tensor.transpose(pc[1 + f // 4][:, (f % 4) * P:(f % 4 + 1) * P], hid[b][:, f * P:(f + 1) * P], ident)
                        if f % 4 == 3:
                            v.then_inc(hid_turned, 1)

                def down(m, e):
                    for f in range(FC):
                        if f % 4 == 0:
                            pe.wait_ge(hid_t_ready, (m + done) * 2 + f // 4 + 1)
                        mm(pa[:, 2, 0:D], hid_t[b][:, f * P:(f + 1) * P], w2[:, bass.ds((e * FC + f) * D, D)], start=f == 0, stop=False)
                    mm(pa[:, 2, 0:D], ones3[0:3, :], bias_rows[0:3, FF:FF + D], start=False, stop=True).then_inc(y_made, 1)

                pe.wait_ge(slots_ready, b + 1)
                pe.wait_ge(experts_in, 32 * E)
                with pe.Fori(0, MOE_TILES) as m:
                    e = pe.value_load(owner_i[:, bass.ds(m, 1)], min_val=0, max_val=E - 1)
                    turn_rows(m)
                    up(m, e)
                    turn_hid(m)
                    down(m, e)

            for b in range(B):
                with pe.Fori(0, IT) as it:
                    tanh_round(b, it)
                pe.wait_ge(rho_in, 16 * (b + 1))
                half = RI * IT // 2
                for n in range(NTB):
                    for k in range(2):
                        at = (n % 3) * 2 * half + k * half
                        v = nc.tensor.transpose(pa[:, n // 3, at:at + half], rho_back[b][0:half, k, n * P:(n + 1) * P], ident[0:half, 0:half])
                v.then_inc(rho_turned, 1)
                with pe.Fori(b * NTB, (b + 1) * NTB) as i:
                    pe.wait_ge(xn4_ready, i + 1)
                    for c in range(DC):
                        v = nc.tensor.transpose(pc[0][:, c * P:(c + 1) * P], xn4[:, c * P:(c + 1) * P], ident)
                    v.then_inc(xn4_turned, 1)
                    pe.wait_ge(xn4_t_ready, i + 1)
                    for k in range(DC):
                        v = mm(pc[1][:, 0:E], xn4_t[:, k, :], w_router[:, k, :], start=k == 0, stop=k == 1)
                    v.then_inc(router_made, 1)
                pe.wait_ge(pick_ready, b + 1)
                T = NTB * E
                mm(pc[0][:, 0:T], before, route[:, 6 * T:7 * T], start=True, stop=True)
                mm(pc[0][:, T:2 * T], ones, route[:, 6 * T:7 * T], start=True, stop=True).then_inc(ranks_made, 1)
                experts(b)


def kernel(**inputs):
    import concourse.bacc as bacc
    from concourse.bass_utils import run_bass_kernel_spmd

    a = {k: np.asarray(v) for k, v in inputs.items()}

    def chunks(w):
        return np.ascontiguousarray(w.reshape(-1, P, w.shape[-1]).transpose(1, 0, 2))

    keys = a["L0_ffn_keys"]
    key_blocks = np.zeros((P, 4, P), keys.dtype)
    for e in range(4):
        for j in range(2):
            key_blocks[64 * j:64 * j + 64, e, 64 * j:64 * j + 64] = keys[2 * (e % 2) + j, :, e // 2, :].T
    lay = {
        "x": a["x"].reshape(B * S, D),
        "mask": a["mask_BxSxS2_fk1"].reshape(B * S, M),
        "ctx_t": chunks(a["ctx_1024"].reshape(B * M, D).T),
        "gates": np.concatenate([a["g_xattn"], a["g_ffn"]]).reshape(4),
        "wq_t": chunks(a["L0_xattn_Wq"].T), "wk_t": chunks(a["L0_xattn_Wk"].T),
        "wv_t": chunks(a["L0_xattn_Wv"].T), "wo_t": chunks(a["L0_xattn_Wo"].T),
        "bq": a["L0_xattn_bq"].reshape(DC, P).T, "bk": a["L0_xattn_bk"].reshape(DC, P).T,
        "bv": a["L0_xattn_bv"], "bo": a["L0_xattn_bo"],
        "w_up_t": chunks(a["L0_ffn_W_up"].T), "w_down_t": chunks(a["L0_ffn_W_down"].T),
        "w_pq_t": chunks(a["L0_ffn_W_q"].T), "keys": key_blocks,
        "de_t": chunks(a["L0_ffn_down_embed"].T), "ue": chunks(a["L0_ffn_up_embed"]),
        "w_feat": chunks(a["L1_xattn_W"]), "w_txt": chunks(a["L1_xattn_Ws"]),
        "b_txt": a["L1_xattn_b"].reshape(DC, P).T,
        "w_rho": a["L1_xattn_w"].reshape(DC, P).T,
        "gate_w": np.stack([a["L1_xattn_Wcw"][0], a["L1_xattn_Wcb"][0]]).reshape(2, DC, P).transpose(2, 0, 1),
        "gate_bias": np.concatenate([a["L1_xattn_bcw"], a["L1_xattn_bcb"]]),
        "q_mask": a["mask_BxS2_ik0"].reshape(B * M),
        "w_router": chunks(a["L1_ffn_router_w"].T),
        "expert_bias": np.concatenate([a["L1_ffn_b1"], a["L1_ffn_b2"]], axis=1).reshape(P, 80),
        "w1": a["L1_ffn_w1"].reshape(E, FF, DC, P).transpose(3, 0, 2, 1).reshape(P, E * DC * FF),
        "w2": a["L1_ffn_w2"].reshape(E, D, FC, P).transpose(3, 0, 2, 1).reshape(P, E * FC * D),
        "before": (np.arange(P)[:, None] < np.arange(P)[None, :]).astype(np.float32),
        "ident": np.eye(P, dtype=np.float32),
        "headmask": (np.arange(P)[:, None] // HD == np.arange(HG)[None, :]).astype(np.float32),
    }
    nc = bacc.Bacc("TRN2", target_bir_lowering=False, num_devices=1)
    arrays, t = {}, {}
    for name, v in lay.items():
        v = np.ascontiguousarray(v)
        arrays["in_" + name] = v
        t[name] = nc.dram_tensor("in_" + name, v.shape, mybir.dt.from_np(v.dtype), kind="ExternalInput").ap()
    out = nc.dram_tensor("out_0", (B * S, D), F32, kind="ExternalOutput").ap()
    build(nc, t, out)
    r = run_bass_kernel_spmd(nc, [arrays], core_ids=[0])
    return np.asarray(r.results[0]["out_0"]).reshape(B, S, D)
```

```python
from contextlib import ExitStack

import numpy as np

import concourse.bass as bass
from concourse import mybir

ALU = mybir.AluOpType
ACT = mybir.ActivationFunctionType
F32 = mybir.dt.float32
BF16 = mybir.dt.bfloat16
I32 = mybir.dt.int32
U32 = mybir.dt.uint32
AX = mybir.AxisListType

P = 128
B, S, D = 2, 1024, 256
M = 154
NT = B * S // P
NTB = S // P
DC = D // P
H, HD = 16, 16
HG = P // HD
MT = M - P
TQ = 4
FF = 1024
FC = FF // P
PH, NK, TOPK = 4, 64, 8
NE = 1024
NX = NE // NK
MASKED = -(2.0 ** 100)
FAR = 3.0e38
EPS = 1e-5
IT, TI = 7, 22
TR = 6
RI = 4 * TR
E = 8
MOE_TILES = 2 * B * S // P + E - 1
VW = 32
NEG = -1e30


def build(nc, t, out):
    ctx = ExitStack()
    with ctx:
        WORDS = 53200
        arena = ctx.enter_context(nc.sbuf_tensor("arena", [P, WORDS], F32))
        top = [0]

        def words(n, at=None):
            o = top[0] if at is None else at
            if at is None:
                top[0] += n
            assert o + n <= WORDS, (o, n)
            return arena[:, o:o + n]

        def sem(name):
            return ctx.enter_context(nc.semaphore(name))

        x = words(NT * D).rearrange("p (i d) -> p i d", i=NT)
        feat0 = top[0]
        feat_t = words(B * DC * S).rearrange("p (b c n) -> p b c n", b=B, c=DC)
        ring0 = top[0]
        ring = words(4 * S).rearrange("p (k n) -> p k n", k=4)
        mean3 = words(NT)
        rstd3 = words(NT)
        gate = words(8)
        ident = words(P)
        ident_bf = words(P // 2).bitcast(BF16)
        headmask = words(HG)
        iota16 = words(NX)
        neg_half = words(NTB)
        window = words(DC * 63).rearrange("p (c n) -> p c n", c=DC)
        w_rho = words(DC)
        q_bias = words(B * IT * RI).rearrange("p (b n) -> p b n", b=B)
        gate_rows = words(2 * B * IT * RI).rearrange("p (k b n) -> p k b n", k=2, b=B)
        gate_bias = words(2)
        w_router = words(DC * E).rearrange("p (c n) -> p c n", c=DC)
        before = words(P)
        ones = words(P)
        steps128 = words(NT)
        tile_no = words(MOE_TILES)
        ones3 = words(P // 2).bitcast(BF16)
        txt_bias = words(DC * B * M).rearrange("p (c m) -> p c m", c=DC)
        rho_rows = words(S)
        gates3 = words(NTB * 2)
        dots = words(NT * 4)
        logits = words(NT * E)
        picks = words(2 * NT)
        slots = words(2 * NT)
        owner = words(MOE_TILES)
        bn8 = words(NTB * 6)
        stat8 = words(NTB * 2)
        var8 = words(NTB)
        rstd8 = words(NTB)
        carrier = words(1)
        front0 = top[0]
        wq = words(DC * D).rearrange("p (c n) -> p c n", c=DC)
        wo = words(DC * D).rearrange("p (c n) -> p c n", c=DC)
        w_feat = words(DC * D).rearrange("p (c n) -> p c n", c=DC)
        w_up = words(DC * FF).rearrange("p (c n) -> p c n", c=DC)
        w_down = words(FC * D).rearrange("p (c n) -> p c n", c=FC)
        w_pq = words(DC * 2 * D).rearrange("p (c n) -> p c n", c=DC)
        keys = words(4 * P).rearrange("p (c n) -> p c n", c=4)
        de = words(DC * NE).rearrange("p (c n) -> p c n", c=DC)
        ue = words(NE // P * D).rearrange("p (c n) -> p c n", c=NE // P)
        bq = words(DC)
        bk = words(DC)
        b_txt = words(DC)
        bo = words(D)
        mask_bias = words(NT * M // 2).bitcast(BF16)
        k_blocks = words(B * H * M)
        v_main = words(B * H * VW).rearrange("p (b h e) -> p b h e", b=B, h=H)
        v_rest = words(B * H * VW).rearrange("p (b h e) -> p b h e", b=B, h=H)
        a_xn = words(D)
        a_xn_t = words(D).rearrange("p (c n) -> p c n", c=DC)
        a_bn = words(6)
        a_stat = words(2)
        a_var = words(1)
        a_rstd = words(1)
        q_t = words(D).rearrange("p (c n) -> p c n", c=DC)
        row_max = words(HG)
        rest_max = words(HG)
        r_den = words(H)
        prob = words(H * M).rearrange("p (g n) -> p g n", g=DC)
        prob_t = words(3 * 512).rearrange("p (k n) -> p k n", k=3)
        o_t = words(512).rearrange("p (q n) -> p q n", q=H // TQ)
        att = words(D)
        att_t = a_xn_t
        proj = a_xn
        f_xn = words(D)
        f_xn_t = words(D).rearrange("p (c n) -> p c n", c=DC)
        f_bn = words(6)
        f_stat = words(2)
        f_var = words(1)
        f_rstd = words(1)
        scores = words(8 * NK)
        top_xy = words(64)
        idx = words(32)
        idx_f = words(32)
        far_off = words(32)
        grid = words(256)
        grid_rep = words(256)
        grid_sel = words(256)
        grid_b = words(256)
        top_s = words(32)
        t8 = words(32)
        t16 = words(64)
        cmp16 = words(512)
        pq_t = cmp16
        e_in = words(4 * 104).rearrange("p (h n) -> p h n", h=PH)
        den4 = words(PH)
        last_sum = words(1)
        big1 = words(PH * NE)
        big2 = words(PH * NE)
        up_act = big2[:, 0:FF]
        up_t = big2[:, FF:2 * FF]
        print("arena words", top[0])
        w1 = words(E * DC * FF, front0)
        w2 = words(E * FC * D, front0 + E * DC * FF)
        late0 = front0 + E * DC * FF + E * FC * D
        rho_t = words(NTB * IT * RI, late0).rearrange("p (i n) -> p i n", i=NTB)
        rho_w = words(NTB // 2 * IT * RI, late0 + NTB * IT * RI).rearrange("p (i n) -> p i n", i=NTB // 2)
        rows_t = words(NTB * D, late0).rearrange("p (i n) -> p i n", i=NTB)
        route = words(12 * NT * E, late0)
        own_w = words(400, late0 + 12 * NT * E)
        row_in = words(D, late0)
        row_t = words(D, late0 + D)
        row_out = words(D, late0 + 2 * D)
        bias_up = words(FF // 2, late0 + 3 * D).bitcast(BF16)
        bias_y = words(D // 2, late0 + 5 * D).bitcast(BF16)
        rho_back = [words(2 * S, feat0 + b * DC * S).rearrange("p (k n) -> p k n", k=2) for b in range(B)]
        rows4 = [words(NTB * D, feat0 + b * DC * S).rearrange("p (i d) -> p i d", i=NTB) for b in range(B)]
        hid = words(FF, ring0)
        hid_t = words(FF, ring0 + FF)
        back = words(2 * NT * D, feat0).rearrange("p (i k d) -> p i k d", k=2, d=D)
        zero_rows = rho_rows[:, 0:D]
        assert NT * M + DC * B * M <= PH * NE
        mask = big2[:, 0:NT * M]
        ctx_t = big2[:, NT * M:NT * M + DC * B * M].rearrange("p (c m) -> p c m", c=DC)
        wk = ring[:, 0, 0:512].rearrange("p (c n) -> p c n", c=DC)
        wv = ring[:, 0, 512:1024].rearrange("p (c n) -> p c n", c=DC)
        w_txt = ring[:, 1, 0:512].rearrange("p (c n) -> p c n", c=DC)
        bv = ring[:, 1, 512:768]
        k_t = ring[:, 2, 0:DC * B * M].rearrange("p (c m) -> p c m", c=DC)
        gate_w = ring[:, 2, 700:704].rearrange("p (k c) -> p k c", k=2)
        q_mask = ring[:, 2, 704:704 + B * M].bitcast(I32)
        bias_all = ring[:, 1, 768:848]
        bias_left = ring[:, 1, 848:928]
        bias_part = [a.bitcast(BF16) for a in (ring[:, 1, 928:968], ring[:, 1, 968:1008], ring[:, 2, 616:656])]
        v_short = ring[:, 3, :].rearrange("p (b h e) -> p b h e", b=B, h=H)

        rho_d = nc.dram_tensor("rho_d", (B, IT * RI, S), F32, kind="Internal").ap()
        rows_d = nc.dram_tensor("rows_d", (MOE_TILES * P, D), F32, kind="Internal").ap()
        outs_d = nc.dram_tensor("outs_d", (MOE_TILES * P, D), F32, kind="Internal").ap()
        bias_d = nc.dram_tensor("bias_d", (3, E, FF + D), BF16, kind="Internal").ap()

        pa = ctx.enter_context(nc.psum_tensor("pa", [P, 3, 512], F32))
        pf = ctx.enter_context(nc.psum_tensor("pf", [P, 3, 512], F32))
        pr = ctx.enter_context(nc.psum_tensor("pr", [P, 2, 512], F32))
        pa_flat = pa[:, :, :].rearrange("p k n -> p (k n)")
        pf_flat = pf[:, :, :].rearrange("p k n -> p (k n)")

        consts_in = sem("consts_in")
        weights_in = sem("weights_in")
        rows_in = sem("rows_in")
        gates_on = sem("gates_on")
        v_rest_in = sem("v_rest_in")
        setup_mm = sem("setup_mm")
        setup_step = sem("setup_step")
        setup_done = sem("setup_done")
        setup_read = sem("setup_read")
        ones_set = sem("ones_set")
        bias_split = sem("bias_split")
        bias_out = sem("bias_out")
        zeroed = sem("zeroed")
        a_var_ready = sem("a_var_ready")
        a_rstd_ready = sem("a_rstd_ready")
        a_xn_ready = sem("a_xn_ready")
        a_turned = sem("a_turned")
        a_xn_t_ready = sem("a_xn_t_ready")
        q_made = sem("q_made")
        q_ready = sem("q_ready")
        scores_made = sem("scores_made")
        shifted = sem("shifted")
        exp_done = sem("exp_done")
        prob_turned = sem("prob_turned")
        prob_t_ready = sem("prob_t_ready")
        pv_done = sem("pv_done")
        o_ready = sem("o_ready")
        o_turned = sem("o_turned")
        att_ready = sem("att_ready")
        att_turned = sem("att_turned")
        att_t_ready = sem("att_t_ready")
        wo_made = sem("wo_made")
        a_step = sem("a_step")
        f_var_ready = sem("f_var_ready")
        f_rstd_ready = sem("f_rstd_ready")
        f_xn_ready = sem("f_xn_ready")
        f_turned = sem("f_turned")
        f_xn_t_ready = sem("f_xn_t_ready")
        up_made = sem("up_made")
        up_tanh = sem("up_tanh")
        up_ready = sem("up_ready")
        pq_made = sem("pq_made")
        pq_ready = sem("pq_ready")
        sims_made = sem("sims_made")
        sims_read = sem("sims_read")
        e_in_ready = sem("e_in_ready")
        e_done = sem("e_done")
        g_made = sem("g_made")
        down_made = sem("down_made")
        u_ready = sem("u_ready")
        u_tanh = sem("u_tanh")
        w_ready = sem("w_ready")
        w_turned = sem("w_turned")
        w_t_ready = sem("w_t_ready")
        ffn_made = sem("ffn_made")
        feat_made = sem("feat_made")
        f_step = sem("f_step")
        feat_done = sem("feat_done")
        h_ready = sem("h_ready")
        h_used = sem("h_used")
        rho_ready = sem("rho_ready")
        rho_out = sem("rho_out")
        rho_in = sem("rho_in")
        rho_turned = sem("rho_turned")
        att1_in = sem("att1_in")
        att1_exp = sem("att1_exp")
        gates_in = sem("gates_in")
        gates_tanh = sem("gates_tanh")
        late_step = sem("late_step")
        var8_ready = sem("var8_ready")
        rstd8_ready = sem("rstd8_ready")
        rows4_ready = sem("rows4_ready")
        rows4_turned = sem("rows4_turned")
        rows4_t_ready = sem("rows4_t_ready")
        router_made = sem("router_made")
        experts_in = sem("experts_in")
        picks_in = sem("picks_in")
        picks_exp = sem("picks_exp")
        pick_ready = sem("pick_ready")
        ranks_made = sem("ranks_made")
        slots_ready = sem("slots_ready")
        scattered = sem("scattered")
        row_landed = sem("row_landed")
        bias_up_in = sem("bias_up_in")
        bias_y_in = sem("bias_y_in")
        row_turned = sem("row_turned")
        row_t_ready = sem("row_t_ready")
        hid_made = sem("hid_made")
        hid_ready = sem("hid_ready")
        hid_turned = sem("hid_turned")
        hid_t_ready = sem("hid_t_ready")
        y_made = sem("y_made")
        y_ready = sem("y_ready")
        y_stored = sem("y_stored")
        gathered = [sem(f"gathered_{g}") for g in range(NT // 4)]
        folded = sem("folded")
        stored = sem("stored")

        CONSTS = 19
        A_STEPS = 9
        F_STEPS = 24
        ORDER = [(r, c, j) for r in range(TR) for c in range(DC) for j in range(4) if 4 * r + j < TI]
        ROUND = len(ORDER)
        HALF = RI * IT // 2
        R = IT * RI
        T = NT * E

        block = ctx.enter_context(nc.Block())

        @block.sync
        def _(sp):
            small = [(ident, t["ident"]), (ctx_t, t["ctx_t"]), (wk, t["wk_t"]), (wv, t["wv_t"]), (w_txt, t["w_txt"]),
                     (headmask, t["headmask"]), (bk, t["bk"]), (bq, t["bq"]), (b_txt, t["b_txt"]),
                     (w_rho, t["w_rho"]), (w_router, t["w_router"]), (before, t["before"]), (gate_w, t["gate_w"]),
                     (gate_bias, t["gate_bias"].partition_broadcast(P)), (q_mask, t["q_mask"].partition_broadcast(P)),
                     (bias_all, t["expert_bias"]),
                     (bv, t["bv"].partition_broadcast(P)), (bo, t["bo"].partition_broadcast(P)),
                     (gate[:, 0:4], t["gates"].partition_broadcast(P))]
            assert len(small) == CONSTS
            for dst, src in small:
                sp.dma_start(dst, src).then_inc(consts_in, 16)
            for b in range(B):
                n = slice(b * NTB, (b + 1) * NTB)
                sp.dma_start(mask.rearrange("p (i m) -> p i m", i=NT)[:, n, :],
                             t["mask"].rearrange("(i p) m -> p i m", p=P)[:, n, :]).then_inc(rows_in, 16)
                sp.dma_start(x[:, n, :], t["x"].rearrange("(i p) d -> p i d", p=P)[:, n, :]).then_inc(rows_in, 16)
            for dst, src in [(wq, t["wq_t"]), (wo, t["wo_t"]), (w_pq, t["w_pq_t"]), (w_up, t["w_up_t"]), (keys, t["keys"]),
                             (de, t["de_t"]), (w_down, t["w_down_t"]), (ue, t["ue"]), (w_feat, t["w_feat"])]:
                sp.dma_start(dst, src).then_inc(weights_in, 16)
            sp.wait_ge(ones_set, 3)
            for b in range(B):
                for j in range(TQ):
                    dst = v_rest[MT * j:MT * j + MT, b, :, :].rearrange("p (q j) e -> p q j e", j=TQ)[:, :, j, :]
                    src = v_short[0:MT, b, :, :].rearrange("p (q j) e -> p q j e", j=TQ)[:, :, j, :]
                    sp.dma_start(dst, src).then_inc(v_rest_in, 16)
            sp.wait_ge(bias_split, 1)
            for k in range(3):
                sp.dma_start(bias_d[k].rearrange("e (q n) -> (e q) n", n=80), bias_part[k]).then_inc(bias_out, 16)
            sp.dma_start(rows_d.rearrange("(i p) d -> p i d", p=P),
                         zero_rows.unsqueeze(1).broadcast_to([P, MOE_TILES, D])).then_inc(zeroed, 16)

            def rho_round(b, it):
                sp.wait_ge(rho_ready, it + b * IT + 2)
                for j in range(4):
                    sp.dma_start(rho_d[b, bass.ds(it * RI + j * TR, TR), :], rho_rows[32 * j:32 * j + TR, :]).then_inc(rho_out, 16)

            def rho_load(b):
                sp.wait_ge(rho_out, 64 * IT * (b + 1) + 64)
                sp.dma_start(rho_back[b][0:HALF, :, :], rho_d[b].rearrange("(k p) n -> p k n", k=2)).then_inc(rho_in, 16)

            with sp.Fori(0, IT) as it:
                rho_round(0, it)
            rho_load(0)
            sp.wait_ge(feat_done, 2)
            for e in range(E):
                sp.dma_start(w1[:, e * DC * FF:(e + 1) * DC * FF], t["w1"][:, e * DC * FF:(e + 1) * DC * FF]).then_inc(experts_in, 16)
                sp.dma_start(w2[:, e * FC * D:(e + 1) * FC * D], t["w2"][:, e * FC * D:(e + 1) * FC * D]).then_inc(experts_in, 16)
            with sp.Fori(0, IT) as it:
                rho_round(1, it)
            rho_load(1)

            owner_i = owner[0:1, :].bitcast(I32)
            sp.wait_ge(bias_out, 48)
            sp.wait_ge(slots_ready, 1)
            sp.wait_ge(scattered, 16 * 2 * NT)

            def expert_of(m):
                at = owner_i[:, m:m + 1] if isinstance(m, int) else owner_i[:, bass.ds(m, 1)]
                return sp.value_load(at, min_val=0, max_val=E - 1)

            def load_rows(m):
                src = rows_d[m * P:m * P + P, :] if isinstance(m, int) else rows_d[bass.ds(m * P, P), :]
                sp.dma_start(row_in, src).then_inc(row_landed, 16)

            def load_bias_up(e):
                sp.dma_start(bias_up[0:3, :], bias_d[:, bass.ds(e, 1), 0:FF].rearrange("k e n -> k (e n)")).then_inc(bias_up_in, 16)

            def load_bias_y(e):
                sp.dma_start(bias_y[0:3, :], bias_d[:, bass.ds(e, 1), FF:FF + D].rearrange("k e n -> k (e n)")).then_inc(bias_y_in, 16)

            load_rows(0)
            load_bias_up(expert_of(0))
            load_bias_y(expert_of(0))
            sp.wait_ge(row_turned, 1)
            load_rows(1)
            sp.wait_ge(hid_made, 1)
            load_bias_up(expert_of(1))

            def expert_tile(m, ahead):
                if ahead >= 2:
                    sp.wait_ge(row_turned, m + 2)
                    load_rows(m + 2)
                    e2 = expert_of(m + 2)
                    sp.wait_ge(hid_made, m + 2)
                    load_bias_up(e2)
                sp.wait_ge(y_ready, m + 1)
                dst = outs_d[m * P:m * P + P, :] if isinstance(m, int) else outs_d[bass.ds(m * P, P), :]
                sp.dma_start(dst, row_out).then_inc(y_stored, 16)
                if ahead >= 1:
                    load_bias_y(expert_of(m + 1))

            with sp.Fori(0, MOE_TILES - 2) as m:
                expert_tile(m, 2)
            expert_tile(MOE_TILES - 2, 1)
            expert_tile(MOE_TILES - 1, 0)
            for n in range(0, NT, 4):
                sp.wait_ge(folded, 2 * (n + 4))
                sp.dma_start(out.rearrange("(i p) d -> p i d", p=P)[:, n:n + 4, :], x[:, n:n + 4, :]).then_inc(stored, 16)
            sp.wait_ge(stored, 16 * NT // 4)

        @block.gpsimd
        def _(pool):
            pool.memset(v_main[:, :, :, :], 0.0)
            pool.memset(v_short[:, :, :, :], 0.0)
            pool.memset(v_rest[:, :, :, :], 0.0)
            pool.memset(neg_half, -0.5)
            pool.memset(ones3, 1.0)
            pool.iota(steps128, [[P, NT]], base=0, channel_multiplier=0, allow_small_or_imprecise_dtypes=True)
            pool.iota(tile_no, [[1, MOE_TILES]], base=0, channel_multiplier=0, allow_small_or_imprecise_dtypes=True)
            pool.memset(zero_rows, 0.0)
            pool.iota(iota16, [[1, NX]], base=0, channel_multiplier=0,
                      allow_small_or_imprecise_dtypes=True).then_inc(ones_set, 1)

            def rstd_a(i):
                pool.wait_ge(a_var_ready, i + 1)
                nc.gpsimd.tensor_tensor(a_rstd, a_var, neg_half[:, 0:1], ALU.pow).then_inc(a_rstd_ready, 1)

            def rstd_f(i, k):
                pool.wait_ge(f_var_ready, i * 2 + k + 1)
                nc.gpsimd.tensor_tensor(f_rstd, f_var, neg_half[:, 0:1], ALU.pow).then_inc(f_rstd_ready, 1)

            def front(i, a_next=True):
                rstd_f(i, 0)
                if a_next:
                    rstd_a(i + 1)
                rstd_f(i, 1)

            rstd_a(0)
            with pool.Fori(0, NT - 1) as i:
                front(i)
            front(NT - 1, a_next=False)
            for b in range(B):
                pool.wait_ge(var8_ready, b + 1)
                nc.gpsimd.tensor_tensor(rstd8, var8, neg_half, ALU.pow).then_inc(rstd8_ready, 1)
            pool.wait_ge(slots_ready, 1)
            pool.wait_ge(zeroed, 16)
            for n in range(NT):
                for k in range(2):
                    at = k * NT + n
                    pool.indirect_dma_start(out=rows_d, out_offset=bass.IndirectOffsetOnAxis(ap=slots[:, at:at + 1].bitcast(U32), axis=0),
                                            in_=rows4[n // NTB][:, n % NTB, :], in_offset=None).then_inc(scattered, 16)
            pool.wait_ge(scattered, 16 * 2 * NT)
            pool.wait_ge(y_stored, 16 * MOE_TILES + 16)
            for n in range(NT):
                for k in range(2):
                    at = k * NT + n
                    pool.indirect_dma_start(out=back[:, n, k, :], out_offset=None, in_=outs_d,
                                            in_offset=bass.IndirectOffsetOnAxis(ap=slots[:, at:at + 1].bitcast(U32), axis=0)).then_inc(gathered[n // 4], 16)

        @block.scalar
        def _(act):
            act.wait_ge(consts_in, 16 * CONSTS)
            nc.scalar.activation(gate[:, 4:8], gate[:, 0:4], ACT.Tanh).then_inc(gates_on, 1)

            def att_exp(i, g):
                act.wait_ge(shifted, i * 2 + g + 1)
                p = prob[:, g, :]
                nc.scalar.activation(p, p, ACT.Exp, scale=0.25).then_inc(exp_done, 1)

            def ffn_up(i):
                act.wait_ge(up_made, i + 1)
                nc.scalar.activation(up_act, pf_flat[:, 0:FF], ACT.Tanh, scale=0.5).then_inc(up_tanh, 1)

            def ffn_exp(i):
                act.wait_ge(e_in_ready, i + 1)
                nc.scalar.activation(e_in[:, :, :], e_in[:, :, :], ACT.Exp).then_inc(e_done, 1)

            def ffn_last(i):
                act.wait_ge(u_ready, i * 3 + 1)
                nc.scalar.activation(grid_rep, grid_b, ACT.Tanh, scale=0.5).then_inc(u_tanh, 1)

            def ffn_u(i, g):
                act.wait_ge(u_ready, i * 3 + g + 2)
                if g == 0:
                    act.wait_ge(down_made, i + 1)
                h = slice(g * 2 * NE, (g + 1) * 2 * NE)
                nc.scalar.activation(big2[:, h], big1[:, h], ACT.Tanh, scale=0.5).then_inc(u_tanh, 1)

            def tanh_rows(b, it, k0, k1):
                for k in range(k0, k1):
                    r, c, j = ORDER[k]
                    act.wait_ge(h_used, (it + b * IT) * ROUND + k + 1)
                    tt = it * TI + (b * M + 4 * r + j)
                    col = txt_bias[:, c, tt:tt + 1] if isinstance(tt, int) else txt_bias[:, c, bass.ds(tt, 1)]
                    nc.scalar.activation(ring[:, k % 4, :], feat_t[:, b, c, :], ACT.Tanh, bias=col).then_inc(h_ready, 1)

            def front(i, a_next=True, tanh=None):
                rows = (lambda k0, k1: tanh_rows(*tanh, k0, k1)) if tanh else (lambda k0, k1: None)
                rows(0, 6)
                ffn_up(i)
                rows(6, 10)
                ffn_exp(i)
                rows(10, 22)
                ffn_last(i)
                rows(22, 24)
                ffn_u(i, 0)
                ffn_u(i, 1)
                rows(24, 28)
                if a_next:
                    att_exp(i + 1, 0)
                rows(28, 34)
                if a_next:
                    att_exp(i + 1, 1)
                rows(34, ROUND)

            att_exp(0, 0)
            att_exp(0, 1)
            with act.Fori(0, NTB - 1) as i:
                front(i)
            front(NTB - 1)
            act.wait_ge(bias_out, 48)
            act.wait_ge(v_rest_in, 16 * TQ * B)
            act.wait_ge(feat_done, 1)
            with act.Fori(0, IT) as it:
                front(it + NTB, tanh=(0, it))
            front(NT - 1, a_next=False)
            act.wait_ge(feat_done, 2)

            def attend_exp(b):
                act.wait_ge(att1_in, b + 1)
                nc.scalar.activation(rho_t[:, :, :], rho_t[:, :, :], ACT.Exp).then_inc(att1_exp, 1)

            def attend_gates(b):
                act.wait_ge(gates_in, b + 1)
                nc.scalar.activation(gates3, gates3, ACT.Tanh).then_inc(gates_tanh, 1)

            tanh_rows(1, 0, 0, 12)
            attend_exp(0)
            tanh_rows(1, 0, 12, 24)
            attend_gates(0)
            tanh_rows(1, 0, 24, ROUND)
            with act.Fori(1, IT) as it:
                tanh_rows(1, it, 0, ROUND)
            attend_exp(1)
            attend_gates(1)
            act.wait_ge(picks_in, 1)
            nc.scalar.activation(route[:, 0:T], route[:, 0:T], ACT.Exp).then_inc(picks_exp, 1)
            nc.scalar.preload_act_table(ACT.Gelu_apprx_tanh)
            with act.Fori(0, MOE_TILES) as m:
                act.wait_ge(hid_made, m + 1)
                nc.scalar.activation(hid, pa_flat[:, 0:FF], ACT.Gelu_apprx_tanh).then_inc(hid_ready, 1)

        @block.vector
        def _(dve):
            steps = [0]

            def link(ins):
                steps[0] += 1
                ins.then_inc(setup_step, 1)
                dve.wait_ge(setup_step, steps[0])

            dve.sem_inc(rho_ready, 1)
            dve.sem_inc(rho_out, 64)
            dve.sem_inc(y_stored, 16)
            dve.wait_ge(consts_in, 16 * CONSTS)
            nc.vector.tensor_copy(ident_bf, ident)
            dve.wait_ge(setup_mm, 1)
            for c in range(DC):
                v = nc.vector.tensor_scalar(txt_bias[:, c, :], pa[:, c, 0:B * M], b_txt[:, c:c + 1], None, ALU.add)
            link(v)
            dve.wait_ge(setup_mm, 2)
            for c in range(DC):
                v = nc.vector.tensor_scalar(k_t[:, c, :], pf[:, c, 0:B * M], bk[:, c:c + 1], None, ALU.add)
            link(v)
            kb = k_blocks.rearrange("p (b g n) -> p b g n", b=B, g=DC)
            for g in range(DC):
                for h in range(HG):
                    for dst, m0, m1 in ((h * P, 0, P), (HG * P + h * MT, P, M)):
                        v = nc.vector.tensor_scalar(kb[:, :, g, dst:dst + m1 - m0],
                                                    k_t[:, g, :].rearrange("p (b m) -> p b m", b=B)[:, :, m0:m1],
                                                    headmask[:, h:h + 1], None, ALU.mult)
            dve.wait_ge(setup_mm, 3)
            dve.wait_ge(ones_set, 1)
            bv_h = bv.rearrange("p (h e) -> p h e", h=H)
            for b in range(B):
                nc.vector.memset(v_main[:, b, :, HD:HD + 1], 1.0)
                nc.vector.memset(v_short[0:MT, b, :, HD:HD + 1], 1.0)
                nc.vector.tensor_tensor(v_main[:, b, :, 0:HD], pr[:, b, 0:D].rearrange("p (h e) -> p h e", h=H),
                                        bv_h, ALU.add)
                v = nc.vector.tensor_tensor(v_short[0:MT, b, :, 0:HD],
                                            pr[0:MT, b, D:2 * D].rearrange("p (h e) -> p h e", h=H),
                                            bv_h[0:MT], ALU.add)
                v.then_inc(ones_set, 1)
            dve.wait_ge(gates_on, 1)
            nc.vector.tensor_scalar(gate[:, 6:7], gate[:, 6:7], 0.5, None, ALU.mult).then_inc(setup_done, 1)
            dve.wait_ge(setup_done, 1)
            link(nc.vector.tensor_copy(bias_part[0], bias_all))
            link(nc.vector.tensor_tensor(bias_left, bias_all, bias_part[0], ALU.subtract))
            link(nc.vector.tensor_copy(bias_part[1], bias_left))
            link(nc.vector.tensor_tensor(bias_left, bias_left, bias_part[1], ALU.subtract))
            nc.vector.tensor_copy(bias_part[2], bias_left).then_inc(bias_split, 1)
            nc.vector.memset(window[:, :, :], 0.0)
            nc.vector.memset(q_bias[:, :, :], -FAR)
            nc.vector.memset(gate_rows[:, :, :, :], 0.0)
            link(nc.vector.memset(ones, 1.0))
            for c in range(DC):
                nc.vector.tensor_copy(window[:, c, 31:32], w_rho[:, c:c + 1])
            dve.wait_ge(setup_mm, 4)
            for r0, r1, nj in ((0, TR - 1, 4), (TR - 1, TR, 2)):
                for b in range(B):
                    for jj in range(nj):
                        for src, dst in ((q_mask[:, b * M:(b + 1) * M], q_bias[:, b, :]),
                                         (pr[:, 0, b * M:(b + 1) * M], gate_rows[:, 0, b, :]),
                                         (pr[:, 1, b * M:(b + 1) * M], gate_rows[:, 1, b, :])):
                            sv = src.rearrange("p (i t) -> p i t", i=IT)[:, :, 4 * r0 + jj:4 * (r1 - 1) + jj + 1:4]
                            dv = dst.rearrange("p (i j r) -> p i j r", i=IT, j=4)[:, :, jj, r0:r1]
                            if src.dtype == I32:
                                v = nc.vector.tensor_scalar(dv, sv, -NEG, NEG, ALU.mult, ALU.add)
                            else:
                                v = nc.vector.tensor_copy(dv, sv)
            link(v)
            dve.wait_ge(rows_in, 64)
            link(nc.vector.tensor_scalar(mask_bias, mask, 0.0, MASKED, ALU.is_equal, ALU.mult))
            nc.vector.memset(carrier, 0.0).then_inc(setup_read, 1)

            def att_link(i, n, ins, plain=False):
                ins.then_inc(a_step, 1)
                dve.wait_ge(a_step, i * A_STEPS + n)
                if plain:
                    nc.vector.memset(carrier, 0.0)

            def ffn_link(i, n, ins, plain=False):
                ins.then_inc(f_step, 1)
                dve.wait_ge(f_step, i * F_STEPS + n)
                if plain:
                    nc.vector.memset(carrier, 0.0)

            def row_of(i):
                return x[:, i, :] if isinstance(i, int) else x[:, bass.ds(i, 1), :].rearrange("p i d -> p (i d)")

            def att_norm(i):
                xi = row_of(i)
                att_link(i, 1, nc.vector.bn_stats(a_bn, xi), plain=True)
                att_link(i, 2, nc.vector.bn_aggr(a_stat, a_bn))
                nc.vector.tensor_scalar(a_var, a_stat[:, 1:2], EPS, None, ALU.add).then_inc(a_var_ready, 1)

            def att_xn(i):
                dve.wait_ge(a_rstd_ready, i + 1)
                nc.vector.tensor_scalar(a_xn, row_of(i), a_stat[:, 0:1], a_rstd, ALU.subtract, ALU.mult).then_inc(a_xn_ready, 1)

            def att_xn_t(i):
                dve.wait_ge(a_turned, i + 1)
                nc.vector.tensor_copy(a_xn_t[:, :, :].rearrange("p c n -> p (c n)"), pa[:, 0, 0:D]).then_inc(a_xn_t_ready, 1)

            def att_q(i):
                dve.wait_ge(q_made, i + 1)
                for c in range(DC):
                    v = nc.vector.tensor_scalar(q_t[:, c, :], pa[:, 1, c * P:(c + 1) * P], bq[:, c:c + 1], None, ALU.add)
                v.then_inc(q_ready, 1)

            def att_shift(i, g):
                dve.wait_ge(scores_made, i * 2 + g + 1)
                first = pa_flat[:, 0:HG * P].rearrange("p (h m) -> p h m", h=HG)
                rest = pa_flat[:, HG * P:HG * M].rearrange("p (h m) -> p h m", h=HG)
                nc.vector.tensor_reduce(row_max, first, AX.X, ALU.max)
                att_link(i, 2 * g + 3, nc.vector.tensor_reduce(rest_max, rest, AX.X, ALU.max))
                att_link(i, 2 * g + 4, nc.vector.tensor_tensor(row_max, row_max, rest_max, ALU.max))
                mx = row_max.unsqueeze(2)
                nc.vector.tensor_tensor(prob[:, g, 0:HG * P].rearrange("p (h m) -> p h m", h=HG), first,
                                        mx.broadcast_to([P, HG, P]), ALU.subtract)
                nc.vector.tensor_tensor(prob[:, g, HG * P:HG * M].rearrange("p (h m) -> p h m", h=HG), rest,
                                        mx.broadcast_to([P, HG, MT]), ALU.subtract).then_inc(shifted, 1)

            def att_prob_t(i, k):
                dve.wait_ge(prob_turned, i * 5 + k + 1)
                rows = TQ * MT if k == 0 else P
                if k >= 3:
                    dve.wait_ge(pv_done, i * 4 + k - 2)
                slot = 0 if k == 0 else 1 + k % 2
                nc.vector.tensor_copy(prob_t[0:rows, slot, :], pa[0:rows, k % 2, :]).then_inc(prob_t_ready, 1)

            def att_o(i):
                dve.wait_ge(pv_done, i * 4 + 4)
                nc.vector.tensor_copy(o_t[:, :, :].rearrange("p q n -> p (q n)"), pa[:, 2, :]).then_inc(o_ready, 1)

            def att_scale(i):
                dve.wait_ge(o_turned, i + 1)
                o = pa[:, 0, :].rearrange("p (h e) -> p h e", h=H)
                att_link(i, 7, nc.vector.reciprocal(r_den.unsqueeze(2), o[:, :, HD:HD + 1]))
                nc.vector.tensor_tensor(att.rearrange("p (h e) -> p h e", h=H), o[:, :, 0:HD],
                                        r_den.unsqueeze(2).broadcast_to([P, H, HD]), ALU.mult).then_inc(att_ready, 1)

            def att_att_t(i):
                dve.wait_ge(att_turned, i + 1)
                nc.vector.tensor_copy(att_t[:, :, :].rearrange("p c n -> p (c n)"), pa[:, 1, 0:D]).then_inc(att_t_ready, 1)

            def att_add(i):
                xi = row_of(i)
                dve.wait_ge(wo_made, i + 1)
                att_link(i, 8, nc.vector.tensor_tensor(proj, pa[:, 2, 0:D], bo, ALU.add))
                att_link(i, 9, nc.vector.scalar_tensor_tensor(xi, proj, gate[:, 4:5], xi, ALU.mult, ALU.add), plain=True)

            tx = top_xy[:, 0:32].rearrange("p (h k) -> p h k", h=PH)
            ty = top_xy[:, 32:64].rearrange("p (h k) -> p h k", h=PH)
            sc = scores.rearrange("p (r k) -> p r k", k=NK)
            gb4 = grid_b.rearrange("p (h i j) -> p h i j", h=PH, i=8)
            b4 = big1.rearrange("p (h x y) -> p h x y", h=PH, x=NX)
            t16_ = t16.rearrange("p (h x) -> p h x", h=PH)
            idx_u = idx.bitcast(U32)

            def ffn_norm(i, k):
                ffn_link(i, 1 + 22 * k, nc.vector.bn_stats(f_bn, row_of(i)), plain=True)
                ffn_link(i, 2 + 22 * k, nc.vector.bn_aggr(f_stat, f_bn))
                nc.vector.tensor_scalar(f_var, f_stat[:, 1:2], EPS, None, ALU.add).then_inc(f_var_ready, 1)

            def ffn_xn(i, k):
                dve.wait_ge(f_rstd_ready, i * 2 + k + 1)
                if k == 1:
                    at = slice(i, i + 1) if isinstance(i, int) else bass.ds(i, 1)
                    nc.vector.tensor_copy(mean3[:, at], f_stat[:, 0:1])
                    nc.vector.tensor_copy(rstd3[:, at], f_rstd)
                nc.vector.tensor_scalar(f_xn, row_of(i), f_stat[:, 0:1], f_rstd, ALU.subtract, ALU.mult).then_inc(f_xn_ready, 1)

            def ffn_xn_t(i, k):
                dve.wait_ge(f_turned, i * 2 + k + 1)
                nc.vector.tensor_copy(f_xn_t[:, :, :].rearrange("p c n -> p (c n)"), pf[:, 2 - 2 * k, 0:D]).then_inc(f_xn_t_ready, 1)

            def ffn_pq(i):
                dve.wait_ge(pq_made, i + 1)
                nc.vector.tensor_copy(pq_t, pf[:, 2, :]).then_inc(pq_ready, 1)

            def ffn_up(i):
                dve.wait_ge(up_tanh, i + 1)
                nc.vector.scalar_tensor_tensor(up_t, up_act, 1.0, pf_flat[:, 0:FF], ALU.add, ALU.mult).then_inc(up_ready, 1)

            def ffn_best(i):
                dve.wait_ge(sims_made, i + 1)
                nc.vector.tensor_copy(scores, pf[:, 2, :]).then_inc(sims_read, 1)
                dve.wait_ge(sims_read, i + 1)
                nc.vector.memset(carrier, 0.0)
                for r in range(2 * PH):
                    v = nc.vector.max(top_xy[:, 8 * r:8 * r + 8], scores[:, NK * r:NK * r + NK])
                ffn_link(i, 3, v, plain=True)
                for h in range(PH):
                    nc.vector.max_index(idx_u[:, 8 * h:8 * h + 8], top_xy[:, 8 * h:8 * h + 8], scores[:, NK * h:NK * h + NK])
                g4 = grid.rearrange("p (h i j) -> p h i j", h=PH, i=8)
                ffn_link(i, 4, nc.vector.tensor_tensor(g4, tx.unsqueeze(3).broadcast_to([P, PH, 8, 8]),
                                                       ty.unsqueeze(2).broadcast_to([P, PH, 8, 8]), ALU.add), plain=True)
                for h in range(PH):
                    v = nc.vector.max(top_s[:, 8 * h:8 * h + 8], grid[:, 64 * h:64 * h + 64])
                ffn_link(i, 5, v)
                ts = top_s.rearrange("p (h k) -> p h k", h=PH)
                for at, src, best in ((0, sc[:, 0:PH, 0:NX], tx), (16, sc[:, PH:2 * PH, :], ty), (80, ts, ts), (88, tx, tx), (96, ty, ty)):
                    w = src.shape[2]
                    v = nc.vector.tensor_tensor(e_in[:, :, at:at + w], src, best[:, :, 0:1].broadcast_to([P, PH, w]), ALU.subtract)
                v.then_inc(e_in_ready, 1)

            def ffn_limits(i):
                nc.vector.tensor_copy(idx_f, idx_u)
                for h in range(PH):
                    v = nc.vector.match_replace(grid_rep[:, 64 * h:64 * h + 64], top_s[:, 8 * h:8 * h + 8],
                                                grid[:, 64 * h:64 * h + 64], -FAR)
                ffn_link(i, 6, v)
                nc.vector.tensor_scalar(far_off, idx_f, float(NX), None, ALU.is_ge)
                ffn_link(i, 7, nc.vector.tensor_tensor(grid_sel, grid_rep, grid, ALU.not_equal))
                ffn_link(i, 8, nc.vector.tensor_scalar(grid_b, grid_sel, 0.0, FAR, ALU.is_equal, ALU.mult))
                ffn_link(i, 9, nc.vector.tensor_tensor(gb4, gb4, ty.unsqueeze(2).broadcast_to([P, PH, 8, 8]), ALU.add))
                t8_ = t8.rearrange("p (h i) -> p h i", h=PH)
                c4 = cmp16.rearrange("p (h x i) -> p h x i", h=PH, x=NX)
                nc.vector.tensor_reduce(t8_, gb4, AX.X, ALU.min)
                ffn_link(i, 10, nc.vector.tensor_tensor(c4, idx_f.rearrange("p (h i) -> p h i", h=PH).unsqueeze(2).broadcast_to([P, PH, NX, 8]),
                                                        iota16.unsqueeze(1).unsqueeze(3).broadcast_to([P, PH, NX, 8]), ALU.not_equal))
                ffn_link(i, 11, nc.vector.tensor_scalar(cmp16, cmp16, FAR, None, ALU.mult))
                ffn_link(i, 12, nc.vector.tensor_tensor(c4, c4, t8_.unsqueeze(2).broadcast_to([P, PH, NX, 8]), ALU.max))
                ffn_link(i, 13, nc.vector.tensor_reduce(t16_, c4, AX.X, ALU.min))

            def ffn_picked(i):
                ffn_link(i, 14, nc.vector.tensor_tensor(b4, sc[:, PH:2 * PH, :].unsqueeze(2).broadcast_to([P, PH, NX, NK]),
                                                        t16_.unsqueeze(3).broadcast_to([P, PH, NX, NK]), ALU.is_ge))
                dve.wait_ge(e_done, i + 1)
                nc.vector.tensor_tensor(b4, b4, e_in[:, :, 16:80].unsqueeze(2).broadcast_to([P, PH, NX, NK]), ALU.mult)
                ffn_link(i, 15, nc.vector.tensor_reduce(den4, e_in[:, :, 80:88], AX.X, ALU.add))
                ffn_link(i, 16, nc.vector.reciprocal(den4, den4))
                d4 = den4.unsqueeze(2)
                nc.vector.tensor_tensor(e_in[:, :, 0:16], e_in[:, :, 0:16], d4.broadcast_to([P, PH, 16]), ALU.mult)
                ffn_link(i, 17, nc.vector.tensor_tensor(e_in[:, :, 88:96], e_in[:, :, 88:96], d4.broadcast_to([P, PH, 8]), ALU.mult))
                nc.vector.tensor_tensor(b4, b4, e_in[:, :, 0:16].unsqueeze(3).broadcast_to([P, PH, NX, NK]), ALU.mult)
                ffn_link(i, 18, nc.vector.tensor_tensor(e_in[:, :, 88:96], e_in[:, :, 88:96], far_off.rearrange("p (h i) -> p h i", h=PH), ALU.mult))
                ffn_link(i, 19, nc.vector.tensor_tensor(gb4, grid_sel.rearrange("p (h i j) -> p h i j", h=PH, i=8),
                                                        e_in[:, :, 88:96].unsqueeze(3).broadcast_to([P, PH, 8, 8]), ALU.mult))
                ffn_link(i, 20, nc.vector.tensor_tensor(gb4, gb4, e_in[:, :, 96:104].unsqueeze(2).broadcast_to([P, PH, 8, 8]), ALU.mult))

            def ffn_weigh(i):
                dve.wait_ge(g_made, i + 1)
                nc.vector.tensor_scalar(grid_b, grid_b, pf_flat[:, NE - 1:NE], None, ALU.mult).then_inc(u_ready, 1)
                for g in range(2):
                    bh = big1[:, g * 2 * NE:(g + 1) * 2 * NE].rearrange("p (h e) -> p h e", h=2)
                    nc.vector.tensor_tensor(bh, bh, pf_flat[:, 0:NE].unsqueeze(1).broadcast_to([P, 2, NE]),
                                            ALU.mult).then_inc(u_ready, 1)

            def ffn_silu(i):
                dve.wait_ge(u_tanh, i * 3 + 1)
                nc.vector.scalar_tensor_tensor(grid, grid_rep, 1.0, grid_b, ALU.add, ALU.mult, accum_out=last_sum)
                for g in range(2):
                    dve.wait_ge(u_tanh, i * 3 + g + 2)
                    h = slice(g * 2 * NE, (g + 1) * 2 * NE)
                    v = nc.vector.scalar_tensor_tensor(big1[:, h], big2[:, h], 1.0, big1[:, h], ALU.add, ALU.mult)
                ffn_link(i, 21, v)
                nc.vector.tensor_scalar(big1[:, NE - 1:NE], big1[:, NE - 1:NE], last_sum, None, ALU.add).then_inc(w_ready, 1)

            def ffn_w_t(i, k):
                dve.wait_ge(w_turned, i * 2 + k + 1)
                nc.vector.tensor_copy(big2[:, 512 * k:512 * k + 512], pf[:, k, :]).then_inc(w_t_ready, 1)

            def ffn_add(i):
                xi = row_of(i)
                dve.wait_ge(ffn_made, i + 1)
                ffn_link(i, 22, nc.vector.scalar_tensor_tensor(xi, pf[:, 2, 0:D], gate[:, 6:7], xi, ALU.mult, ALU.add), plain=True)

            def ffn_feat(i, b, last=False):
                dve.wait_ge(feat_made, i + 1)
                m = i - b * NTB
                f = feat_t[:, b, :, m * P:m * P + P] if isinstance(m, int) else feat_t[:, b, :, bass.ds(m * P, P)]
                v = nc.vector.tensor_copy(f, pf[:, 1, 0:D].rearrange("p (c n) -> p c n", c=DC))
                if last:
                    v.then_inc(feat_done, 1)

            def rho_round(b, it):
                n = it + b * IT
                dve.wait_ge(h_used, (n + 1) * ROUND + 4)
                dve.wait_ge(rho_out, n * 64 + 64)
                nc.vector.tensor_copy(rho_rows, pr[:, :, :].rearrange("p k n -> p (k n)")).then_inc(rho_ready, 1)

            def attention(i):
                att_norm(i)
                att_xn(i)
                att_xn_t(i)
                att_q(i)
                att_shift(i, 0)
                att_shift(i, 1)
                for k in range(5):
                    att_prob_t(i, k)
                att_o(i)
                att_scale(i)
                att_att_t(i)
                att_add(i)

            def front(i, b, a_next=True, last=False):
                j = i + 1
                ffn_norm(i, 0)
                ffn_xn(i, 0)
                if a_next:
                    att_norm(j)
                ffn_xn_t(i, 0)
                if a_next:
                    att_xn(j)
                    att_xn_t(j)
                ffn_pq(i)
                if a_next:
                    att_q(j)
                ffn_best(i)
                ffn_limits(i)
                ffn_up(i)
                ffn_picked(i)
                ffn_weigh(i)
                if a_next:
                    att_shift(j, 0)
                ffn_silu(i)
                if a_next:
                    att_shift(j, 1)
                ffn_w_t(i, 0)
                if a_next:
                    att_prob_t(j, 0)
                ffn_w_t(i, 1)
                if a_next:
                    att_prob_t(j, 1)
                    att_prob_t(j, 2)
                ffn_add(i)
                ffn_norm(i, 1)
                if a_next:
                    att_prob_t(j, 3)
                ffn_xn(i, 1)
                if a_next:
                    att_prob_t(j, 4)
                ffn_xn_t(i, 1)
                if a_next:
                    att_o(j)
                ffn_feat(i, b, last)
                if a_next:
                    att_scale(j)
                    att_att_t(j)
                    att_add(j)

            attention(0)
            with dve.Fori(0, NTB - 1) as i:
                front(i, 0)
            front(NTB - 1, 0, last=True)
            dve.wait_ge(zeroed, 16)
            with dve.Fori(0, IT) as it:
                front(it + NTB, 1)
                rho_round(0, it)
            front(NT - 1, 1, a_next=False, last=True)

            late = [0]

            def late_link(ins):
                late[0] += 1
                ins.then_inc(late_step, 1)
                dve.wait_ge(late_step, late[0])

            def attend(b):
                def wide(a, w):
                    return a.unsqueeze(2).broadcast_to([P, NTB, w])

                dve.wait_ge(rho_turned, b + 1)
                for k in range(3):
                    i0, i1 = 3 * k, min(3 * k + 3, NTB)
                    v = nc.vector.tensor_tensor(rho_t[:, i0:i1, :], pa[:, k, 0:(i1 - i0) * R].rearrange("p (i n) -> p i n", n=R),
                                                q_bias[:, b, :].unsqueeze(1).broadcast_to([P, i1 - i0, R]), ALU.add)
                late_link(v)
                mx, den, dot = dots[:, 0:NTB], dots[:, NTB:2 * NTB], dots[:, 2 * NTB:4 * NTB].rearrange("p (k i) -> p k i", k=2)
                late_link(nc.vector.tensor_reduce(mx, rho_t, AX.X, ALU.max))
                nc.vector.tensor_tensor(rho_t, rho_t, wide(mx, R), ALU.subtract).then_inc(att1_in, 1)
                dve.wait_ge(att1_exp, b + 1)
                nc.vector.tensor_reduce(den, rho_t, AX.X, ALU.add)
                hn = NTB // 2
                for k in range(2):
                    for h in range(0, NTB, hn):
                        late_link(nc.vector.tensor_tensor(rho_w, rho_t[:, h:h + hn, :],
                                                          gate_rows[:, k, b, :].unsqueeze(1).broadcast_to([P, hn, R]), ALU.mult))
                        late_link(nc.vector.tensor_reduce(dot[:, k, h:h + hn], rho_w, AX.X, ALU.add))
                late_link(nc.vector.reciprocal(den, den))
                g3 = gates3.rearrange("p (k i) -> p k i", k=2)
                late_link(nc.vector.tensor_tensor(g3, dot, den.unsqueeze(1).broadcast_to([P, 2, NTB]), ALU.mult))
                nc.vector.tensor_tensor(g3, g3, gate_bias.unsqueeze(2).broadcast_to([P, 2, NTB]), ALU.add).then_inc(gates_in, 1)
                dve.wait_ge(gates_tanh, b + 1)
                late_link(nc.vector.tensor_scalar(gates3, gates3, gate[:, 5:6], None, ALU.mult))

            def post(b):
                xb = x[:, b * NTB:(b + 1) * NTB, :]
                for m in range(NTB):
                    i = b * NTB + m
                    v = nc.vector.tensor_scalar(rows4[b][:, m, :], x[:, i, :], mean3[:, i:i + 1], rstd3[:, i:i + 1], ALU.subtract, ALU.mult)
                late_link(v)
                for m in range(NTB):
                    v = nc.vector.tensor_scalar(rows4[b][:, m, :], rows4[b][:, m, :], gates3[:, m:m + 1], gates3[:, m + NTB:m + NTB + 1],
                                                ALU.mult, ALU.add)
                late_link(v)
                late_link(nc.vector.tensor_tensor(xb, xb, rows4[b], ALU.add))
                for m in range(NTB):
                    v = nc.vector.bn_stats(bn8[:, 6 * m:6 * m + 6], x[:, b * NTB + m, :])
                late_link(v)
                for m in range(NTB):
                    v = nc.vector.bn_aggr(stat8[:, 2 * m:2 * m + 2], bn8[:, 6 * m:6 * m + 6])
                late_link(v)
                s8 = stat8.rearrange("p (m k) -> p m k", k=2)
                nc.vector.tensor_scalar(var8.unsqueeze(2), s8[:, :, 1:2], EPS, None, ALU.add).then_inc(var8_ready, 1)
                dve.wait_ge(rstd8_ready, b + 1)
                for m in range(NTB):
                    nc.vector.tensor_scalar(rows4[b][:, m, :], x[:, b * NTB + m, :], stat8[:, 2 * m:2 * m + 1], rstd8[:, m:m + 1],
                                            ALU.subtract, ALU.mult).then_inc(rows4_ready, 1)
                for k in range(4):
                    dve.wait_ge(rows4_turned, b * 4 + k + 1)
                    nc.vector.tensor_copy(rows_t[:, 2 * k:2 * k + 2, :].rearrange("p i n -> p (i n)"),
                                          (pa if k % 2 else pf)[:, k // 2, :]).then_inc(rows4_t_ready, 1)
                dve.wait_ge(router_made, b + 1)
                late_link(nc.vector.tensor_copy(logits[:, b * NTB * E:(b + 1) * NTB * E], pa[:, 2, 0:NTB * E]))

            def routing():
                part = [route[:, k * T:(k + 1) * T] for k in range(12)]
                v3 = [a.rearrange("p (i e) -> p i e", i=NT) for a in part]
                best, ids, hot = part[1], part[2], [v3[3], v3[4]]
                for i in range(NT):
                    v = nc.vector.max(best[:, i * E:(i + 1) * E], logits[:, i * E:(i + 1) * E])
                late_link(v)
                for i in range(NT):
                    v = nc.vector.max_index(ids.bitcast(U32)[:, i * E:(i + 1) * E], best[:, i * E:(i + 1) * E], logits[:, i * E:(i + 1) * E])
                late_link(v)
                nc.vector.tensor_tensor(v3[0], v3[1], v3[1][:, :, 0:1].broadcast_to([P, NT, E]), ALU.subtract).then_inc(picks_in, 1)
                late_link(nc.vector.tensor_copy(part[5], ids.bitcast(U32)))
                for k in range(2):
                    v = nc.vector.tensor_tensor(hot[k], v3[5][:, :, k:k + 1].broadcast_to([P, NT, E]),
                                                iota16[:, 0:E].unsqueeze(1).broadcast_to([P, NT, E]), ALU.is_equal)
                late_link(v)
                nc.vector.tensor_tensor(part[6], part[3], part[4], ALU.add).then_inc(pick_ready, 1)
                dve.wait_ge(picks_exp, 1)
                d0, d1 = dots[:, 0:NT], dots[:, NT:2 * NT]
                late_link(nc.vector.tensor_reduce(d0, v3[0], AX.X, ALU.add))
                late_link(nc.vector.reciprocal(d0, d0))
                pk = picks.rearrange("p (k i) -> p i k", k=2)
                late_link(nc.vector.tensor_tensor(pk, v3[0][:, :, 0:2], d0.unsqueeze(2).broadcast_to([P, NT, 2]), ALU.mult))
                late_link(nc.vector.tensor_reduce(d1, pk, AX.X, ALU.add))
                late_link(nc.vector.tensor_scalar(d1, d1, 1e-8, None, ALU.add))
                late_link(nc.vector.reciprocal(d1, d1))
                late_link(nc.vector.tensor_tensor(pk, pk, d1.unsqueeze(2).broadcast_to([P, NT, 2]), ALU.mult))
                nc.vector.tensor_scalar(picks, picks, gate[:, 7:8], None, ALU.mult)
                dve.wait_ge(ranks_made, 1)
                rank, total, first = part[7], part[8], part[9]
                nc.vector.tensor_copy(rank, pf[:, 0, 0:T])
                nc.vector.tensor_copy(total, pf[:, 0, T:2 * T])
                late_link(nc.vector.memset(first, 0.0))
                for i in range(1, NT):
                    late_link(nc.vector.tensor_tensor(v3[9][:, i, :], v3[9][:, i - 1, :], v3[8][:, i - 1, :], ALU.add))
                cnt, tiles, start = part[0][:, 0:E], part[0][:, E:2 * E], part[0][:, 2 * E:3 * E]
                late_link(nc.vector.tensor_tensor(cnt, v3[9][:, NT - 1, :], v3[8][:, NT - 1, :], ALU.add))
                many = part[10].rearrange("p (e k) -> p e k", e=E)
                late_link(nc.vector.tensor_tensor(many, cnt.unsqueeze(2).broadcast_to([P, E, NT]),
                                                  steps128.unsqueeze(1).broadcast_to([P, E, NT]), ALU.is_gt))
                nc.vector.memset(start, 0.0)
                late_link(nc.vector.tensor_reduce(tiles, many, AX.X, ALU.add))
                for e in range(1, E):
                    late_link(nc.vector.tensor_tensor(start[:, e:e + 1], start[:, e - 1:e], tiles[:, e - 1:e], ALU.add))
                late_link(nc.vector.tensor_scalar(tiles, start, float(P), None, ALU.mult))
                late_link(nc.vector.tensor_tensor(rank, rank, first, ALU.add))
                late_link(nc.vector.tensor_tensor(v3[7], v3[7], tiles.unsqueeze(1).broadcast_to([P, NT, E]), ALU.add))
                for k in range(2):
                    late_link(nc.vector.tensor_tensor(v3[10], hot[k], v3[7], ALU.mult))
                    late_link(nc.vector.tensor_reduce(d0, v3[10], AX.X, ALU.add))
                    late_link(nc.vector.tensor_copy(slots[:, k * NT:(k + 1) * NT].bitcast(I32), d0))
                own = own_w[:, 0:MOE_TILES * E].rearrange("p (m e) -> p m e", e=E)
                late_link(nc.vector.tensor_tensor(own, tile_no.unsqueeze(2).broadcast_to([P, MOE_TILES, E]),
                                                  start.unsqueeze(1).broadcast_to([P, MOE_TILES, E]), ALU.is_ge))
                late_link(nc.vector.tensor_reduce(own_w[:, 320:320 + MOE_TILES], own, AX.X, ALU.add))
                nc.vector.tensor_scalar(owner.bitcast(I32), own_w[:, 320:320 + MOE_TILES],
                                        -1.0, None, ALU.add).then_inc(slots_ready, 1)

            attend(0)
            rho_round(1, 0)
            post(0)
            with dve.Fori(1, IT) as it:
                rho_round(1, it)
            attend(1)
            post(1)
            routing()

            def take_rows(m):
                dve.wait_ge(row_turned, m + 1)
                nc.vector.tensor_copy(row_t, pf[:, 0, 0:D]).then_inc(row_t_ready, 1)

            def take_hid(m):
                for k in range(2):
                    dve.wait_ge(hid_turned, m * 2 + k + 1)
                    nc.vector.tensor_copy(hid_t[:, 512 * k:512 * k + 512], pf[:, 1 + k, :]).then_inc(hid_t_ready, 1)

            def take_y(m):
                dve.wait_ge(y_made, m + 1)
                dve.wait_ge(y_stored, m * 16 + 16)
                nc.vector.tensor_copy(row_out, pa[:, 2, 0:D]).then_inc(y_ready, 1)

            take_rows(0)
            take_rows(1)
            with dve.Fori(0, MOE_TILES - 2) as m:
                take_hid(m)
                take_rows(m + 2)
                take_y(m)
            for m in (MOE_TILES - 2, MOE_TILES - 1):
                take_hid(m)
                take_y(m)

            for n in range(NT):
                if n % 4 == 0:
                    dve.wait_ge(gathered[n // 4], 16 * 8)
                for k in range(2):
                    at = k * NT + n
                    nc.vector.scalar_tensor_tensor(x[:, n, :], back[:, n, k, :], picks[:, at:at + 1], x[:, n, :],
                                                   ALU.mult, ALU.add).then_inc(folded, 1)
                    dve.wait_ge(folded, 2 * n + k + 1)

        @block.tensor
        def _(pe):
            mm = nc.tensor.matmul
            turn = nc.tensor.transpose
            pe.sem_inc(h_used, 4)
            pe.wait_ge(consts_in, 16 * CONSTS)
            for c in range(DC):
                for k in range(DC):
                    v = mm(pa[:, c, 0:B * M], w_txt[:, k, c * P:(c + 1) * P], ctx_t[:, k, :], start=k == 0, stop=k == 1)
            v.then_inc(setup_mm, 1)
            for c in range(DC):
                for k in range(DC):
                    v = mm(pf[:, c, 0:B * M], wk[:, k, c * P:(c + 1) * P], ctx_t[:, k, :], start=k == 0, stop=k == 1)
            v.then_inc(setup_mm, 1)
            for b in range(B):
                for at, m in ((0, P), (P, MT)):
                    for k in range(DC):
                        v = mm(pr[0:m, b, at * 2:at * 2 + D], ctx_t[:, k, b * M + at:b * M + at + m], wv[:, k, :],
                               start=k == 0, stop=k == 1)
            v.then_inc(setup_mm, 1)
            pe.wait_ge(setup_done, 1)
            for k in range(2):
                for c in range(DC):
                    v = mm(pr[:, k, 0:B * M], gate_w[:, k, c:c + 1].broadcast_to([P, P]), ctx_t[:, c, :], start=c == 0, stop=c == 1)
            v.then_inc(setup_mm, 1)
            pe.wait_ge(weights_in, 16 * 9)
            pe.wait_ge(v_rest_in, 16 * 8)
            pe.wait_ge(setup_read, 1)

            def att_turn(i):
                pe.wait_ge(a_xn_ready, i + 1)
                for c in range(DC):
                    v = turn(pa[:, 0, c * P:(c + 1) * P], a_xn[:, c * P:(c + 1) * P], ident)
                v.then_inc(a_turned, 1)

            def att_q(i):
                pe.wait_ge(a_xn_t_ready, i + 1)
                for g in range(DC):
                    for k in range(DC):
                        v = mm(pa[:, 1, g * P:(g + 1) * P], wq[:, k, g * P:(g + 1) * P], a_xn_t[:, k, :], start=k == 0, stop=k == 1)
                v.then_inc(q_made, 1)

            def att_scores(i, b, g):
                if g == 0:
                    pe.wait_ge(q_ready, i + 1)
                else:
                    pe.wait_ge(shifted, i * 2 + g)
                for k, (nh, m0, m1) in enumerate(((TQ, 0, P), (TQ, 0, P), (HG, P, M))):
                    at = (b * DC + g) * HG * M + 512 * k
                    n = nh * (m1 - m0)
                    mm(pa[:, k, 0:n], q_t[:, g, :], k_blocks[:, at:at + n], start=True, stop=False)
                    mb = mask_bias[:, i * M + m0:i * M + m1] if isinstance(i, int) else mask_bias[:, bass.ds(i * M + m0, m1 - m0)]
                    v = mm(pa[:, k, 0:n], ident_bf, mb.unsqueeze(1).broadcast_to([P, nh, m1 - m0]), start=False, stop=True)
                v.then_inc(scores_made, 1)

            def att_prob(i, k):
                if k == 0:
                    pe.wait_ge(exp_done, i * 2 + 2)
                if k >= 2:
                    pe.wait_ge(prob_t_ready, i * 5 + k - 1)
                for j in range(TQ):
                    if k == 0:
                        v = turn(pa[0:TQ * MT, k % 2, j * P:(j + 1) * P],
                                 prob[:, j // 2, HG * P + (j % 2) * TQ * MT:HG * P + (j % 2 + 1) * TQ * MT], ident)
                    else:
                        h = TQ * ((k - 1) % 2) + j
                        v = turn(pa[:, k % 2, j * P:(j + 1) * P], prob[:, (k - 1) // 2, h * P:(h + 1) * P], ident)
                v.then_inc(prob_turned, 1)

            def att_pv(i, b, q):
                pe.wait_ge(prob_t_ready, i * 5 + q + 2)
                for j in range(TQ):
                    mm(pa[VW * j:VW * j + VW, 2, q * P:(q + 1) * P], v_rest[0:TQ * MT, b, TQ * q + j, :],
                       prob_t[0:TQ * MT, 0, q * P:(q + 1) * P], start=True, stop=False)
                for j in range(TQ):
                    v = mm(pa[VW * j:VW * j + VW, 2, q * P:(q + 1) * P], v_main[:, b, TQ * q + j, :],
                           prob_t[:, 1 + (q + 1) % 2, j * P:(j + 1) * P], start=False, stop=True)
                v.then_inc(pv_done, 1)

            def att_o(i):
                pe.wait_ge(o_ready, i + 1)
                for q in range(H // TQ):
                    v = turn(pa[:, 0, q * P:(q + 1) * P], o_t[:, q, :], ident)
                v.then_inc(o_turned, 1)

            def att_out(i):
                pe.wait_ge(att_ready, i + 1)
                for c in range(DC):
                    v = turn(pa[:, 1, c * P:(c + 1) * P], att[:, c * P:(c + 1) * P], ident)
                v.then_inc(att_turned, 1)

            def att_wo(i):
                pe.wait_ge(att_t_ready, i + 1)
                for k in range(DC):
                    v = mm(pa[:, 2, 0:D], att_t[:, k, :], wo[:, k, :], start=k == 0, stop=k == 1)
                v.then_inc(wo_made, 1)

            def ffn_turn(i, k):
                pe.wait_ge(f_xn_ready, i * 2 + k + 1)
                for c in range(DC):
                    v = turn(pf[:, 2 - 2 * k, c * P:(c + 1) * P], f_xn[:, c * P:(c + 1) * P], ident)
                v.then_inc(f_turned, 1)

            def ffn_pq(i):
                pe.wait_ge(f_xn_t_ready, i * 2 + 1)
                for e in range(4):
                    for k in range(DC):
                        v = mm(pf[:, 2, e * P:(e + 1) * P], w_pq[:, k, e * P:(e + 1) * P], f_xn_t[:, k, :], start=k == 0, stop=k == 1)
                v.then_inc(pq_made, 1)

            def ffn_up(i):
                for f in range(FC):
                    for k in range(DC):
                        v = mm(pf_flat[:, f * P:(f + 1) * P], w_up[:, k, f * P:(f + 1) * P], f_xn_t[:, k, :], start=k == 0, stop=k == 1)
                v.then_inc(up_made, 1)

            def ffn_sims(i):
                pe.wait_ge(pq_ready, i + 1)
                for e in range(4):
                    v = mm(pf[:, 2, e * P:(e + 1) * P], pq_t[:, e * P:(e + 1) * P], keys[:, e, :], start=True, stop=True)
                v.then_inc(sims_made, 1)

            def ffn_g(i):
                pe.wait_ge(up_ready, i + 1)
                for n in range(2):
                    for k in range(DC):
                        v = mm(pf[:, n, :], f_xn_t[:, k, :], de[:, k, n * 512:(n + 1) * 512], start=k == 0, stop=k == 1)
                v.then_inc(g_made, 1)

            def ffn_down(i):
                pe.wait_ge(sims_read, i + 1)
                for f in range(FC):
                    v = mm(pf[:, 2, 0:D], up_t[:, f * P:(f + 1) * P], w_down[:, f, :], start=f == 0, stop=False)
                v.then_inc(down_made, 1)

            def ffn_w(i, k):
                pe.wait_ge(w_ready, i + 1)
                for e in range(4 * k, 4 * k + 4):
                    for h in range(PH):
                        v = mm(pf[:, k, (e % 4) * P:(e % 4 + 1) * P], big1[:, h * NE + e * P:h * NE + (e + 1) * P], ident,
                               start=h == 0, stop=h == PH - 1)
                v.then_inc(w_turned, 1)

            def ffn_out(i):
                for e in range(NE // P):
                    if e % 4 == 0:
                        pe.wait_ge(w_t_ready, i * 2 + e // 4 + 1)
                    v = mm(pf[:, 2, 0:D], big2[:, e * P:(e + 1) * P], ue[:, e, :], start=False, stop=e == NE // P - 1)
                v.then_inc(ffn_made, 1)

            def ffn_feat(i):
                pe.wait_ge(f_xn_t_ready, i * 2 + 2)
                for c in range(DC):
                    for k in range(DC):
                        v = mm(pf[:, 1, c * P:(c + 1) * P], w_feat[:, k, c * P:(c + 1) * P], f_xn_t[:, k, :], start=k == 0, stop=k == 1)
                v.then_inc(feat_made, 1)

            def tanh_rows(b, it, k0, k1):
                n0 = (it + b * IT) * ROUND
                for k in range(k0, k1, 2):
                    if k == 0:
                        pe.wait_ge(rho_ready, it + b * IT + 1)
                    pe.wait_ge(h_ready, n0 + k + 2)
                    for h in range(2):
                        for kk in (k, k + 1):
                            r, c, j = ORDER[kk]
                            last = c == DC - 1 and (r == TR - 1 or 4 * (r + 1) + j >= TI)
                            v = mm(pr[32 * j:32 * j + 32, h, :], window[:, c, 31 - r:63 - r], ring[:, kk % 4, h * 512:(h + 1) * 512],
                                   start=r == 0 and c == 0, stop=last)
                    v.then_inc(h_used, 2)

            def attention(i, b):
                att_turn(i)
                att_q(i)
                att_scores(i, b, 0)
                att_scores(i, b, 1)
                att_prob(i, 0)
                att_prob(i, 1)
                for q in range(H // TQ):
                    if q < 3:
                        att_prob(i, q + 2)
                    att_pv(i, b, q)
                att_o(i)
                att_out(i)
                att_wo(i)

            def front(i, b, a_next=True, tanh=None):
                rows = (lambda k0, k1: tanh_rows(*tanh, k0, k1)) if tanh else (lambda k0, k1: None)
                j = i + 1
                ffn_turn(i, 0)
                rows(0, 2)
                ffn_pq(i)
                if a_next:
                    att_turn(j)
                    att_q(j)
                ffn_sims(i)
                rows(2, 4)
                ffn_up(i)
                rows(4, 10)
                ffn_g(i)
                rows(10, 14)
                ffn_down(i)
                rows(14, 22)
                if a_next:
                    att_scores(j, b, 0)
                    rows(22, 26)
                    att_scores(j, b, 1)
                else:
                    rows(22, 26)
                rows(26, 30)
                ffn_w(i, 0)
                rows(30, 32)
                ffn_w(i, 1)
                if a_next:
                    att_prob(j, 0)
                    att_prob(j, 1)
                rows(32, 34)
                ffn_out(i)
                rows(34, 36)
                if a_next:
                    att_prob(j, 2)
                    att_pv(j, b, 0)
                    att_prob(j, 3)
                    att_pv(j, b, 1)
                rows(36, 38)
                ffn_turn(i, 1)
                if a_next:
                    att_prob(j, 4)
                    att_pv(j, b, 2)
                    att_pv(j, b, 3)
                rows(38, 40)
                ffn_feat(i)
                if a_next:
                    att_o(j)
                    rows(40, 42)
                    att_out(j)
                    rows(42, ROUND)
                    att_wo(j)
                else:
                    rows(40, ROUND)

            attention(0, 0)
            with pe.Fori(0, NTB - 1) as i:
                front(i, 0)
            front(NTB - 1, 1)
            with pe.Fori(0, IT) as it:
                front(it + NTB, 1, tanh=(0, it))
            front(NT - 1, 1, a_next=False)

            def rho_turn(b):
                pe.wait_ge(rho_in, 16 * (b + 1))
                if b == 0:
                    pe.wait_ge(feat_done, 2)
                for n in range(NTB):
                    for k in range(2):
                        at = (n % 3) * R + k * HALF
                        v = turn(pa[:, n // 3, at:at + HALF], rho_back[b][0:HALF, k, n * P:(n + 1) * P], ident[0:HALF, 0:HALF])
                v.then_inc(rho_turned, 1)

            def rows4_turn(b, k):
                pe.wait_ge(rows4_ready, b * NTB + 2 * k + 2)
                for m in range(2 * k, 2 * k + 2):
                    for c in range(DC):
                        v = turn((pa if k % 2 else pf)[:, k // 2, ((m % 2) * DC + c) * P:((m % 2) * DC + c + 1) * P],
                                 rows4[b][:, m, c * P:(c + 1) * P], ident)
                v.then_inc(rows4_turned, 1)

            def router(b):
                pe.wait_ge(rows4_t_ready, b * 4 + 4)
                for m in range(NTB):
                    for c in range(DC):
                        v = mm(pa[:, 2, m * E:(m + 1) * E], rows_t[:, m, c * P:(c + 1) * P], w_router[:, c, :], start=c == 0, stop=c == 1)
                v.then_inc(router_made, 1)

            rho_turn(0)
            tanh_rows(1, 0, 0, ROUND)
            tanh_rows(1, 1, 0, 16)
            for k in range(4):
                rows4_turn(0, k)
            tanh_rows(1, 1, 16, 24)
            router(0)
            tanh_rows(1, 1, 24, ROUND)
            with pe.Fori(2, IT) as it:
                tanh_rows(1, it, 0, ROUND)
            rho_turn(1)
            for k in range(4):
                rows4_turn(1, k)
            router(1)
            pe.wait_ge(pick_ready, 1)
            mm(pf[:, 0, 0:T], before, route[:, 6 * T:7 * T], start=True, stop=True)
            mm(pf[:, 0, T:2 * T], ones, route[:, 6 * T:7 * T], start=True, stop=True).then_inc(ranks_made, 1)

            owner_i = owner[0:1, :].bitcast(I32)

            def expert_of(m):
                at = owner_i[:, m:m + 1] if isinstance(m, int) else owner_i[:, bass.ds(m, 1)]
                return pe.value_load(at, min_val=0, max_val=E - 1)

            def turn_rows(m):
                pe.wait_ge(row_landed, m * 16 + 16)
                for c in range(DC):
                    v = turn(pf[:, 0, c * P:(c + 1) * P], row_in[:, c * P:(c + 1) * P], ident)
                v.then_inc(row_turned, 1)

            def up(m):
                e = expert_of(m)
                pe.wait_ge(row_t_ready, m + 1)
                pe.wait_ge(bias_up_in, m * 16 + 16)
                for n in range(2):
                    for k in range(DC):
                        mm(pa[:, n, :], row_t[:, k * P:(k + 1) * P], w1[:, bass.ds((e * DC + k) * FF + n * 512, 512)], start=k == 0, stop=False)
                    v = mm(pa[:, n, :], ones3[0:3, :], bias_up[0:3, n * 512:(n + 1) * 512], start=False, stop=True)
                v.then_inc(hid_made, 1)

            def turn_hid(m):
                pe.wait_ge(hid_ready, m + 1)
                for f in range(FC):
                    v = turn(pf[:, 1 + f // 4, (f % 4) * P:(f % 4 + 1) * P], hid[:, f * P:(f + 1) * P], ident)
                    if f % 4 == 3:
                        v.then_inc(hid_turned, 1)

            def down(m):
                e = expert_of(m)
                for f in range(FC):
                    if f % 4 == 0:
                        pe.wait_ge(hid_t_ready, m * 2 + f // 4 + 1)
                    mm(pa[:, 2, 0:D], hid_t[:, f * P:(f + 1) * P], w2[:, bass.ds((e * FC + f) * D, D)], start=f == 0, stop=False)
                pe.wait_ge(bias_y_in, m * 16 + 16)
                mm(pa[:, 2, 0:D], ones3[0:3, :], bias_y[0:3, :], start=False, stop=True).then_inc(y_made, 1)

            pe.wait_ge(slots_ready, 1)
            pe.wait_ge(experts_in, 32 * E)
            turn_rows(0)
            up(0)
            turn_rows(1)
            with pe.Fori(0, MOE_TILES - 2) as m:
                turn_hid(m)
                up(m + 1)
                turn_rows(m + 2)
                down(m)
            turn_hid(MOE_TILES - 2)
            up(MOE_TILES - 1)
            down(MOE_TILES - 2)
            turn_hid(MOE_TILES - 1)
            down(MOE_TILES - 1)


def kernel(**inputs):
    import concourse.bacc as bacc
    from concourse.bass_utils import run_bass_kernel_spmd

    a = {k: np.asarray(v) for k, v in inputs.items()}

    def chunks(w):
        return np.ascontiguousarray(w.reshape(-1, P, w.shape[-1]).transpose(1, 0, 2))

    keys = a["L0_ffn_keys"]
    key_blocks = np.zeros((P, 4, P), keys.dtype)
    for e in range(4):
        for j in range(2):
            key_blocks[64 * j:64 * j + 64, e, 64 * j:64 * j + 64] = keys[2 * (e % 2) + j, :, e // 2, :].T
    lay = {
        "x": a["x"].reshape(B * S, D),
        "mask": a["mask_BxSxS2_fk1"].reshape(B * S, M),
        "ctx_t": chunks(a["ctx_1024"].reshape(B * M, D).T),
        "gates": np.concatenate([a["g_xattn"], a["g_ffn"]]).reshape(4),
        "wq_t": chunks(a["L0_xattn_Wq"].T), "wk_t": chunks(a["L0_xattn_Wk"].T),
        "wv_t": chunks(a["L0_xattn_Wv"].T), "wo_t": chunks(a["L0_xattn_Wo"].T),
        "bq": a["L0_xattn_bq"].reshape(DC, P).T, "bk": a["L0_xattn_bk"].reshape(DC, P).T,
        "bv": a["L0_xattn_bv"], "bo": a["L0_xattn_bo"],
        "w_up_t": chunks(a["L0_ffn_W_up"].T), "w_down_t": chunks(a["L0_ffn_W_down"].T),
        "w_pq_t": chunks(a["L0_ffn_W_q"].T), "keys": key_blocks,
        "de_t": chunks(a["L0_ffn_down_embed"].T), "ue": chunks(a["L0_ffn_up_embed"]),
        "w_feat": chunks(a["L1_xattn_W"]), "w_txt": chunks(a["L1_xattn_Ws"]),
        "b_txt": a["L1_xattn_b"].reshape(DC, P).T,
        "w_rho": a["L1_xattn_w"].reshape(DC, P).T,
        "gate_w": np.stack([a["L1_xattn_Wcw"][0], a["L1_xattn_Wcb"][0]]).reshape(2, DC, P).transpose(2, 0, 1),
        "gate_bias": np.concatenate([a["L1_xattn_bcw"], a["L1_xattn_bcb"]]),
        "q_mask": a["mask_BxS2_ik0"].reshape(B * M),
        "w_router": chunks(a["L1_ffn_router_w"].T),
        "expert_bias": np.concatenate([a["L1_ffn_b1"], a["L1_ffn_b2"]], axis=1).reshape(P, 80),
        "w1": a["L1_ffn_w1"].reshape(E, FF, DC, P).transpose(3, 0, 2, 1).reshape(P, E * DC * FF),
        "w2": a["L1_ffn_w2"].reshape(E, D, FC, P).transpose(3, 0, 2, 1).reshape(P, E * FC * D),
        "before": (np.arange(P)[:, None] < np.arange(P)[None, :]).astype(np.float32),
        "ident": np.eye(P, dtype=np.float32),
        "headmask": (np.arange(P)[:, None] // HD == np.arange(HG)[None, :]).astype(np.float32),
    }
    nc = bacc.Bacc("TRN2", target_bir_lowering=False, num_devices=1)
    arrays, t = {}, {}
    for name, v in lay.items():
        v = np.ascontiguousarray(v)
        arrays["in_" + name] = v
        t[name] = nc.dram_tensor("in_" + name, v.shape, mybir.dt.from_np(v.dtype), kind="ExternalInput").ap()
    out = nc.dram_tensor("out_0", (B * S, D), F32, kind="ExternalOutput").ap()
    build(nc, t, out)
    r = run_bass_kernel_spmd(nc, [arrays], core_ids=[0])
    return np.asarray(r.results[0]["out_0"]).reshape(B, S, D)
```

```python
from contextlib import ExitStack

import numpy as np

import concourse.bass as bass
from concourse import mybir

ALU = mybir.AluOpType
ACT = mybir.ActivationFunctionType
F32 = mybir.dt.float32
BF16 = mybir.dt.bfloat16
I32 = mybir.dt.int32
U32 = mybir.dt.uint32
AX = mybir.AxisListType

P = 128
B, S, D = 2, 1024, 256
M = 154
NT = B * S // P
NTB = S // P
DC = D // P
H, HD = 16, 16
HG = P // HD
MT = M - P
TQ = 4
FF = 1024
FC = FF // P
PH, NK, TOPK = 4, 64, 8
NE = 1024
NX = NE // NK
MASKED = -(2.0 ** 100)
FAR = 3.0e38
EPS = 1e-5
NTU = 4
UN = NTU * P
UNITS = NT // NTU
IT, TI = 4, 39
TR = 10
RI = 4 * TR
R = IT * RI
RING = 13
E = 8
MOE_TILES = 2 * B * S // P + E - 1
PLACES = B * S
VW = 32
NEG = -1e30


def build(nc, t, out):
    ctx = ExitStack()
    with ctx:
        WORDS = 53200
        arena = ctx.enter_context(nc.sbuf_tensor("arena", [P, WORDS], F32))
        top = [0]

        def words(n, at=None):
            o = top[0] if at is None else at
            if at is None:
                top[0] += n
            assert o + n <= WORDS, (o, n)
            return arena[:, o:o + n]

        def sem(name):
            return ctx.enter_context(nc.semaphore(name))

        x = words(NT * D).rearrange("p (i d) -> p i d", i=NT)
        feat0 = top[0]
        feat_t = words(UNITS * DC * UN).rearrange("p (u c n) -> p u c n", u=UNITS, c=DC)
        ring0 = top[0]
        ring = words(RING * UN).rearrange("p (k n) -> p k n", k=RING)
        mean3 = words(NT)
        rstd3 = words(NT)
        gate = words(8)
        ident = words(P)
        ident_bf = words(P // 2).bitcast(BF16)
        even_odd = words(2)
        iota16 = words(NX)
        neg_half = words(NTU)
        window = words(DC * 63).rearrange("p (c n) -> p c n", c=DC)
        w_rho = words(DC)
        q_bias = words(B * R).rearrange("p (b n) -> p b n", b=B)
        gate_rows = words(2 * B * R).rearrange("p (k b n) -> p k b n", k=2, b=B)
        gate_bias = words(2)
        w_router = words(DC * E).rearrange("p (c n) -> p c n", c=DC)
        before = words(P)
        ones = words(P)
        steps128 = words(NT)
        tile_no = words(MOE_TILES)
        ones3 = words(P // 2).bitcast(BF16)
        txt_bias = words(DC * (B * M + 2)).rearrange("p (c m) -> p c m", c=DC)
        rho_rows = words(UN)
        gates3 = words(NTU * 2)
        dots = words(NT * 4)
        logits = words(NT * E)
        picks = words(2 * NT)
        slots = words(2 * NT)
        owner = words(MOE_TILES)
        tile_at = words(MOE_TILES)
        best = words(NT * E)
        pick_p = words(NT * E)
        pick_e = words(2 * NT)
        place_f = words(2 * NT)
        slots_out = words(2 * NT)
        start = words(E)
        shift_e = words(E)
        count = words(E)
        place0 = words(E)
        bn4 = words(NTU * 6)
        stat4 = words(NTU * 2)
        var4 = words(NTU)
        rstd4 = words(NTU)
        carrier = words(1)
        front0 = top[0]
        wq = words(DC * D).rearrange("p (c n) -> p c n", c=DC)
        wo = words(DC * D).rearrange("p (c n) -> p c n", c=DC)
        w_feat = words(DC * D).rearrange("p (c n) -> p c n", c=DC)
        w_up = words(DC * FF).rearrange("p (c n) -> p c n", c=DC)
        w_down = words(FC * D).rearrange("p (c n) -> p c n", c=FC)
        w_pq = words(DC * 2 * D).rearrange("p (c n) -> p c n", c=DC)
        keys = words(4 * P).rearrange("p (c n) -> p c n", c=4)
        de = words(DC * NE).rearrange("p (c n) -> p c n", c=DC)
        ue = words(NE // P * D).rearrange("p (c n) -> p c n", c=NE // P)
        bq = words(DC)
        bk = words(DC)
        b_txt = words(DC)
        bo = words(D)
        mask_bias = words(NT * M // 2).bitcast(BF16)
        k_blocks = words(B * DC * 2 * M).rearrange("p (b g n) -> p b g n", b=B, g=DC)
        v_main = words(B * H * VW).rearrange("p (b h e) -> p b h e", b=B, h=H)
        v_rest = words(B * H * VW).rearrange("p (b h e) -> p b h e", b=B, h=H)
        a_xn = words(D)
        a_xn_t = words(D).rearrange("p (c n) -> p c n", c=DC)
        a_bn = words(6)
        a_stat = words(2)
        a_var = words(1)
        a_rstd = words(1)
        q_t = words(D).rearrange("p (c n) -> p c n", c=DC)
        row_max = words(HG)
        r_den = words(H)
        prob = words(H * M).rearrange("p (g n) -> p g n", g=DC)
        prob_t = words(3 * 512).rearrange("p (k n) -> p k n", k=3)
        o_t = words(512).rearrange("p (q n) -> p q n", q=H // TQ)
        att = words(D)
        att_t = a_xn_t
        proj = a_xn
        n_xn = words(D)
        n_xn_t = words(D).rearrange("p (c n) -> p c n", c=DC)
        n_bn = words(6)
        n_stat = words(2)
        n_var = words(1)
        n_rstd = words(1)
        f_xn = words(D)
        f_xn_t = words(D).rearrange("p (c n) -> p c n", c=DC)
        f_bn = words(6)
        f_stat = words(2)
        f_var = words(1)
        f_rstd = words(1)
        scores = words(8 * NK)
        top_xy = words(64)
        idx = words(32)
        idx_f = words(32)
        far_off = words(32)
        grid = words(256)
        grid_rep = words(256)
        grid_sel = words(256)
        grid_b = words(256)
        top_s = words(32)
        t8 = words(32)
        t16 = words(64)
        cmp16 = words(512)
        pq_t = cmp16
        e_in = words(4 * 104).rearrange("p (h n) -> p h n", h=PH)
        den4 = words(PH)
        last_sum = words(1)
        big1 = words(PH * NE)
        big2 = words(PH * NE)
        up_act = big2[:, 0:FF]
        up_t = big2[:, FF:2 * FF]
        print("arena words", top[0])
        w1 = words(E * DC * FF, front0)
        w2 = words(E * FC * D, front0 + E * DC * FF)
        late0 = front0 + E * DC * FF + E * FC * D
        rho_t = words(NTU * R, late0).rearrange("p (i n) -> p i n", i=NTU)
        rho_w = words(NTU * R, late0 + NTU * R).rearrange("p (i n) -> p i n", i=NTU)
        rows_t = words(NTU * D, late0).rearrange("p (i n) -> p i n", i=NTU)
        route = words(8 * NTU * E, late0 + 6 * D)
        own_w = words(MOE_TILES * (2 * E + 4) + 3 * E + E * NT, late0)
        row_in = words(D, late0)
        row_t = words(D, late0 + D)
        row_out = words(D, late0 + 2 * D)
        bias_up = words(FF // 2, late0 + 3 * D).bitcast(BF16)
        bias_y = words(D // 2, late0 + 5 * D).bitcast(BF16)
        rho_back = [words(2 * UN, feat0 + u * DC * UN).rearrange("p (k n) -> p k n", k=2) for u in range(UNITS)]
        rows4 = [words(NTU * D, feat0 + u * DC * UN).rearrange("p (i d) -> p i d", i=NTU) for u in range(UNITS)]
        hid = words(FF, ring0)
        hid_t = words(FF, ring0 + FF)
        back = words(2 * NT * D, feat0).rearrange("p (i k d) -> p i k d", k=2, d=D)
        zero_rows = rho_rows[:, 0:D]
        assert NT * M + DC * B * M <= PH * NE
        mask = big2[:, 0:NT * M]
        ctx_t = big2[:, NT * M:NT * M + DC * B * M].rearrange("p (c m) -> p c m", c=DC)
        stage = words(4 * S, ring0).rearrange("p (k n) -> p k n", k=4)
        wk = stage[:, 0, 0:512].rearrange("p (c n) -> p c n", c=DC)
        wv = stage[:, 0, 512:1024].rearrange("p (c n) -> p c n", c=DC)
        w_txt = stage[:, 1, 0:512].rearrange("p (c n) -> p c n", c=DC)
        bv = stage[:, 1, 512:768]
        k_t = stage[:, 2, 0:DC * B * M].rearrange("p (c m) -> p c m", c=DC)
        gate_w = stage[:, 2, 700:704].rearrange("p (k c) -> p k c", k=2)
        q_mask = stage[:, 2, 704:704 + B * M].bitcast(I32)
        bias_all = stage[:, 1, 768:848]
        bias_left = stage[:, 1, 848:928]
        bias_part = [a.bitcast(BF16) for a in (stage[:, 1, 928:968], stage[:, 1, 968:1008], stage[:, 2, 616:656])]
        v_short = stage[:, 3, :].rearrange("p (b h e) -> p b h e", b=B, h=H)

        rho_d = nc.dram_tensor("rho_d", (UNITS, R, UN), F32, kind="Internal").ap()
        rows_d = nc.dram_tensor("rows_d", (E * PLACES + P, D), F32, kind="Internal").ap()
        outs_d = nc.dram_tensor("outs_d", (MOE_TILES * P, D), F32, kind="Internal").ap()
        bias_d = nc.dram_tensor("bias_d", (3, E, FF + D), BF16, kind="Internal").ap()

        pa = ctx.enter_context(nc.psum_tensor("pa", [P, 4, 512], F32))
        pf = ctx.enter_context(nc.psum_tensor("pf", [P, 3, 512], F32))
        pr = ctx.enter_context(nc.psum_tensor("pr", [P, 512], F32))[:, :]
        pa_flat = pa[:, :, :].rearrange("p k n -> p (k n)")
        gate_acc = [pf[:, 2, :], pr]
        pf_flat = pf[:, :, :].rearrange("p k n -> p (k n)")

        consts_in = sem("consts_in")
        weights_in = sem("weights_in")
        rows_in = sem("rows_in")
        gates_on = sem("gates_on")
        v_rest_in = sem("v_rest_in")
        setup_mm = sem("setup_mm")
        setup_step = sem("setup_step")
        setup_done = sem("setup_done")
        setup_read = sem("setup_read")
        ones_set = sem("ones_set")
        bias_split = sem("bias_split")
        bias_out = sem("bias_out")
        zeroed = sem("zeroed")
        a_var_ready = sem("a_var_ready")
        a_rstd_ready = sem("a_rstd_ready")
        a_xn_ready = sem("a_xn_ready")
        a_turned = sem("a_turned")
        a_xn_t_ready = sem("a_xn_t_ready")
        q_made = sem("q_made")
        q_ready = sem("q_ready")
        scores_made = sem("scores_made")
        shifted = sem("shifted")
        exp_done = sem("exp_done")
        prob_turned = sem("prob_turned")
        prob_t_ready = sem("prob_t_ready")
        pv_done = sem("pv_done")
        o_ready = sem("o_ready")
        o_turned = sem("o_turned")
        att_ready = sem("att_ready")
        att_turned = sem("att_turned")
        att_t_ready = sem("att_t_ready")
        wo_made = sem("wo_made")
        a_step = sem("a_step")
        f_var_ready = sem("f_var_ready")
        f_rstd_ready = sem("f_rstd_ready")
        f_xn_ready = sem("f_xn_ready")
        f_turned = sem("f_turned")
        f_xn_t_ready = sem("f_xn_t_ready")
        up_made = sem("up_made")
        up_tanh = sem("up_tanh")
        up_ready = sem("up_ready")
        pq_made = sem("pq_made")
        pq_ready = sem("pq_ready")
        sims_made = sem("sims_made")
        sims_read = sem("sims_read")
        e_in_ready = sem("e_in_ready")
        e_done = sem("e_done")
        g_made = sem("g_made")
        down_made = sem("down_made")
        u_ready = sem("u_ready")
        u_tanh = sem("u_tanh")
        w_ready = sem("w_ready")
        w_turned = sem("w_turned")
        w_t_ready = sem("w_t_ready")
        ffn_made = sem("ffn_made")
        feat_made = sem("feat_made")
        f_step = sem("f_step")
        n_var_ready = sem("n_var_ready")
        n_rstd_ready = sem("n_rstd_ready")
        n_xn_ready = sem("n_xn_ready")
        n_turned = sem("n_turned")
        n_xn_t_ready = sem("n_xn_t_ready")
        n_step = sem("n_step")
        g_step = sem("g_step")
        feat_done = sem("feat_done")
        h_ready = sem("h_ready")
        h_used = sem("h_used")
        rho_ready = sem("rho_ready")
        rho_out = sem("rho_out")
        rho_in = [sem(f"rho_in_{u}") for u in range(UNITS)]
        rho_turned = sem("rho_turned")
        att1_in = sem("att1_in")
        att1_exp = sem("att1_exp")
        gates_in = sem("gates_in")
        gates_tanh = sem("gates_tanh")
        late_step = sem("late_step")
        var4_ready = sem("var4_ready")
        rstd4_ready = sem("rstd4_ready")
        rows4_ready = sem("rows4_ready")
        rows4_turned = sem("rows4_turned")
        rows4_t_ready = sem("rows4_t_ready")
        router_made = sem("router_made")
        experts_in = sem("experts_in")
        picks_in = sem("picks_in")
        picks_exp = sem("picks_exp")
        pick_ready = sem("pick_ready")
        ranks_made = sem("ranks_made")
        slots_ready = sem("slots_ready")
        tiles_ready = sem("tiles_ready")
        out_slots_ready = sem("out_slots_ready")
        scattered = sem("scattered")
        row_landed = sem("row_landed")
        bias_up_in = sem("bias_up_in")
        bias_y_in = sem("bias_y_in")
        row_turned = sem("row_turned")
        row_t_ready = sem("row_t_ready")
        hid_made = sem("hid_made")
        hid_ready = sem("hid_ready")
        hid_turned = sem("hid_turned")
        hid_t_ready = sem("hid_t_ready")
        y_made = sem("y_made")
        y_ready = sem("y_ready")
        y_stored = sem("y_stored")
        gathered = [sem(f"gathered_{g}") for g in range(NT // 4)]
        folded = sem("folded")
        stored = sem("stored")

        CONSTS = 19
        A_STEPS = 7
        F_STEPS = 21
        N_STEPS = 3
        G_STEPS = 2
        ORDER = [(r, c, j) for r in range(TR) for c in range(DC) for j in range(4) if 4 * r + j < TI]
        ROUND = len(ORDER)
        HALF = R // 2
        T = NTU * E
        FUSED = [(4, 2, 0, 0, 0, 0), (6, 1, 0, 2, 0, 1), (7, 1, 0, 3, 1, 1), (8, 4, 1, 0, 1, 1), (12, 2, 2, 0, 1, 1),
                 (14, 1, 2, 2, 1, None), (15, 1, 2, 3, None, None)]

        block = ctx.enter_context(nc.Block())

        @block.sync
        def _(sp):
            small = [(ident, t["ident"]), (ctx_t, t["ctx_t"]), (wk, t["wk_t"]), (wv, t["wv_t"]), (w_txt, t["w_txt"]),
                     (even_odd, t["even_odd"]), (bk, t["bk"]), (bq, t["bq"]), (b_txt, t["b_txt"]),
                     (w_rho, t["w_rho"]), (w_router, t["w_router"]), (before, t["before"]), (gate_w, t["gate_w"]),
                     (gate_bias, t["gate_bias"].partition_broadcast(P)), (q_mask, t["q_mask"].partition_broadcast(P)),
                     (bias_all, t["expert_bias"]),
                     (bv, t["bv"].partition_broadcast(P)), (bo, t["bo"].partition_broadcast(P)),
                     (gate[:, 0:4], t["gates"].partition_broadcast(P))]
            assert len(small) == CONSTS
            for dst, src in small:
                sp.dma_start(dst, src).then_inc(consts_in, 16)
            for b in range(B):
                n = slice(b * NTB, (b + 1) * NTB)
                sp.dma_start(mask.rearrange("p (i m) -> p i m", i=NT)[:, n, :],
                             t["mask"].rearrange("(i p) m -> p i m", p=P)[:, n, :]).then_inc(rows_in, 16)
                sp.dma_start(x[:, n, :], t["x"].rearrange("(i p) d -> p i d", p=P)[:, n, :]).then_inc(rows_in, 16)
            for dst, src in [(wq, t["wq_t"]), (wo, t["wo_t"]), (w_pq, t["w_pq_t"]), (w_up, t["w_up_t"]), (keys, t["keys"]),
                             (de, t["de_t"]), (w_down, t["w_down_t"]), (ue, t["ue"]), (w_feat, t["w_feat"])]:
                sp.dma_start(dst, src).then_inc(weights_in, 16)
            sp.wait_ge(ones_set, 3)
            for b in range(B):
                for j in range(TQ):
                    dst = v_rest[MT * j:MT * j + MT, b, :, :].rearrange("p (q j) e -> p q j e", j=TQ)[:, :, j, :]
                    src = v_short[0:MT, b, :, :].rearrange("p (q j) e -> p q j e", j=TQ)[:, :, j, :]
                    sp.dma_start(dst, src).then_inc(v_rest_in, 16)
            sp.wait_ge(bias_split, 1)
            for k in range(3):
                sp.dma_start(bias_d[k].rearrange("e (q n) -> (e q) n", n=80), bias_part[k]).then_inc(bias_out, 16)
            sp.dma_start(rows_d.rearrange("(p i) d -> p i d", p=P),
                         zero_rows.unsqueeze(1).broadcast_to([P, E * PLACES // P + 1, D])).then_inc(zeroed, 16)

            def rho_round(u, it):
                sp.wait_ge(rho_ready, it + u * IT + 2)
                for j in range(4):
                    sp.dma_start(rho_d[u, bass.ds(it * RI + j * TR, TR), :], rho_rows[32 * j:32 * j + TR, :]).then_inc(rho_out, 16)

            def rho_load(u):
                sp.wait_ge(rho_out, 64 * IT * (u + 1) + 64)
                sp.dma_start(rho_back[u][0:HALF, :, :], rho_d[u].rearrange("(k p) n -> p k n", k=2)).then_inc(rho_in[u], 16)

            for u in range(UNITS):
                if u == UNITS - 1:
                    sp.wait_ge(feat_done, NT)
                    for e in range(E):
                        sp.dma_start(w1[:, e * DC * FF:(e + 1) * DC * FF], t["w1"][:, e * DC * FF:(e + 1) * DC * FF]).then_inc(experts_in, 16)
                        sp.dma_start(w2[:, e * FC * D:(e + 1) * FC * D], t["w2"][:, e * FC * D:(e + 1) * FC * D]).then_inc(experts_in, 16)
                with sp.Fori(0, IT) as it:
                    rho_round(u, it)
                rho_load(u)

            owner_i = owner[0:1, :].bitcast(I32)
            tile_at_i = tile_at[0:1, :].bitcast(I32)
            sp.wait_ge(bias_out, 48)
            sp.wait_ge(tiles_ready, 1)
            sp.wait_ge(scattered, 16 * 2 * NT)

            def expert_of(m):
                at = owner_i[:, m:m + 1] if isinstance(m, int) else owner_i[:, bass.ds(m, 1)]
                return sp.value_load(at, min_val=0, max_val=E - 1)

            def place_of(m):
                at = tile_at_i[:, m:m + 1] if isinstance(m, int) else tile_at_i[:, bass.ds(m, 1)]
                return bass.ds(sp.value_load(at, min_val=0, max_val=E * PLACES // P) * P, P)

            def load_rows(m):
                sp.dma_start(row_in, rows_d[place_of(m), :]).then_inc(row_landed, 16)

            def load_bias_up(m):
                e = expert_of(m)
                sp.dma_start(bias_up[0:3, :], bias_d[:, bass.ds(e, 1), 0:FF].rearrange("k e n -> k (e n)")).then_inc(bias_up_in, 16)

            def load_bias_y(m):
                e = expert_of(m)
                sp.dma_start(bias_y[0:3, :], bias_d[:, bass.ds(e, 1), FF:FF + D].rearrange("k e n -> k (e n)")).then_inc(bias_y_in, 16)

            load_rows(0)
            load_bias_up(0)
            load_bias_y(0)
            sp.wait_ge(row_turned, 1)
            load_rows(1)
            sp.wait_ge(hid_made, 1)
            load_bias_up(1)
            sp.wait_ge(row_turned, 2)
            load_rows(2)

            def expert_tile(m, ahead):
                if ahead >= 2:
                    sp.wait_ge(hid_made, m + 2)
                    load_bias_up(m + 2)
                if ahead >= 3:
                    sp.wait_ge(row_turned, m + 3)
                    load_rows(m + 3)
                sp.wait_ge(y_ready, m + 1)
                dst = outs_d[m * P:m * P + P, :] if isinstance(m, int) else outs_d[bass.ds(m * P, P), :]
                sp.dma_start(dst, row_out).then_inc(y_stored, 16)
                if ahead >= 1:
                    load_bias_y(m + 1)

            with sp.Fori(0, MOE_TILES - 3) as m:
                expert_tile(m, 3)
            for ahead in (2, 1, 0):
                expert_tile(MOE_TILES - 1 - ahead, ahead)
            for n in range(0, NT, 4):
                sp.wait_ge(folded, 2 * (n + 4))
                sp.dma_start(out.rearrange("(i p) d -> p i d", p=P)[:, n:n + 4, :], x[:, n:n + 4, :]).then_inc(stored, 16)
            sp.wait_ge(stored, 16 * NT // 4)

        @block.gpsimd
        def _(pool):
            pool.memset(v_main[:, :, :, :], 0.0)
            pool.memset(v_short[:, :, :, :], 0.0)
            pool.memset(v_rest[:, :, :, :], 0.0)
            pool.memset(neg_half, -0.5)
            pool.memset(ones3, 1.0)
            pool.iota(steps128, [[P, NT]], base=0, channel_multiplier=0, allow_small_or_imprecise_dtypes=True)
            pool.iota(tile_no, [[1, MOE_TILES]], base=0, channel_multiplier=0, allow_small_or_imprecise_dtypes=True)
            pool.memset(zero_rows, 0.0)
            pool.iota(iota16, [[1, NX]], base=0, channel_multiplier=0,
                      allow_small_or_imprecise_dtypes=True).then_inc(ones_set, 1)

            def rstd_a(i):
                pool.wait_ge(a_var_ready, i + 1)
                nc.gpsimd.tensor_tensor(a_rstd, a_var, neg_half[:, 0:1], ALU.pow).then_inc(a_rstd_ready, 1)

            def rstd_f(i):
                pool.wait_ge(f_var_ready, i + 1)
                nc.gpsimd.tensor_tensor(f_rstd, f_var, neg_half[:, 0:1], ALU.pow).then_inc(f_rstd_ready, 1)

            def rstd_n(i):
                pool.wait_ge(n_var_ready, i + 1)
                nc.gpsimd.tensor_tensor(n_rstd, n_var, neg_half[:, 0:1], ALU.pow).then_inc(n_rstd_ready, 1)

            def front(i, one=True, two=True):
                if one:
                    rstd_f(i + 1)
                if two:
                    rstd_a(i + 2)
                rstd_n(i)

            rstd_a(0)
            rstd_f(0)
            rstd_a(1)
            with pool.Fori(0, NT - 2) as i:
                front(i)
            front(NT - 2, two=False)
            front(NT - 1, one=False, two=False)
            pool.wait_ge(zeroed, 16)
            for u in range(UNITS):
                pool.wait_ge(var4_ready, u + 1)
                nc.gpsimd.tensor_tensor(rstd4, var4, neg_half, ALU.pow).then_inc(rstd4_ready, 1)
                pool.wait_ge(slots_ready, u + 1)
                for m in range(NTU):
                    for k in range(2):
                        at = k * NT + u * NTU + m
                        pool.indirect_dma_start(out=rows_d, out_offset=bass.IndirectOffsetOnAxis(ap=slots[:, at:at + 1].bitcast(U32), axis=0),
                                                in_=rows4[u][:, m, :], in_offset=None).then_inc(scattered, 16)
            pool.wait_ge(scattered, 16 * 2 * NT)
            pool.wait_ge(out_slots_ready, 1)
            pool.wait_ge(y_stored, 16 * MOE_TILES + 16)
            for n in range(NT):
                for k in range(2):
                    at = k * NT + n
                    pool.indirect_dma_start(out=back[:, n, k, :], out_offset=None, in_=outs_d,
                                            in_offset=bass.IndirectOffsetOnAxis(ap=slots_out[:, at:at + 1].bitcast(U32), axis=0)).then_inc(gathered[n // 4], 16)

        @block.scalar
        def _(act):
            act.wait_ge(consts_in, 16 * CONSTS)
            nc.scalar.activation(gate[:, 4:8], gate[:, 0:4], ACT.Tanh).then_inc(gates_on, 1)

            def att_exp(i, g):
                act.wait_ge(shifted, i * 2 + g + 1)
                p = prob[:, g, :]
                nc.scalar.activation(p, p, ACT.Exp, scale=0.25).then_inc(exp_done, 1)

            def ffn_up(i):
                act.wait_ge(up_made, i + 1)
                nc.scalar.activation(up_act, pf_flat[:, 0:FF], ACT.Tanh, scale=0.5).then_inc(up_tanh, 1)

            def ffn_exp(i):
                act.wait_ge(e_in_ready, i + 1)
                nc.scalar.activation(e_in[:, :, :], e_in[:, :, :], ACT.Exp).then_inc(e_done, 1)

            def ffn_last(i):
                act.wait_ge(u_ready, i * 3 + 1)
                nc.scalar.activation(grid_rep, grid_b, ACT.Tanh, scale=0.5).then_inc(u_tanh, 1)

            def ffn_u(i, g):
                act.wait_ge(u_ready, i * 3 + g + 2)
                if g == 0:
                    act.wait_ge(down_made, i + 1)
                h = slice(g * 2 * NE, (g + 1) * 2 * NE)
                nc.scalar.activation(big2[:, h], big1[:, h], ACT.Tanh, scale=0.5).then_inc(u_tanh, 1)

            def tanh_rows(u, it, k0, k1):
                for k in range(k0, k1):
                    r, c, j = ORDER[k]
                    act.wait_ge(h_used, (it + u * IT) * ROUND + k + 1)
                    tt = it * TI + (u * NTU // NTB * M + 4 * r + j)
                    col = txt_bias[:, c, tt:tt + 1] if isinstance(tt, int) else txt_bias[:, c, bass.ds(tt, 1)]
                    nc.scalar.activation(ring[:, k % RING, :], feat_t[:, u, c, :], ACT.Tanh, bias=col).then_inc(h_ready, 1)

            def front(i, tanh=None, one=True):
                rows = (lambda k0, k1: tanh_rows(*tanh, k0, k1)) if tanh else (lambda k0, k1: None)
                rows(0, 10)
                ffn_exp(i)
                rows(10, 12)
                if one:
                    att_exp(i + 1, 0)
                rows(12, 14)
                ffn_up(i)
                rows(14, 24)
                if one:
                    att_exp(i + 1, 1)
                rows(24, 40)
                ffn_last(i)
                ffn_u(i, 0)
                ffn_u(i, 1)
                rows(40, ROUND)

            att_exp(0, 0)
            att_exp(0, 1)
            with act.Fori(0, NTU) as i:
                front(i)
            act.wait_ge(bias_out, 48)
            act.wait_ge(v_rest_in, 16 * TQ * B)
            for i0, n, u, it0, b1, b2 in FUSED:
                act.wait_ge(feat_done, (u + 1) * NTU)
                with act.Fori(0, n) as k:
                    front(k + i0, tanh=(u, k + it0), one=b1 is not None)
            act.wait_ge(feat_done, NT)

            def attend_exp(u):
                act.wait_ge(att1_in, u + 1)
                nc.scalar.activation(rho_t[:, :, :], rho_t[:, :, :], ACT.Exp).then_inc(att1_exp, 1)

            def attend_gates(u):
                act.wait_ge(gates_in, u + 1)
                nc.scalar.activation(gates3, gates3, ACT.Tanh).then_inc(gates_tanh, 1)

            for it in range(UNITS - 1):
                tanh_rows(UNITS - 1, it, 0, 16)
                attend_exp(it)
                tanh_rows(UNITS - 1, it, 16, 28)
                attend_gates(it)
                tanh_rows(UNITS - 1, it, 28, ROUND)
            tanh_rows(UNITS - 1, IT - 1, 0, ROUND)
            attend_exp(UNITS - 1)
            attend_gates(UNITS - 1)
            act.wait_ge(picks_in, 1)
            nc.scalar.activation(pick_p, pick_p, ACT.Exp).then_inc(picks_exp, 1)
            nc.scalar.preload_act_table(ACT.Gelu_apprx_tanh)
            with act.Fori(0, MOE_TILES) as m:
                act.wait_ge(hid_made, m + 1)
                nc.scalar.activation(hid, pa_flat[:, 0:FF], ACT.Gelu_apprx_tanh).then_inc(hid_ready, 1)

        @block.vector
        def _(dve):
            steps = [0]

            def link(ins):
                steps[0] += 1
                ins.then_inc(setup_step, 1)
                dve.wait_ge(setup_step, steps[0])

            dve.sem_inc(rho_ready, 1)
            dve.sem_inc(rho_out, 64)
            dve.sem_inc(y_stored, 16)
            dve.wait_ge(consts_in, 16 * CONSTS)
            nc.vector.tensor_copy(ident_bf, ident)
            dve.wait_ge(setup_mm, 1)
            for c in range(DC):
                nc.vector.memset(txt_bias[:, c, B * M:B * M + 2], 0.0)
                v = nc.vector.tensor_scalar(txt_bias[:, c, 0:B * M], pa[:, c, 0:B * M], b_txt[:, c:c + 1], None, ALU.add)
            link(v)
            dve.wait_ge(setup_mm, 2)
            for c in range(DC):
                v = nc.vector.tensor_scalar(k_t[:, c, :], pf[:, c, 0:B * M], bk[:, c:c + 1], None, ALU.add)
            link(v)
            for g in range(DC):
                for j in range(2):
                    v = nc.vector.tensor_scalar(k_blocks[:, :, g, j * M:(j + 1) * M], k_t[:, g, :].rearrange("p (b m) -> p b m", b=B),
                                                even_odd[:, j:j + 1], None, ALU.mult)
            dve.wait_ge(setup_mm, 3)
            dve.wait_ge(ones_set, 1)
            bv_h = bv.rearrange("p (h e) -> p h e", h=H)
            for b in range(B):
                nc.vector.memset(v_main[:, b, :, HD:HD + 1], 1.0)
                nc.vector.memset(v_short[0:MT, b, :, HD:HD + 1], 1.0)
                nc.vector.tensor_tensor(v_main[:, b, :, 0:HD], pa[:, 2 + b, 0:D].rearrange("p (h e) -> p h e", h=H),
                                        bv_h, ALU.add)
                v = nc.vector.tensor_tensor(v_short[0:MT, b, :, 0:HD],
                                            pa[0:MT, 2 + b, D:2 * D].rearrange("p (h e) -> p h e", h=H),
                                            bv_h[0:MT], ALU.add)
                v.then_inc(ones_set, 1)
            nc.vector.tensor_scalar(place0, iota16[:, 0:E], float(PLACES), None, ALU.mult)
            nc.vector.memset(count, 0.0)
            dve.wait_ge(gates_on, 1)
            nc.vector.tensor_scalar(gate[:, 6:7], gate[:, 6:7], 0.5, None, ALU.mult).then_inc(setup_done, 1)
            dve.wait_ge(setup_done, 1)
            link(nc.vector.tensor_copy(bias_part[0], bias_all))
            link(nc.vector.tensor_tensor(bias_left, bias_all, bias_part[0], ALU.subtract))
            link(nc.vector.tensor_copy(bias_part[1], bias_left))
            link(nc.vector.tensor_tensor(bias_left, bias_left, bias_part[1], ALU.subtract))
            nc.vector.tensor_copy(bias_part[2], bias_left).then_inc(bias_split, 1)
            nc.vector.memset(window[:, :, :], 0.0)
            nc.vector.memset(q_bias[:, :, :], -FAR)
            nc.vector.memset(gate_rows[:, :, :, :], 0.0)
            link(nc.vector.memset(ones, 1.0))
            for c in range(DC):
                nc.vector.tensor_copy(window[:, c, 31:32], w_rho[:, c:c + 1])
            dve.wait_ge(setup_mm, 4)
            for its, n in ((slice(0, IT - 1), TI), (slice(IT - 1, IT), M - (IT - 1) * TI)):
                n_it = its.stop - its.start
                for j in range(4):
                    nr = (n - j + 3) // 4
                    for b in range(B):
                        for src, dst in ((q_mask, q_bias), (gate_acc[0], gate_rows[:, 0]), (gate_acc[1], gate_rows[:, 1])):
                            t0 = b * M + its.start * TI
                            sv = src[:, t0:t0 + n_it * n].rearrange("p (i t) -> p i t", i=n_it)[:, :, j:4 * (nr - 1) + j + 1:4]
                            dv = dst[:, b, :].rearrange("p (i j r) -> p i j r", i=IT, j=4)[:, its, j, 0:nr]
                            if src is q_mask:
                                v = nc.vector.tensor_scalar(dv, sv, -NEG, NEG, ALU.mult, ALU.add)
                            else:
                                v = nc.vector.tensor_copy(dv, sv)
            link(v)
            dve.wait_ge(rows_in, 64)
            link(nc.vector.tensor_scalar(mask_bias, mask, 0.0, MASKED, ALU.is_equal, ALU.mult))
            nc.vector.memset(carrier, 0.0).then_inc(setup_read, 1)

            def att_link(i, n, ins, plain=False):
                ins.then_inc(a_step, 1)
                dve.wait_ge(a_step, i * A_STEPS + n)
                if plain:
                    nc.vector.memset(carrier, 0.0)

            def ffn_link(i, n, ins, plain=False):
                ins.then_inc(f_step, 1)
                dve.wait_ge(f_step, i * F_STEPS + n)
                if plain:
                    nc.vector.memset(carrier, 0.0)

            def first_link(i, n, ins, plain=False):
                ins.then_inc(g_step, 1)
                dve.wait_ge(g_step, i * G_STEPS + n)
                if plain:
                    nc.vector.memset(carrier, 0.0)

            def norm_link(i, n, ins, plain=False):
                ins.then_inc(n_step, 1)
                dve.wait_ge(n_step, i * N_STEPS + n)
                if plain:
                    nc.vector.memset(carrier, 0.0)

            def row_of(i):
                return x[:, i, :] if isinstance(i, int) else x[:, bass.ds(i, 1), :].rearrange("p i d -> p (i d)")

            def att_norm(i):
                xi = row_of(i)
                att_link(i, 1, nc.vector.bn_stats(a_bn, xi), plain=True)
                att_link(i, 2, nc.vector.bn_aggr(a_stat, a_bn))
                nc.vector.tensor_scalar(a_var, a_stat[:, 1:2], EPS, None, ALU.add).then_inc(a_var_ready, 1)

            def att_xn(i):
                dve.wait_ge(a_rstd_ready, i + 1)
                nc.vector.tensor_scalar(a_xn, row_of(i), a_stat[:, 0:1], a_rstd, ALU.subtract, ALU.mult).then_inc(a_xn_ready, 1)

            def att_xn_t(i):
                dve.wait_ge(a_turned, i + 1)
                nc.vector.tensor_copy(a_xn_t[:, :, :].rearrange("p c n -> p (c n)"), pa[:, 0, 0:D]).then_inc(a_xn_t_ready, 1)

            def att_q(i):
                dve.wait_ge(q_made, i + 1)
                for c in range(DC):
                    v = nc.vector.tensor_scalar(q_t[:, c, :], pa[:, 1, c * P:(c + 1) * P], bq[:, c:c + 1], None, ALU.add)
                v.then_inc(q_ready, 1)

            def att_shift(i, g):
                dve.wait_ge(scores_made, i * 2 + g + 1)
                sc = pa[:, :, 0:2 * M].rearrange("p k (j m) -> p k j m", j=2)
                att_link(i, g + 3, nc.vector.tensor_reduce(row_max.rearrange("p (k j) -> p k j", k=4), sc, AX.X, ALU.max))
                mx = row_max.rearrange("p (k j) -> p k j", k=4).unsqueeze(3)
                for at, m0, m1 in ((0, 0, P), (HG * P, P, M)):
                    v = nc.vector.tensor_tensor(prob[:, g, at:at + HG * (m1 - m0)].rearrange("p (k j m) -> p k j m", k=4, j=2),
                                                sc[:, :, :, m0:m1], mx.broadcast_to([P, 4, 2, m1 - m0]), ALU.subtract)
                v.then_inc(shifted, 1)

            def att_prob_t(i, k):
                dve.wait_ge(prob_turned, i * 5 + k + 1)
                rows = TQ * MT if k == 0 else P
                if k >= 3:
                    dve.wait_ge(pv_done, i * 4 + k - 2)
                slot = 0 if k == 0 else 1 + k % 2
                nc.vector.tensor_copy(prob_t[0:rows, slot, :], pa[0:rows, k % 2, :]).then_inc(prob_t_ready, 1)

            def att_o(i):
                dve.wait_ge(pv_done, i * 4 + 4)
                nc.vector.tensor_copy(o_t[:, :, :].rearrange("p q n -> p (q n)"), pa[:, 2, :]).then_inc(o_ready, 1)

            def att_scale(i):
                dve.wait_ge(o_turned, i + 1)
                o = pa[:, 0, :].rearrange("p (h e) -> p h e", h=H)
                att_link(i, 5, nc.vector.reciprocal(r_den.unsqueeze(2), o[:, :, HD:HD + 1]))
                nc.vector.tensor_tensor(att.rearrange("p (h e) -> p h e", h=H), o[:, :, 0:HD],
                                        r_den.unsqueeze(2).broadcast_to([P, H, HD]), ALU.mult).then_inc(att_ready, 1)

            def att_att_t(i):
                dve.wait_ge(att_turned, i + 1)
                nc.vector.tensor_copy(att_t[:, :, :].rearrange("p c n -> p (c n)"), pa[:, 1, 0:D]).then_inc(att_t_ready, 1)

            def att_add(i):
                xi = row_of(i)
                dve.wait_ge(wo_made, i + 1)
                att_link(i, 6, nc.vector.tensor_tensor(proj, pa[:, 2, 0:D], bo, ALU.add))
                att_link(i, 7, nc.vector.scalar_tensor_tensor(xi, proj, gate[:, 4:5], xi, ALU.mult, ALU.add), plain=True)

            tx = top_xy[:, 0:32].rearrange("p (h k) -> p h k", h=PH)
            ty = top_xy[:, 32:64].rearrange("p (h k) -> p h k", h=PH)
            sc = scores.rearrange("p (r k) -> p r k", k=NK)
            gb4 = grid_b.rearrange("p (h i j) -> p h i j", h=PH, i=8)
            b4 = big1.rearrange("p (h x y) -> p h x y", h=PH, x=NX)
            t16_ = t16.rearrange("p (h x) -> p h x", h=PH)
            idx_u = idx.bitcast(U32)

            def ffn_norm(i):
                first_link(i, 1, nc.vector.bn_stats(f_bn, row_of(i)), plain=True)
                first_link(i, 2, nc.vector.bn_aggr(f_stat, f_bn))
                nc.vector.tensor_scalar(f_var, f_stat[:, 1:2], EPS, None, ALU.add).then_inc(f_var_ready, 1)

            def ffn_xn(i):
                dve.wait_ge(f_rstd_ready, i + 1)
                nc.vector.tensor_scalar(f_xn, row_of(i), f_stat[:, 0:1], f_rstd, ALU.subtract, ALU.mult).then_inc(f_xn_ready, 1)

            def ffn_xn_t(i):
                dve.wait_ge(f_turned, i + 1)
                nc.vector.tensor_copy(f_xn_t[:, :, :].rearrange("p c n -> p (c n)"), pf[:, 1, 0:D]).then_inc(f_xn_t_ready, 1)

            def last_norm(i):
                norm_link(i, 2, nc.vector.bn_stats(n_bn, row_of(i)), plain=True)
                norm_link(i, 3, nc.vector.bn_aggr(n_stat, n_bn))
                nc.vector.tensor_scalar(n_var, n_stat[:, 1:2], EPS, None, ALU.add).then_inc(n_var_ready, 1)

            def last_xn(i):
                dve.wait_ge(n_rstd_ready, i + 1)
                at = slice(i, i + 1) if isinstance(i, int) else bass.ds(i, 1)
                nc.vector.tensor_copy(mean3[:, at], n_stat[:, 0:1])
                nc.vector.tensor_copy(rstd3[:, at], n_rstd)
                nc.vector.tensor_scalar(n_xn, row_of(i), n_stat[:, 0:1], n_rstd, ALU.subtract, ALU.mult).then_inc(n_xn_ready, 1)

            def last_xn_t(i):
                dve.wait_ge(n_turned, i + 1)
                nc.vector.tensor_copy(n_xn_t[:, :, :].rearrange("p c n -> p (c n)"), pf[:, 2, 0:D]).then_inc(n_xn_t_ready, 1)

            def ffn_pq(i):
                dve.wait_ge(pq_made, i + 1)
                nc.vector.tensor_copy(pq_t, pf[:, 1, :]).then_inc(pq_ready, 1)

            def ffn_up(i):
                dve.wait_ge(up_tanh, i + 1)
                nc.vector.scalar_tensor_tensor(up_t, up_act, 1.0, pf_flat[:, 0:FF], ALU.add, ALU.mult).then_inc(up_ready, 1)

            def ffn_best(i):
                dve.wait_ge(sims_made, i + 1)
                nc.vector.tensor_copy(scores, pf[:, 1, :]).then_inc(sims_read, 1)
                dve.wait_ge(sims_read, i + 1)
                nc.vector.memset(carrier, 0.0)
                for r in range(2 * PH):
                    v = nc.vector.max(top_xy[:, 8 * r:8 * r + 8], scores[:, NK * r:NK * r + NK])
                ffn_link(i, 1, v, plain=True)
                for h in range(PH):
                    nc.vector.max_index(idx_u[:, 8 * h:8 * h + 8], top_xy[:, 8 * h:8 * h + 8], scores[:, NK * h:NK * h + NK])
                g4 = grid.rearrange("p (h i j) -> p h i j", h=PH, i=8)
                ffn_link(i, 2, nc.vector.tensor_tensor(g4, tx.unsqueeze(3).broadcast_to([P, PH, 8, 8]),
                                                       ty.unsqueeze(2).broadcast_to([P, PH, 8, 8]), ALU.add), plain=True)
                for h in range(PH):
                    v = nc.vector.max(top_s[:, 8 * h:8 * h + 8], grid[:, 64 * h:64 * h + 64])
                ffn_link(i, 3, v)
                ts = top_s.rearrange("p (h k) -> p h k", h=PH)
                for at, src, best in ((0, sc[:, 0:PH, 0:NX], tx), (16, sc[:, PH:2 * PH, :], ty), (80, ts, ts), (88, tx, tx), (96, ty, ty)):
                    w = src.shape[2]
                    v = nc.vector.tensor_tensor(e_in[:, :, at:at + w], src, best[:, :, 0:1].broadcast_to([P, PH, w]), ALU.subtract)
                v.then_inc(e_in_ready, 1)

            def ffn_limits(i):
                nc.vector.tensor_copy(idx_f, idx_u)
                for h in range(PH):
                    v = nc.vector.match_replace(grid_rep[:, 64 * h:64 * h + 64], top_s[:, 8 * h:8 * h + 8],
                                                grid[:, 64 * h:64 * h + 64], -FAR)
                ffn_link(i, 4, v)
                nc.vector.tensor_scalar(far_off, idx_f, float(NX), None, ALU.is_ge)
                ffn_link(i, 5, nc.vector.tensor_tensor(grid_sel, grid_rep, grid, ALU.not_equal))
                ffn_link(i, 6, nc.vector.tensor_scalar(grid_b, grid_sel, 0.0, FAR, ALU.is_equal, ALU.mult))
                ffn_link(i, 7, nc.vector.tensor_tensor(gb4, gb4, ty.unsqueeze(2).broadcast_to([P, PH, 8, 8]), ALU.add))

            def ffn_rows(i):
                t8_ = t8.rearrange("p (h i) -> p h i", h=PH)
                c4 = cmp16.rearrange("p (h x i) -> p h x i", h=PH, x=NX)
                nc.vector.tensor_reduce(t8_, gb4, AX.X, ALU.min)
                ffn_link(i, 8, nc.vector.tensor_tensor(c4, idx_f.rearrange("p (h i) -> p h i", h=PH).unsqueeze(2).broadcast_to([P, PH, NX, 8]),
                                                        iota16.unsqueeze(1).unsqueeze(3).broadcast_to([P, PH, NX, 8]), ALU.not_equal))
                ffn_link(i, 9, nc.vector.tensor_scalar(cmp16, cmp16, FAR, None, ALU.mult))
                ffn_link(i, 10, nc.vector.tensor_tensor(c4, c4, t8_.unsqueeze(2).broadcast_to([P, PH, NX, 8]), ALU.max))
                ffn_link(i, 11, nc.vector.tensor_reduce(t16_, c4, AX.X, ALU.min))

            def ffn_picked(i):
                ffn_link(i, 12, nc.vector.tensor_tensor(b4, sc[:, PH:2 * PH, :].unsqueeze(2).broadcast_to([P, PH, NX, NK]),
                                                        t16_.unsqueeze(3).broadcast_to([P, PH, NX, NK]), ALU.is_ge))

            def ffn_columns(i):
                dve.wait_ge(e_done, i + 1)
                nc.vector.tensor_tensor(b4, b4, e_in[:, :, 16:80].unsqueeze(2).broadcast_to([P, PH, NX, NK]), ALU.mult)

            def ffn_gated(i):
                ffn_link(i, 13, nc.vector.tensor_reduce(den4, e_in[:, :, 80:88], AX.X, ALU.add))
                ffn_link(i, 14, nc.vector.reciprocal(den4, den4))
                d4 = den4.unsqueeze(2)
                nc.vector.tensor_tensor(e_in[:, :, 0:16], e_in[:, :, 0:16], d4.broadcast_to([P, PH, 16]), ALU.mult)
                ffn_link(i, 15, nc.vector.tensor_tensor(e_in[:, :, 88:96], e_in[:, :, 88:96], d4.broadcast_to([P, PH, 8]), ALU.mult))
                nc.vector.tensor_tensor(b4, b4, e_in[:, :, 0:16].unsqueeze(3).broadcast_to([P, PH, NX, NK]), ALU.mult)
                ffn_link(i, 16, nc.vector.tensor_tensor(e_in[:, :, 88:96], e_in[:, :, 88:96], far_off.rearrange("p (h i) -> p h i", h=PH), ALU.mult))
                ffn_link(i, 17, nc.vector.tensor_tensor(gb4, grid_sel.rearrange("p (h i j) -> p h i j", h=PH, i=8),
                                                        e_in[:, :, 88:96].unsqueeze(3).broadcast_to([P, PH, 8, 8]), ALU.mult))
                ffn_link(i, 18, nc.vector.tensor_tensor(gb4, gb4, e_in[:, :, 96:104].unsqueeze(2).broadcast_to([P, PH, 8, 8]), ALU.mult))

            def ffn_weigh(i):
                dve.wait_ge(g_made, i + 1)
                nc.vector.tensor_scalar(grid_b, grid_b, pf_flat[:, NE - 1:NE], None, ALU.mult).then_inc(u_ready, 1)
                for g in range(2):
                    bh = big1[:, g * 2 * NE:(g + 1) * 2 * NE].rearrange("p (h e) -> p h e", h=2)
                    nc.vector.tensor_tensor(bh, bh, pf_flat[:, 0:NE].unsqueeze(1).broadcast_to([P, 2, NE]),
                                            ALU.mult).then_inc(u_ready, 1)

            def ffn_silu(i, k):
                if k == 2:
                    dve.wait_ge(u_tanh, i * 3 + 1)
                    nc.vector.scalar_tensor_tensor(grid, grid_rep, 1.0, grid_b, ALU.add, ALU.mult, accum_out=last_sum)
                else:
                    dve.wait_ge(u_tanh, i * 3 + k + 2)
                    h = slice(k * 2 * NE, (k + 1) * 2 * NE)
                    v = nc.vector.scalar_tensor_tensor(big1[:, h], big2[:, h], 1.0, big1[:, h], ALU.add, ALU.mult)
                    if k == 1:
                        ffn_link(i, 19, v)

            def ffn_sum(i, k):
                if k == 0:
                    ffn_link(i, 20, nc.vector.tensor_tensor(big1[:, 0:2 * NE], big1[:, 0:2 * NE], big1[:, 2 * NE:4 * NE], ALU.add))
                else:
                    ffn_link(i, 21, nc.vector.tensor_tensor(big1[:, 0:NE], big1[:, 0:NE], big1[:, NE:2 * NE], ALU.add))
                    nc.vector.tensor_scalar(big1[:, NE - 1:NE], big1[:, NE - 1:NE], last_sum, None, ALU.add).then_inc(w_ready, 1)

            def ffn_w_t(i, k):
                dve.wait_ge(w_turned, i * 2 + k + 1)
                nc.vector.tensor_copy(big2[:, 512 * k:512 * k + 512], pf[:, 0, :]).then_inc(w_t_ready, 1)

            def ffn_add(i):
                xi = row_of(i)
                dve.wait_ge(ffn_made, i + 1)
                norm_link(i, 1, nc.vector.scalar_tensor_tensor(xi, pf[:, 2, 0:D], gate[:, 6:7], xi, ALU.mult, ALU.add), plain=True)

            def ffn_feat(i, u):
                dve.wait_ge(feat_made, i + 1)
                m = i - u * NTU
                f = feat_t[:, u, :, m * P:m * P + P] if isinstance(m, int) else feat_t[:, u, :, bass.ds(m * P, P)]
                nc.vector.tensor_copy(f, pf[:, 2, 0:D].rearrange("p (c n) -> p c n", c=DC)).then_inc(feat_done, 1)

            def rho_round(u, it):
                n = it + u * IT
                dve.wait_ge(h_used, (n + 1) * ROUND + RING)
                dve.wait_ge(rho_out, n * 64 + 64)
                nc.vector.tensor_copy(rho_rows, pr).then_inc(rho_ready, 1)

            def attention(i):
                att_norm(i)
                att_xn(i)
                att_xn_t(i)
                att_q(i)
                att_shift(i, 0)
                att_shift(i, 1)
                for k in range(5):
                    att_prob_t(i, k)
                att_o(i)
                att_scale(i)
                att_att_t(i)
                att_add(i)

            def front(i, u, one=True, two=True):
                j, l = i + 1, i + 2
                if one:
                    att_shift(j, 0)
                ffn_picked(i)
                ffn_up(i)
                ffn_columns(i)
                if one:
                    att_shift(j, 1)
                ffn_gated(i)
                if one:
                    att_prob_t(j, 0)
                    att_prob_t(j, 1)
                ffn_weigh(i)
                if one:
                    att_prob_t(j, 2)
                    att_prob_t(j, 3)
                ffn_silu(i, 2)
                ffn_silu(i, 0)
                if one:
                    att_prob_t(j, 4)
                    att_o(j)
                ffn_silu(i, 1)
                if one:
                    att_scale(j)
                ffn_sum(i, 0)
                if one:
                    att_att_t(j)
                ffn_sum(i, 1)
                if one:
                    att_add(j)
                    ffn_norm(j)
                if two:
                    att_norm(l)
                ffn_w_t(i, 0)
                if one:
                    ffn_xn(j)
                if two:
                    att_xn(l)
                ffn_w_t(i, 1)
                if one:
                    ffn_xn_t(j)
                if two:
                    att_xn_t(l)
                if one:
                    ffn_pq(j)
                ffn_add(i)
                last_norm(i)
                if two:
                    att_q(l)
                last_xn(i)
                if one:
                    ffn_best(j)
                last_xn_t(i)
                if one:
                    ffn_limits(j)
                ffn_feat(i, u)
                if one:
                    ffn_rows(j)

            attention(0)
            ffn_norm(0)
            att_norm(1)
            ffn_xn(0)
            att_xn(1)
            ffn_xn_t(0)
            att_xn_t(1)
            ffn_pq(0)
            att_q(1)
            ffn_best(0)
            ffn_limits(0)
            ffn_rows(0)
            with dve.Fori(0, NTU) as i:
                front(i, 0)
            dve.wait_ge(zeroed, 16)
            for i0, n, u, it0, b1, b2 in FUSED:
                with dve.Fori(0, n) as k:
                    front(k + i0, u + 1, b1 is not None, b2 is not None)
                    rho_round(u, k + it0)

            late = [0]

            def late_link(ins):
                late[0] += 1
                ins.then_inc(late_step, 1)
                dve.wait_ge(late_step, late[0])

            def attend(u):
                b = u * NTU // NTB
                dve.wait_ge(rho_turned, u + 1)
                late_link(nc.vector.tensor_tensor(rho_t.rearrange("p (k i) n -> p k i n", k=2),
                                                  pa[:, 0:2, 0:2 * R].rearrange("p k (i n) -> p k i n", i=2),
                                                  q_bias[:, b, :].unsqueeze(1).unsqueeze(1).broadcast_to([P, 2, 2, R]), ALU.add))
                mx, den, dot = dots[:, 0:NTU], dots[:, NTU:2 * NTU], dots[:, 2 * NTU:4 * NTU].rearrange("p (k i) -> p k i", k=2)
                late_link(nc.vector.tensor_reduce(mx, rho_t, AX.X, ALU.max))
                nc.vector.tensor_tensor(rho_t, rho_t, mx.unsqueeze(2).broadcast_to([P, NTU, R]), ALU.subtract).then_inc(att1_in, 1)
                dve.wait_ge(att1_exp, u + 1)
                nc.vector.tensor_reduce(den, rho_t, AX.X, ALU.add)
                for k in range(2):
                    late_link(nc.vector.tensor_tensor(rho_w, rho_t, gate_rows[:, k, b, :].unsqueeze(1).broadcast_to([P, NTU, R]), ALU.mult))
                    late_link(nc.vector.tensor_reduce(dot[:, k, :], rho_w, AX.X, ALU.add))
                late_link(nc.vector.reciprocal(den, den))
                g3 = gates3.rearrange("p (k i) -> p k i", k=2)
                late_link(nc.vector.tensor_tensor(g3, dot, den.unsqueeze(1).broadcast_to([P, 2, NTU]), ALU.mult))
                nc.vector.tensor_tensor(g3, g3, gate_bias.unsqueeze(2).broadcast_to([P, 2, NTU]), ALU.add).then_inc(gates_in, 1)
                dve.wait_ge(gates_tanh, u + 1)
                late_link(nc.vector.tensor_scalar(gates3, gates3, gate[:, 5:6], None, ALU.mult))

            def post(u):
                i0 = u * NTU
                xu = x[:, i0:i0 + NTU, :]
                for m in range(NTU):
                    v = nc.vector.tensor_scalar(rows4[u][:, m, :], x[:, i0 + m, :], mean3[:, i0 + m:i0 + m + 1],
                                                rstd3[:, i0 + m:i0 + m + 1], ALU.subtract, ALU.mult)
                late_link(v)
                for m in range(NTU):
                    v = nc.vector.tensor_scalar(rows4[u][:, m, :], rows4[u][:, m, :], gates3[:, m:m + 1], gates3[:, m + NTU:m + NTU + 1],
                                                ALU.mult, ALU.add)
                late_link(v)
                late_link(nc.vector.tensor_tensor(xu, xu, rows4[u], ALU.add))
                for m in range(NTU):
                    v = nc.vector.bn_stats(bn4[:, 6 * m:6 * m + 6], x[:, i0 + m, :])
                late_link(v)
                for m in range(NTU):
                    v = nc.vector.bn_aggr(stat4[:, 2 * m:2 * m + 2], bn4[:, 6 * m:6 * m + 6])
                late_link(v)
                s4 = stat4.rearrange("p (m k) -> p m k", k=2)
                nc.vector.tensor_scalar(var4.unsqueeze(2), s4[:, :, 1:2], EPS, None, ALU.add).then_inc(var4_ready, 1)
                dve.wait_ge(rstd4_ready, u + 1)
                for m in range(NTU):
                    nc.vector.tensor_scalar(rows4[u][:, m, :], x[:, i0 + m, :], stat4[:, 2 * m:2 * m + 1], rstd4[:, m:m + 1],
                                            ALU.subtract, ALU.mult).then_inc(rows4_ready, 1)
                for k in range(2):
                    dve.wait_ge(rows4_turned, u * 2 + k + 1)
                    nc.vector.tensor_copy(rows_t[:, 2 * k:2 * k + 2, :].rearrange("p i n -> p (i n)"), pf[:, k, :]).then_inc(rows4_t_ready, 1)
                dve.wait_ge(router_made, u + 1)
                late_link(nc.vector.tensor_copy(logits[:, i0 * E:(i0 + NTU) * E], pa[:, 2, 0:NTU * E]))

            def route_rows(u):
                part = [route[:, k * T:(k + 1) * T] for k in range(8)]
                v3 = [a.rearrange("p (i e) -> p i e", i=NTU) for a in part]
                ids, ids_f, hot, place = part[0], v3[1], [v3[2], v3[3]], v3[4]
                picked, total, first, mine = part[5], v3[6], v3[7], v3[5]
                i0 = u * NTU
                for i in range(i0, i0 + NTU):
                    v = nc.vector.max(best[:, i * E:(i + 1) * E], logits[:, i * E:(i + 1) * E])
                late_link(v)
                nc.vector.memset(carrier, 0.0)
                for m in range(NTU):
                    i = i0 + m
                    v = nc.vector.max_index(ids.bitcast(U32)[:, m * E:(m + 1) * E], best[:, i * E:(i + 1) * E], logits[:, i * E:(i + 1) * E])
                late_link(v)
                late_link(nc.vector.tensor_copy(part[1], ids.bitcast(U32)))
                for k in range(2):
                    v = nc.vector.tensor_tensor(hot[k], ids_f[:, :, k:k + 1].broadcast_to([P, NTU, E]),
                                                iota16[:, 0:E].unsqueeze(1).broadcast_to([P, NTU, E]), ALU.is_equal)
                late_link(v)
                nc.vector.tensor_tensor(picked, part[2], part[3], ALU.add).then_inc(pick_ready, 1)
                dve.wait_ge(ranks_made, u + 1)
                nc.vector.tensor_copy(part[4], pf[:, 0, 0:T])
                nc.vector.tensor_copy(first[:, 0, :], count)
                late_link(nc.vector.tensor_copy(part[6], pf[:, 0, T:2 * T]))
                for m in range(1, NTU):
                    late_link(nc.vector.tensor_tensor(first[:, m, :], first[:, m - 1, :], total[:, m - 1, :], ALU.add))
                nc.vector.tensor_tensor(count, first[:, NTU - 1, :], total[:, NTU - 1, :], ALU.add)
                late_link(nc.vector.tensor_tensor(place, place, first, ALU.add))
                late_link(nc.vector.tensor_tensor(place, place, place0.unsqueeze(1).broadcast_to([P, NTU, E]), ALU.add))
                d0 = dots[:, 0:NTU]
                for k in range(2):
                    late_link(nc.vector.tensor_tensor(mine, hot[k], place, ALU.mult))
                    late_link(nc.vector.tensor_reduce(d0, mine, AX.X, ALU.add))
                    nc.vector.tensor_copy(pick_e[:, k * NT + i0:k * NT + i0 + NTU].unsqueeze(2), ids_f[:, :, k:k + 1])
                    nc.vector.tensor_copy(place_f[:, k * NT + i0:k * NT + i0 + NTU], d0)
                    v = nc.vector.tensor_copy(slots[:, k * NT + i0:k * NT + i0 + NTU].bitcast(I32), d0)
                    if k == 0:
                        late_link(v)
                v.then_inc(slots_ready, 1)

            def lay_tiles():
                W = MOE_TILES * E
                own = own_w[:, 0:W].rearrange("p (m e) -> p m e", e=E)
                own_start = own_w[:, W:2 * W].rearrange("p (m e) -> p m e", e=E)
                per = [own_w[:, 2 * W + k * MOE_TILES:2 * W + (k + 1) * MOE_TILES] for k in range(4)]
                at = 2 * W + 4 * MOE_TILES
                tiles = own_w[:, at:at + E]
                many = own_w[:, at + 3 * E:at + 3 * E + E * NT].rearrange("p (e k) -> p e k", e=E)
                late_link(nc.vector.tensor_tensor(many, count.unsqueeze(2).broadcast_to([P, E, NT]),
                                                  steps128.unsqueeze(1).broadcast_to([P, E, NT]), ALU.is_gt))
                nc.vector.memset(start, 0.0)
                late_link(nc.vector.tensor_reduce(tiles, many, AX.X, ALU.add))
                for e in range(1, E):
                    late_link(nc.vector.tensor_tensor(start[:, e:e + 1], start[:, e - 1:e], tiles[:, e - 1:e], ALU.add))
                late_link(nc.vector.tensor_tensor(own, tile_no.unsqueeze(2).broadcast_to([P, MOE_TILES, E]),
                                                  start.unsqueeze(1).broadcast_to([P, MOE_TILES, E]), ALU.is_ge))
                nc.vector.tensor_reduce(per[0], own, AX.X, ALU.add)
                late_link(nc.vector.tensor_tensor(own_start, own, start.unsqueeze(1).broadcast_to([P, MOE_TILES, E]), ALU.mult))
                late_link(nc.vector.tensor_reduce(per[1], own_start, AX.X, ALU.max))
                nc.vector.tensor_scalar(owner.bitcast(I32), per[0], -1.0, None, ALU.add)
                late_link(nc.vector.tensor_tensor(per[2], tile_no, per[1], ALU.subtract))
                nc.vector.tensor_scalar(per[3], per[0], float(PLACES // P), -float(PLACES // P), ALU.mult, ALU.add)
                late_link(nc.vector.tensor_scalar(per[2], per[2], float(PLACES // P), None, ALU.min))
                late_link(nc.vector.tensor_tensor(per[2], per[2], per[3], ALU.add))
                nc.vector.tensor_copy(tile_at.bitcast(I32), per[2]).then_inc(tiles_ready, 1)

            def pick_gates():
                b3 = best.rearrange("p (i e) -> p i e", i=NT)
                p3 = pick_p.rearrange("p (i e) -> p i e", i=NT)
                nc.vector.tensor_tensor(p3, b3, b3[:, :, 0:1].broadcast_to([P, NT, E]), ALU.subtract).then_inc(picks_in, 1)
                dve.wait_ge(picks_exp, 1)
                d0, d1 = dots[:, 0:NT], dots[:, NT:2 * NT]
                late_link(nc.vector.tensor_reduce(d0, p3, AX.X, ALU.add))
                late_link(nc.vector.reciprocal(d0, d0))
                pk = picks.rearrange("p (k i) -> p i k", k=2)
                late_link(nc.vector.tensor_tensor(pk, p3[:, :, 0:2], d0.unsqueeze(2).broadcast_to([P, NT, 2]), ALU.mult))
                late_link(nc.vector.tensor_reduce(d1, pk, AX.X, ALU.add))
                late_link(nc.vector.tensor_scalar(d1, d1, 1e-8, None, ALU.add))
                late_link(nc.vector.reciprocal(d1, d1))
                late_link(nc.vector.tensor_tensor(pk, pk, d1.unsqueeze(2).broadcast_to([P, NT, 2]), ALU.mult))
                nc.vector.tensor_scalar(picks, picks, gate[:, 7:8], None, ALU.mult)

            def out_slots():
                hot = logits.rearrange("p (i e) -> p i e", i=NT)
                late_link(nc.vector.tensor_scalar(shift_e, start, float(P), None, ALU.mult))
                late_link(nc.vector.tensor_tensor(shift_e, shift_e, place0, ALU.subtract))
                for k in range(2):
                    late_link(nc.vector.tensor_tensor(hot, pick_e[:, k * NT:(k + 1) * NT].unsqueeze(2).broadcast_to([P, NT, E]),
                                                      iota16[:, 0:E].unsqueeze(1).broadcast_to([P, NT, E]), ALU.is_equal))
                    late_link(nc.vector.tensor_tensor(hot, hot, shift_e.unsqueeze(1).broadcast_to([P, NT, E]), ALU.mult))
                    late_link(nc.vector.tensor_reduce(pick_e[:, k * NT:(k + 1) * NT], hot, AX.X, ALU.add))
                late_link(nc.vector.tensor_tensor(place_f, place_f, pick_e, ALU.add))
                nc.vector.tensor_copy(slots_out.bitcast(I32), place_f).then_inc(out_slots_ready, 1)

            for it in range(UNITS - 1):
                attend(it)
                post(it)
                route_rows(it)
                rho_round(UNITS - 1, it)
            rho_round(UNITS - 1, IT - 1)
            attend(UNITS - 1)
            post(UNITS - 1)
            route_rows(UNITS - 1)
            lay_tiles()
            pick_gates()

            def take_rows(m):
                dve.wait_ge(row_turned, m + 1)
                nc.vector.tensor_copy(row_t, pf[:, 0, 0:D]).then_inc(row_t_ready, 1)

            def take_hid(m):
                for k in range(2):
                    dve.wait_ge(hid_turned, m * 2 + k + 1)
                    nc.vector.tensor_copy(hid_t[:, 512 * k:512 * k + 512], pf[:, 1 + k, :]).then_inc(hid_t_ready, 1)

            def take_y(m):
                dve.wait_ge(y_made, m + 1)
                dve.wait_ge(y_stored, m * 16 + 16)
                nc.vector.tensor_copy(row_out, pa[:, 2, 0:D]).then_inc(y_ready, 1)

            take_rows(0)
            take_rows(1)
            out_slots()
            with dve.Fori(0, MOE_TILES - 2) as m:
                take_hid(m)
                take_rows(m + 2)
                take_y(m)
            for m in (MOE_TILES - 2, MOE_TILES - 1):
                take_hid(m)
                take_y(m)

            for n in range(NT):
                if n % 4 == 0:
                    dve.wait_ge(gathered[n // 4], 16 * 8)
                for k in range(2):
                    at = k * NT + n
                    nc.vector.scalar_tensor_tensor(x[:, n, :], back[:, n, k, :], picks[:, at:at + 1], x[:, n, :],
                                                   ALU.mult, ALU.add).then_inc(folded, 1)
                    dve.wait_ge(folded, 2 * n + k + 1)

        @block.tensor
        def _(pe):
            mm = nc.tensor.matmul
            turn = nc.tensor.transpose
            pe.sem_inc(h_used, RING)
            pe.wait_ge(consts_in, 16 * CONSTS)
            for c in range(DC):
                for k in range(DC):
                    v = mm(pa[:, c, 0:B * M], w_txt[:, k, c * P:(c + 1) * P], ctx_t[:, k, :], start=k == 0, stop=k == 1)
            v.then_inc(setup_mm, 1)
            for c in range(DC):
                for k in range(DC):
                    v = mm(pf[:, c, 0:B * M], wk[:, k, c * P:(c + 1) * P], ctx_t[:, k, :], start=k == 0, stop=k == 1)
            v.then_inc(setup_mm, 1)
            for b in range(B):
                for at, m in ((0, P), (P, MT)):
                    for k in range(DC):
                        v = mm(pa[0:m, 2 + b, at * 2:at * 2 + D], ctx_t[:, k, b * M + at:b * M + at + m], wv[:, k, :],
                               start=k == 0, stop=k == 1)
            v.then_inc(setup_mm, 1)
            pe.wait_ge(setup_done, 1)
            for k in range(2):
                for c in range(DC):
                    v = mm(gate_acc[k][:, 0:B * M], gate_w[:, k, c:c + 1].broadcast_to([P, P]), ctx_t[:, c, :], start=c == 0, stop=c == 1)
            v.then_inc(setup_mm, 1)
            pe.wait_ge(weights_in, 16 * 9)
            pe.wait_ge(v_rest_in, 16 * 8)
            pe.wait_ge(setup_read, 1)

            def att_turn(i):
                pe.wait_ge(a_xn_ready, i + 1)
                for c in range(DC):
                    v = turn(pa[:, 0, c * P:(c + 1) * P], a_xn[:, c * P:(c + 1) * P], ident)
                v.then_inc(a_turned, 1)

            def att_q(i):
                pe.wait_ge(a_xn_t_ready, i + 1)
                for g in range(DC):
                    for k in range(DC):
                        v = mm(pa[:, 1, g * P:(g + 1) * P], wq[:, k, g * P:(g + 1) * P], a_xn_t[:, k, :], start=k == 0, stop=k == 1)
                v.then_inc(q_made, 1)

            def att_scores(i, b, g):
                if g == 0:
                    pe.wait_ge(q_ready, i + 1)
                else:
                    pe.wait_ge(shifted, i * 2 + g)
                for k in range(4):
                    rows = slice(32 * k, 32 * k + 32)
                    mm(pa[:, k, 0:2 * M], q_t[rows, g, :], k_blocks[rows, b, g, :], start=True, stop=False)
                for k in range(4):
                    mb = mask_bias[:, i * M:(i + 1) * M] if isinstance(i, int) else mask_bias[:, bass.ds(i * M, M)]
                    v = mm(pa[:, k, 0:2 * M], ident_bf, mb.unsqueeze(1).broadcast_to([P, 2, M]), start=False, stop=True)
                v.then_inc(scores_made, 1)

            def att_prob(i, k):
                if k == 0:
                    pe.wait_ge(exp_done, i * 2 + 2)
                if k >= 2:
                    pe.wait_ge(prob_t_ready, i * 5 + k - 1)
                for j in range(TQ):
                    if k == 0:
                        v = turn(pa[0:TQ * MT, k % 2, j * P:(j + 1) * P],
                                 prob[:, j // 2, HG * P + (j % 2) * TQ * MT:HG * P + (j % 2 + 1) * TQ * MT], ident)
                    else:
                        h = TQ * ((k - 1) % 2) + j
                        v = turn(pa[:, k % 2, j * P:(j + 1) * P], prob[:, (k - 1) // 2, h * P:(h + 1) * P], ident)
                v.then_inc(prob_turned, 1)

            def att_pv(i, b, q):
                pe.wait_ge(prob_t_ready, i * 5 + q + 2)
                for j in range(TQ):
                    mm(pa[VW * j:VW * j + VW, 2, q * P:(q + 1) * P], v_rest[0:TQ * MT, b, TQ * q + j, :],
                       prob_t[0:TQ * MT, 0, q * P:(q + 1) * P], start=True, stop=False)
                for j in range(TQ):
                    v = mm(pa[VW * j:VW * j + VW, 2, q * P:(q + 1) * P], v_main[:, b, TQ * q + j, :],
                           prob_t[:, 1 + (q + 1) % 2, j * P:(j + 1) * P], start=False, stop=True)
                v.then_inc(pv_done, 1)

            def att_o(i):
                pe.wait_ge(o_ready, i + 1)
                for q in range(H // TQ):
                    v = turn(pa[:, 0, q * P:(q + 1) * P], o_t[:, q, :], ident)
                v.then_inc(o_turned, 1)

            def att_out(i):
                pe.wait_ge(att_ready, i + 1)
                for c in range(DC):
                    v = turn(pa[:, 1, c * P:(c + 1) * P], att[:, c * P:(c + 1) * P], ident)
                v.then_inc(att_turned, 1)

            def att_wo(i):
                pe.wait_ge(att_t_ready, i + 1)
                for k in range(DC):
                    v = mm(pa[:, 2, 0:D], att_t[:, k, :], wo[:, k, :], start=k == 0, stop=k == 1)
                v.then_inc(wo_made, 1)

            def ffn_turn(i):
                pe.wait_ge(f_xn_ready, i + 1)
                for c in range(DC):
                    v = turn(pf[:, 1, c * P:(c + 1) * P], f_xn[:, c * P:(c + 1) * P], ident)
                v.then_inc(f_turned, 1)

            def last_turn(i):
                pe.wait_ge(n_xn_ready, i + 1)
                for c in range(DC):
                    v = turn(pf[:, 2, c * P:(c + 1) * P], n_xn[:, c * P:(c + 1) * P], ident)
                v.then_inc(n_turned, 1)

            def ffn_pq(i):
                pe.wait_ge(f_xn_t_ready, i + 1)
                for e in range(4):
                    for k in range(DC):
                        v = mm(pf[:, 1, e * P:(e + 1) * P], w_pq[:, k, e * P:(e + 1) * P], f_xn_t[:, k, :], start=k == 0, stop=k == 1)
                v.then_inc(pq_made, 1)

            def ffn_up(i):
                pe.wait_ge(sims_read, i + 1)
                for f in range(FC):
                    for k in range(DC):
                        v = mm(pf_flat[:, f * P:(f + 1) * P], w_up[:, k, f * P:(f + 1) * P], f_xn_t[:, k, :], start=k == 0, stop=k == 1)
                v.then_inc(up_made, 1)

            def ffn_sims(i):
                pe.wait_ge(pq_ready, i + 1)
                for e in range(4):
                    v = mm(pf[:, 1, e * P:(e + 1) * P], pq_t[:, e * P:(e + 1) * P], keys[:, e, :], start=True, stop=True)
                v.then_inc(sims_made, 1)

            def ffn_g(i):
                pe.wait_ge(up_ready, i + 1)
                for n in range(2):
                    for k in range(DC):
                        v = mm(pf[:, n, :], f_xn_t[:, k, :], de[:, k, n * 512:(n + 1) * 512], start=k == 0, stop=k == 1)
                v.then_inc(g_made, 1)

            def ffn_down(i):
                for f in range(FC):
                    v = mm(pf[:, 2, 0:D], up_t[:, f * P:(f + 1) * P], w_down[:, f, :], start=f == 0, stop=False)
                v.then_inc(down_made, 1)

            def ffn_w(i, k):
                if k == 0:
                    pe.wait_ge(w_ready, i + 1)
                else:
                    pe.wait_ge(w_t_ready, i * 2 + 1)
                for e in range(4 * k, 4 * k + 4):
                    v = turn(pf[:, 0, (e % 4) * P:(e % 4 + 1) * P], big1[:, e * P:(e + 1) * P], ident)
                v.then_inc(w_turned, 1)

            def ffn_out(i, k):
                pe.wait_ge(w_t_ready, i * 2 + k + 1)
                for e in range(4 * k, 4 * k + 4):
                    v = mm(pf[:, 2, 0:D], big2[:, e * P:(e + 1) * P], ue[:, e, :], start=False, stop=e == NE // P - 1)
                if k == 1:
                    v.then_inc(ffn_made, 1)

            def ffn_feat(i):
                pe.wait_ge(n_xn_t_ready, i + 1)
                for c in range(DC):
                    for k in range(DC):
                        v = mm(pf[:, 2, c * P:(c + 1) * P], w_feat[:, k, c * P:(c + 1) * P], n_xn_t[:, k, :], start=k == 0, stop=k == 1)
                v.then_inc(feat_made, 1)

            def tanh_rows(u, it, k0, k1):
                n0 = (it + u * IT) * ROUND
                for k in range(k0, k1, 4):
                    m = min(4, ROUND - k)
                    if k == 0:
                        pe.wait_ge(rho_ready, it + u * IT + 1)
                    pe.wait_ge(h_ready, n0 + k + m)
                    for kk in range(k, k + m):
                        r, c, j = ORDER[kk]
                        last = c == DC - 1 and 4 * (r + 1) + j >= TI
                        v = mm(pr[32 * j:32 * j + 32, :], window[:, c, 31 - r:63 - r], ring[:, kk % RING, :],
                               start=r == 0 and c == 0, stop=last)
                    v.then_inc(h_used, m)

            def attention(i, b):
                att_turn(i)
                att_q(i)
                att_scores(i, b, 0)
                att_scores(i, b, 1)
                att_prob(i, 0)
                att_prob(i, 1)
                for q in range(H // TQ):
                    if q < 3:
                        att_prob(i, q + 2)
                    att_pv(i, b, q)
                att_o(i)
                att_out(i)
                att_wo(i)

            def front(i, b1, b2, tanh=None):
                rows = (lambda k0, k1: tanh_rows(*tanh, k0, k1)) if tanh else (lambda k0, k1: None)
                one, two = b1 is not None, b2 is not None
                j, l = i + 1, i + 2
                ffn_up(i)
                rows(0, 8)
                if one:
                    att_scores(j, b1, 1)
                rows(8, 16)
                ffn_g(i)
                rows(16, 20)
                ffn_down(i)
                rows(20, 28)
                if one:
                    att_prob(j, 0)
                    att_prob(j, 1)
                rows(28, 32)
                if one:
                    att_prob(j, 2)
                    att_pv(j, b1, 0)
                rows(32, 36)
                if one:
                    att_prob(j, 3)
                    att_pv(j, b1, 1)
                rows(36, 40)
                if one:
                    att_prob(j, 4)
                    att_pv(j, b1, 2)
                    att_pv(j, b1, 3)
                rows(40, 44)
                if one:
                    att_o(j)
                rows(44, 48)
                if one:
                    att_out(j)
                rows(48, 52)
                if one:
                    att_wo(j)
                rows(52, 56)
                ffn_w(i, 0)
                rows(56, 60)
                ffn_w(i, 1)
                if one:
                    ffn_turn(j)
                if two:
                    att_turn(l)
                ffn_out(i, 0)
                if one:
                    ffn_pq(j)
                ffn_out(i, 1)
                rows(60, 64)
                if two:
                    att_q(l)
                if one:
                    ffn_sims(j)
                rows(64, 68)
                last_turn(i)
                if two:
                    att_scores(l, b2, 0)
                rows(68, 76)
                ffn_feat(i)
                rows(76, ROUND)

            attention(0, 0)
            ffn_turn(0)
            att_turn(1)
            ffn_pq(0)
            ffn_sims(0)
            att_q(1)
            att_scores(1, 0, 0)
            with pe.Fori(0, NTU) as i:
                front(i, 0, 0)
            for i0, n, u, it0, b1, b2 in FUSED:
                with pe.Fori(0, n) as k:
                    front(k + i0, b1, b2, (u, k + it0))

            def rho_turn(u):
                pe.wait_ge(rho_in[u], 16)
                if u == 0:
                    pe.wait_ge(feat_done, NT)
                for n in range(NTU):
                    for k in range(2):
                        at = (n % 2) * R + k * HALF
                        v = turn(pa[:, n // 2, at:at + HALF], rho_back[u][0:HALF, k, n * P:(n + 1) * P], ident[0:HALF, 0:HALF])
                v.then_inc(rho_turned, 1)

            def rows4_turn(u, k):
                pe.wait_ge(rows4_ready, u * NTU + 2 * k + 2)
                for m in range(2 * k, 2 * k + 2):
                    for c in range(DC):
                        v = turn(pf[:, k, ((m % 2) * DC + c) * P:((m % 2) * DC + c + 1) * P], rows4[u][:, m, c * P:(c + 1) * P], ident)
                v.then_inc(rows4_turned, 1)

            def router(u):
                pe.wait_ge(rows4_t_ready, u * 2 + 2)
                for m in range(NTU):
                    for c in range(DC):
                        v = mm(pa[:, 2, m * E:(m + 1) * E], rows_t[:, m, c * P:(c + 1) * P], w_router[:, c, :], start=c == 0, stop=c == 1)
                v.then_inc(router_made, 1)

            def ranks(u):
                pe.wait_ge(pick_ready, u + 1)
                mm(pf[:, 0, 0:T], before, route[:, 5 * T:6 * T], start=True, stop=True)
                mm(pf[:, 0, T:2 * T], ones, route[:, 5 * T:6 * T], start=True, stop=True).then_inc(ranks_made, 1)

            for it in range(UNITS - 1):
                rho_turn(it)
                tanh_rows(UNITS - 1, it, 0, 40)
                rows4_turn(it, 0)
                rows4_turn(it, 1)
                tanh_rows(UNITS - 1, it, 40, 56)
                router(it)
                tanh_rows(UNITS - 1, it, 56, 64)
                ranks(it)
                tanh_rows(UNITS - 1, it, 64, ROUND)
            tanh_rows(UNITS - 1, IT - 1, 0, ROUND)
            rho_turn(UNITS - 1)
            rows4_turn(UNITS - 1, 0)
            rows4_turn(UNITS - 1, 1)
            router(UNITS - 1)
            ranks(UNITS - 1)

            owner_i = owner[0:1, :].bitcast(I32)

            def expert_of(m):
                at = owner_i[:, m:m + 1] if isinstance(m, int) else owner_i[:, bass.ds(m, 1)]
                return pe.value_load(at, min_val=0, max_val=E - 1)

            def turn_rows(m):
                pe.wait_ge(row_landed, m * 16 + 16)
                for c in range(DC):
                    v = turn(pf[:, 0, c * P:(c + 1) * P], row_in[:, c * P:(c + 1) * P], ident)
                v.then_inc(row_turned, 1)

            def up(m, e):
                pe.wait_ge(row_t_ready, m + 1)
                pe.wait_ge(bias_up_in, m * 16 + 16)
                for n in range(2):
                    for k in range(DC):
                        mm(pa[:, n, :], row_t[:, k * P:(k + 1) * P], w1[:, bass.ds((e * DC + k) * FF + n * 512, 512)], start=k == 0, stop=False)
                    v = mm(pa[:, n, :], ones3[0:3, :], bias_up[0:3, n * 512:(n + 1) * 512], start=False, stop=True)
                v.then_inc(hid_made, 1)

            def turn_hid(m):
                pe.wait_ge(hid_ready, m + 1)
                for f in range(FC):
                    v = turn(pf[:, 1 + f // 4, (f % 4) * P:(f % 4 + 1) * P], hid[:, f * P:(f + 1) * P], ident)
                    if f % 4 == 3:
                        v.then_inc(hid_turned, 1)

            def down(m, e):
                for f in range(FC):
                    if f % 4 == 0:
                        pe.wait_ge(hid_t_ready, m * 2 + f // 4 + 1)
                    mm(pa[:, 2, 0:D], hid_t[:, f * P:(f + 1) * P], w2[:, bass.ds((e * FC + f) * D, D)], start=f == 0, stop=False)
                pe.wait_ge(bias_y_in, m * 16 + 16)
                mm(pa[:, 2, 0:D], ones3[0:3, :], bias_y[0:3, :], start=False, stop=True).then_inc(y_made, 1)

            pe.wait_ge(tiles_ready, 1)
            pe.wait_ge(experts_in, 32 * E)
            turn_rows(0)
            up(0, expert_of(0))
            turn_rows(1)
            with pe.Fori(0, MOE_TILES - 2) as m:
                e_down, e_up = expert_of(m), expert_of(m + 1)
                turn_hid(m)
                up(m + 1, e_up)
                turn_rows(m + 2)
                down(m, e_down)
            e_down, e_up = expert_of(MOE_TILES - 2), expert_of(MOE_TILES - 1)
            turn_hid(MOE_TILES - 2)
            up(MOE_TILES - 1, e_up)
            down(MOE_TILES - 2, e_down)
            turn_hid(MOE_TILES - 1)
            down(MOE_TILES - 1, e_up)


def kernel(**inputs):
    import concourse.bacc as bacc
    from concourse.bass_utils import run_bass_kernel_spmd

    a = {k: np.asarray(v) for k, v in inputs.items()}

    def chunks(w):
        return np.ascontiguousarray(w.reshape(-1, P, w.shape[-1]).transpose(1, 0, 2))

    keys = a["L0_ffn_keys"]
    key_blocks = np.zeros((P, 4, P), keys.dtype)
    for e in range(4):
        for j in range(2):
            key_blocks[64 * j:64 * j + 64, e, 64 * j:64 * j + 64] = keys[2 * (e % 2) + j, :, e // 2, :].T
    lay = {
        "x": a["x"].reshape(B * S, D),
        "mask": a["mask_BxSxS2_fk1"].reshape(B * S, M),
        "ctx_t": chunks(a["ctx_1024"].reshape(B * M, D).T),
        "gates": np.concatenate([a["g_xattn"], a["g_ffn"]]).reshape(4),
        "wq_t": chunks(a["L0_xattn_Wq"].T), "wk_t": chunks(a["L0_xattn_Wk"].T),
        "wv_t": chunks(a["L0_xattn_Wv"].T), "wo_t": chunks(a["L0_xattn_Wo"].T),
        "bq": a["L0_xattn_bq"].reshape(DC, P).T, "bk": a["L0_xattn_bk"].reshape(DC, P).T,
        "bv": a["L0_xattn_bv"], "bo": a["L0_xattn_bo"],
        "w_up_t": chunks(a["L0_ffn_W_up"].T), "w_down_t": chunks(a["L0_ffn_W_down"].T),
        "w_pq_t": chunks(a["L0_ffn_W_q"].T), "keys": key_blocks,
        "de_t": chunks(a["L0_ffn_down_embed"].T), "ue": chunks(a["L0_ffn_up_embed"]),
        "w_feat": chunks(a["L1_xattn_W"]), "w_txt": chunks(a["L1_xattn_Ws"]),
        "b_txt": a["L1_xattn_b"].reshape(DC, P).T,
        "w_rho": a["L1_xattn_w"].reshape(DC, P).T,
        "gate_w": np.stack([a["L1_xattn_Wcw"][0], a["L1_xattn_Wcb"][0]]).reshape(2, DC, P).transpose(2, 0, 1),
        "gate_bias": np.concatenate([a["L1_xattn_bcw"], a["L1_xattn_bcb"]]),
        "q_mask": a["mask_BxS2_ik0"].reshape(B * M),
        "w_router": chunks(a["L1_ffn_router_w"].T),
        "expert_bias": np.concatenate([a["L1_ffn_b1"], a["L1_ffn_b2"]], axis=1).reshape(P, 80),
        "w1": a["L1_ffn_w1"].reshape(E, FF, DC, P).transpose(3, 0, 2, 1).reshape(P, E * DC * FF),
        "w2": a["L1_ffn_w2"].reshape(E, D, FC, P).transpose(3, 0, 2, 1).reshape(P, E * FC * D),
        "before": (np.arange(P)[:, None] < np.arange(P)[None, :]).astype(np.float32),
        "ident": np.eye(P, dtype=np.float32),
        "even_odd": (np.arange(P)[:, None] // HD % 2 == np.arange(2)[None, :]).astype(np.float32),
    }
    nc = bacc.Bacc("TRN2", target_bir_lowering=False, num_devices=1)
    arrays, t = {}, {}
    for name, v in lay.items():
        v = np.ascontiguousarray(v)
        arrays["in_" + name] = v
        t[name] = nc.dram_tensor("in_" + name, v.shape, mybir.dt.from_np(v.dtype), kind="ExternalInput").ap()
    out = nc.dram_tensor("out_0", (B * S, D), F32, kind="ExternalOutput").ap()
    build(nc, t, out)
    r = run_bass_kernel_spmd(nc, [arrays], core_ids=[0])
    return np.asarray(r.results[0]["out_0"]).reshape(B, S, D)
```
